# Optimizing a Trainium2 kernel written in Bass

```python
import numpy as np
import jax
import jax.numpy as jnp

def _softmax(x, axis=-1):
    return jax.nn.softmax(x, axis=axis)

def _gelu(x):
    return jax.nn.gelu(x, approximate=True)

def _silu(x):
    return jax.nn.silu(x)

def _sigmoid(x):
    return jax.nn.sigmoid(x)

def _layernorm(x, axis=-1, eps=1e-05):
    m = jnp.mean(x, axis=axis, keepdims=True)
    v = jnp.var(x, axis=axis, keepdims=True)
    return (x - m) / jnp.sqrt(v + eps)

def _scatter_add(tgt, idx, src, axis=0):
    return tgt.at[idx].add(src)

def _segment_sum(src, seg, n):
    return jax.ops.segment_sum(src, seg, n)
kernel_name = 'mk_gnn_preln_d2_gnn_r32_9ed1c3'

def setup_inputs(seed: int=0):
    np.random.seed(seed)
    _w = jnp.asarray

    def _rec_inputs():
        import jax
        import jax.numpy as jnp
        _gk = jax.random.key(seed)
        x = -0.0003713 + 1 * jax.random.normal(jax.random.fold_in(_gk, 1), (50000, 256), jnp.float32)
        src = jax.random.randint(jax.random.fold_in(_gk, 2), (50000,), 0, 50000, jnp.int32)
        dst = jnp.minimum((50000 * jax.random.uniform(jax.random.fold_in(_gk, 3), (50000,)) ** 2.0).astype(jnp.int32), 49999)
        _o = jnp.argsort(dst, stable=True)
        src = src[_o]
        dst = dst[_o]
        edge_weight = -7.32377e-05 + 0.176746 * jax.random.normal(jax.random.fold_in(_gk, 13), (50000,), jnp.float32)
        return (x, src, dst, edge_weight)
    x, src, dst, edge_weight = _rec_inputs()

    def _L0_gnn_setup():
        import jax, jax.numpy as jnp
        import numpy as np
        N_NODES = 50000
        NNZ = 50000
        D_FEAT = 256
        key = jax.random.key(seed)
        k_x, k_v, k_r, k_c = jax.random.split(key, 4)
        x = jax.random.normal(k_x, (N_NODES, D_FEAT), dtype=jnp.float32)
        std = 1.0 / np.sqrt(NNZ / N_NODES)
        values = jax.random.normal(k_v, (NNZ,), dtype=jnp.float32) * std
        row = jax.random.randint(k_r, (NNZ,), 0, N_NODES, dtype=jnp.int64)
        col = jax.random.randint(k_c, (NNZ,), 0, N_NODES, dtype=jnp.int64)
        return {'x': x, 'values': values, 'row': row, 'col': col}
    _L0_gnn_all = _L0_gnn_setup()
    _L0_gnn_in = {k: v for k, v in _L0_gnn_all.items() if k in ()}
    del _L0_gnn_all

    def _L1_gnn_setup():
        import jax, jax.numpy as jnp
        import numpy as np
        N = 50000
        E = 12500
        IN = 256
        HID = 128
        HEADS = 4
        OUT = 256
        NEG = 0.2

        def _glorot(key, shape, fan_in):
            return jax.random.normal(key, shape, jnp.float32) * (1.0 / np.sqrt(fan_in))

        def gatv2_conv(x, src, dst, Wl, Wr, att, bias, heads, ch, concat):
            n = x.shape[0]
            xl = (x @ Wl).reshape(n, heads, ch)
            xr = (x @ Wr).reshape(n, heads, ch)
            g = xl[src] + xr[dst]
            e = jnp.einsum('ehc,hc->eh', jax.nn.leaky_relu(g, NEG), att)
            e_max = jax.ops.segment_max(e, dst, num_segments=n)
            p = jnp.exp(e - e_max[dst])
            denom = jax.ops.segment_sum(p, dst, num_segments=n)
            alpha = p / denom[dst]
            out = jax.ops.segment_sum(alpha[:, :, None] * xl[src], dst, num_segments=n)
            out = out.reshape(n, heads * ch) if concat else out.mean(axis=1)
            return out + bias
        key = jax.random.key(seed)
        ks = jax.random.split(key, 8)
        x = jax.random.normal(ks[0], (N, IN), jnp.float32)
        edge_index = jax.random.randint(ks[1], (2, E), 0, N, dtype=jnp.int64)
        W1l = _glorot(ks[2], (IN, HEADS * HID), IN)
        W1r = _glorot(ks[3], (IN, HEADS * HID), IN)
        a1 = _glorot(ks[4], (HEADS, HID), HID)
        b1 = jnp.zeros((HEADS * HID,), jnp.float32)
        W2l = _glorot(ks[5], (HEADS * HID, OUT), HEADS * HID)
        W2r = _glorot(ks[6], (HEADS * HID, OUT), HEADS * HID)
        a2 = _glorot(ks[7], (1, OUT), OUT)
        b2 = jnp.zeros((OUT,), jnp.float32)
        return dict(x=x, edge_index=edge_index, W1l=W1l, W1r=W1r, a1=a1, b1=b1, W2l=W2l, W2r=W2r, a2=a2, b2=b2)
    _L1_gnn_all = _L1_gnn_setup()
    _L1_gnn_in = {k: v for k, v in _L1_gnn_all.items() if k in ('W1l', 'W1r', 'a1', 'b1', 'W2l', 'W2r', 'a2', 'b2')}
    del _L1_gnn_all
    return {'x': x, 'src': src, 'dst': dst, 'edge_weight': edge_weight, 'L1_gnn_W1l': _L1_gnn_in['W1l'], 'L1_gnn_W1r': _L1_gnn_in['W1r'], 'L1_gnn_a1': _L1_gnn_in['a1'], 'L1_gnn_b1': _L1_gnn_in['b1'], 'L1_gnn_W2l': _L1_gnn_in['W2l'], 'L1_gnn_W2r': _L1_gnn_in['W2r'], 'L1_gnn_a2': _L1_gnn_in['a2'], 'L1_gnn_b2': _L1_gnn_in['b2']}

def reference(x, src, dst, edge_weight, L1_gnn_W1l, L1_gnn_W1r, L1_gnn_a1, L1_gnn_b1, L1_gnn_W2l, L1_gnn_W2r, L1_gnn_a2, L1_gnn_b2):
    import jax
    import jax.numpy as jnp

    def _L0_gnn_ref(x, values, row, col):
        import jax, jax.numpy as jnp
        import numpy as np
        N_NODES = 50000
        NNZ = 50000
        D_FEAT = 256
        msgs = values[:, None] * x[col]
        out = jax.ops.segment_sum(msgs, row, num_segments=N_NODES)
        return out

    def _L1_gnn_ref(x, edge_index, W1l, W1r, a1, b1, W2l, W2r, a2, b2):
        import jax, jax.numpy as jnp
        import numpy as np
        N = 50000
        E = 12500
        IN = 256
        HID = 128
        HEADS = 4
        OUT = 256
        NEG = 0.2

        def _glorot(key, shape, fan_in):
            return jax.random.normal(key, shape, jnp.float32) * (1.0 / np.sqrt(fan_in))

        def gatv2_conv(x, src, dst, Wl, Wr, att, bias, heads, ch, concat):
            n = x.shape[0]
            xl = (x @ Wl).reshape(n, heads, ch)
            xr = (x @ Wr).reshape(n, heads, ch)
            g = xl[src] + xr[dst]
            e = jnp.einsum('ehc,hc->eh', jax.nn.leaky_relu(g, NEG), att)
            e_max = jax.ops.segment_max(e, dst, num_segments=n)
            p = jnp.exp(e - e_max[dst])
            denom = jax.ops.segment_sum(p, dst, num_segments=n)
            alpha = p / denom[dst]
            out = jax.ops.segment_sum(alpha[:, :, None] * xl[src], dst, num_segments=n)
            out = out.reshape(n, heads * ch) if concat else out.mean(axis=1)
            return out + bias
        loop = jnp.arange(x.shape[0], dtype=edge_index.dtype)
        src = jnp.concatenate([edge_index[0], loop])
        dst = jnp.concatenate([edge_index[1], loop])
        h = jax.nn.relu(gatv2_conv(x, src, dst, W1l, W1r, a1, b1, HEADS, HID, True))
        return gatv2_conv(h, src, dst, W2l, W2r, a2, b2, 1, OUT, False)
    edge_index = jnp.stack([src, dst])
    h = jnp.maximum(_layernorm(x, axis=-1), 0.0)
    x = x + _L0_gnn_ref(h, edge_weight, src, dst)
    h = jnp.maximum(_layernorm(x, axis=-1), 0.0)
    x = x + _L1_gnn_ref(h, edge_index, L1_gnn_W1l, L1_gnn_W1r, L1_gnn_a1, L1_gnn_b1, L1_gnn_W2l, L1_gnn_W2r, L1_gnn_a2, L1_gnn_b2)
    return x

_drawn_inputs = setup_inputs


def setup_inputs(seed=0):
    import zlib

    import numpy as np

    out = dict(_drawn_inputs(seed))
    spreads = {'L1_gnn_b1': (0.0, 0.1), 'L1_gnn_b2': (0.0, 0.1)}
    factors = {'L1_gnn_W1r': 5.285, 'L1_gnn_W2r': 8.0, 'L1_gnn_a2': 4.917}
    for name, (base, spread) in spreads.items():
        noise = np.random.default_rng([zlib.crc32(name.encode()), seed]).standard_normal(out[name].shape)
        drawn = base * np.exp(spread * noise) if base else spread * noise
        out[name] = jnp.asarray(drawn.astype(out[name].dtype))
    for name, factor in factors.items():
        out[name] = (out[name] * factor).astype(out[name].dtype)
    return out
```

```python
from contextlib import ExitStack

import concourse.bass as bass
from concourse import mybir

ALU = mybir.AluOpType
ACT = mybir.ActivationFunctionType
F32 = mybir.dt.float32
I32 = mybir.dt.int32

P = 128
BIG = 1.0e30
EPS = 1e-5
SLOPE = 0.2
SKIP = 60000


class Tile:

    def __init__(self, u, slot, unroll, static):
        self.u, self.slot, self.static = u, slot, static
        self.n = u * unroll + slot


def pipeline(eng, count, unroll, steps, rolled_to=None):
    rolled_to = count if rolled_to is None else rolled_to
    longest = max(lag for lag, _ in steps)
    start = longest + unroll
    loops = max(0, (rolled_to - start) // unroll)

    def beat(base, offset, static):
        for lag, fn in steps:
            c = offset - lag
            if static:
                n = base * unroll + c
                if 0 <= n < count:
                    fn(Tile(n // unroll, n % unroll, unroll, True))
            else:
                fn(Tile(base + c // unroll, c % unroll, unroll, False))

    for i in range(min(start, count + longest)):
        beat(0, i, True)
    if loops > 0:
        with eng.Fori(0, loops) as r:
            for k in range(unroll):
                beat(r, start + k, False)
    for i in range(start + loops * unroll, count + longest):
        beat(0, i, True)


def staggered(rows, items):
    def of(fn, j):
        return lambda t: fn(t, j) if j < rows.width(t) else None

    last = max(offset for offset, _, _ in items)
    return [(lag, of(fn, at - offset)) for at in range(J + last) for offset, lag, fn in items
            if 0 <= at - offset < J]


def wait_count(eng, semaphore, value):
    if isinstance(value, int) and value <= 0:
        return
    eng.wait_ge(semaphore, value)


def settle(eng, passed):
    eng.sem_inc(passed, 1)


class Phase:

    def __init__(self, nc, ctx, name, last=False):
        self.nc, self.ctx, self.name, self.taken = nc, ctx, name, []
        if not last:
            ctx.callback(self.end)

    def end(self):
        self.nc.clear_and_free_semaphores(self.taken)
        self.nc.all_engine_barrier()

    def sb(self, name, shape, dt=F32):
        return self.ctx.enter_context(self.nc.sbuf_tensor(f"{self.name}_{name}", shape, dt))

    def ps(self, name, shape, dt=F32):
        return self.ctx.enter_context(self.nc.psum_tensor(f"{self.name}_{name}", shape, dt))

    def sem(self, name):
        self.taken.append(self.nc.alloc_semaphore(f"{self.name}_{name}"))
        return self.taken[-1]

    def sems(self, name, n):
        return [self.sem(f"{name}{k}") for k in range(n)]


J = 6


class Rows:
    def __init__(self, n):
        self.n = n
        self.supers = n // (P * J)
        self.tail = n - self.supers * P * J
        assert 0 < self.tail <= P and self.tail % 16 == 0
        self.turns = self.supers + 1
        self.tiles = self.supers * J + 1

    def is_tail(self, tile):
        return tile.static and tile.n == self.supers

    def width(self, tile):
        return 1 if self.is_tail(tile) else J

    def dram(self, table, tile, cols=None):
        d = table.shape[1] if cols is None else cols
        if self.is_tail(tile):
            return table[self.supers * P * J:self.n, 0:d].rearrange("(p j) d -> p j d", j=1), self.tail
        return table[bass.ds(tile.n * (P * J), P * J), 0:d].rearrange("(p j) d -> p j d", j=J), P


def constants(nc, k):
    with ExitStack() as ctx:
        ph = Phase(nc, ctx, "consts")
        filled = ph.sem("filled")
        block = ctx.enter_context(nc.Block())

        @block.gpsimd
        def _(pool):
            nc.gpsimd.memset(k["ident"][:], 0.0).then_inc(filled, 1)
            nc.gpsimd.memset(k["last_row"][:], 0.0).then_inc(filled, 1)
            nc.gpsimd.memset(k["first_row"][:], 0.0).then_inc(filled, 1)
            nc.gpsimd.memset(k["below"][:], 1.0).then_inc(filled, 1)
            nc.gpsimd.iota(k["dump_i"][:], [[0, 1]], base=k["n"], channel_multiplier=1).then_inc(filled, 1)
            pool.wait_ge(filled, 5)
            nc.gpsimd.affine_select(out=k["ident"][:], in_=k["ident"][:], compare_op=ALU.not_equal, fill=1.0,
                                    base=0, pattern=[[-1, P]], channel_multiplier=1).then_inc(filled, 1)
            nc.gpsimd.affine_select(out=k["last_row"][:], in_=k["last_row"][:], compare_op=ALU.not_equal, fill=1.0,
                                    base=-(P - 1), pattern=[[0, P]], channel_multiplier=1).then_inc(filled, 1)
            nc.gpsimd.affine_select(out=k["first_row"][:], in_=k["first_row"][:], compare_op=ALU.not_equal, fill=1.0,
                                    base=0, pattern=[[0, P]], channel_multiplier=1).then_inc(filled, 1)
            nc.gpsimd.affine_select(out=k["below"][:], in_=k["below"][:], compare_op=ALU.is_gt, fill=0.0,
                                    base=0, pattern=[[-1, P]], channel_multiplier=1).then_inc(filled, 1)
            nc.gpsimd.tensor_copy(k["dump"][:], k["dump_i"][:]).then_inc(filled, 1)
            nc.gpsimd.memset(k["eps"][:], EPS).then_inc(filled, 1)
            pool.wait_ge(filled, 11)


def edge_columns(nc, k, src, dst, weight, next_dst):
    E, N, T = k["e"], k["n"], k["t"]
    full = E // P
    rest = E - full * P
    chunks = [(c * P, min(P, T - c * P)) for c in range((T + P - 1) // P)]
    with ExitStack() as ctx:
        ph = Phase(nc, ctx, "cols")
        NC = len(chunks)
        raw_src = [ph.sb(f"raw_src{c}", [P, P], I32) for c in range(NC)]
        raw_dst = [ph.sb(f"raw_dst{c}", [P, P], I32) for c in range(NC)]
        raw_nxt = [ph.sb(f"raw_nxt{c}", [P, P], I32) for c in range(NC)]
        raw_prev = [ph.sb(f"raw_prev{c}", [P, 1], I32) for c in range(NC)]
        wt = [ph.sb(f"wt{c}", [P, P]) for c in range(NC)]
        names = ["src", "dst", "gather_dst", "last", "pen", "prev", "weight"]
        val = {n: [ph.sb(f"v_{n}{c}", [P, P]) if n != "weight" else wt[c] for c in range(NC)] for n in names}
        nxt = [ph.sb(f"nxt{c}", [P, P]) for c in range(NC)]
        prev_col = [ph.sb(f"prev_col{c}", [P, 1]) for c in range(NC)]
        tp = [ph.ps(f"tp{b}", [P, P]) for b in range(2)]
        padded, loaded, order = ph.sem("padded"), ph.sem("loaded"), ph.sem("order")
        values_ready, turned, copied = ph.sem("values_ready"), ph.sem("turned"), ph.sem("copied")
        loads = []
        for c, (t0, rows) in enumerate(chunks):
            f = min(rows, full - t0)
            for buf, a, shift in ((raw_src, src, 0), (raw_dst, dst, 0), (wt, weight, 0), (raw_nxt, next_dst, 0)):
                loads.append((buf[c][0:f, :], a[t0 * P:(t0 + f) * P].rearrange("(t p) -> t p", p=P)))
            if f < rows and rest:
                n_next = next_dst.shape[0] - full * P
                for buf, a, n in ((raw_src, src, rest), (raw_dst, dst, rest), (wt, weight, rest),
                                  (raw_nxt, next_dst, n_next)):
                    loads.append((buf[c][f:f + 1, 0:n], a[full * P:full * P + n].rearrange("(t p) -> t p", t=1)))
            first = 1 if c == 0 else 0
            a0 = (t0 + first) * P - 1
            loads.append((raw_prev[c][first:rows, :],
                          dst[a0:a0 + (rows - first - 1) * P + 1:P].rearrange("(t o) -> t o", o=1)))
        block = ctx.enter_context(nc.Block())

        @block.gpsimd
        def _(pool):
            for c in range(NC):
                nc.gpsimd.memset(raw_src[c][:], 0).then_inc(padded, 1)
                nc.gpsimd.memset(raw_dst[c][:], N).then_inc(padded, 1)
                nc.gpsimd.memset(raw_nxt[c][:], N + 1).then_inc(padded, 1)
                nc.gpsimd.memset(raw_prev[c][:], -5).then_inc(padded, 1)
                nc.gpsimd.memset(wt[c][:], 0.0).then_inc(padded, 1)
                nc.gpsimd.memset(val["prev"][c][:], -5.0).then_inc(padded, 1)

        @block.sync
        def _(sp):
            sp.wait_ge(padded, 6 * NC)
            for to, frm in loads:
                sp.dma_start(to, frm, allow_slow_non_contiguous=True).then_inc(loaded, 16)

        @block.vector
        def _(dve):
            dve.wait_ge(padded, 6 * NC)
            dve.wait_ge(loaded, 16 * len(loads))
            n = 0
            for c in range(NC):
                nc.vector.tensor_copy(val["src"][c][:], raw_src[c][:]).then_inc(order, 1)
                nc.vector.tensor_copy(val["dst"][c][:], raw_dst[c][:]).then_inc(order, 1)
                nc.vector.tensor_copy(nxt[c][:], raw_nxt[c][:]).then_inc(order, 1)
                nc.vector.tensor_copy(prev_col[c][:], raw_prev[c][:]).then_inc(order, 1)
                n += 4
            dve.wait_ge(order, n)
            for c in range(NC):
                d = val["dst"][c]
                nc.vector.tensor_scalar(val["gather_dst"][c][:], d[:], float(N - 1), None, ALU.min).then_inc(order, 1)
                nc.vector.tensor_scalar(val["pen"][c][:], d[:], prev_col[c][:, 0:1], BIG, ALU.is_equal,
                                        ALU.mult).then_inc(order, 1)
                nc.vector.tensor_copy(val["prev"][c][:, P - 1:P], prev_col[c][:]).then_inc(order, 1)
                nc.vector.tensor_tensor(nxt[c][:], d[:], nxt[c][:], ALU.not_equal).then_inc(order, 1)
                n += 4
            dve.wait_ge(order, n)
            for c in range(NC):
                nc.vector.tensor_scalar(val["pen"][c][:], val["pen"][c][:], -BIG, None, ALU.add).then_inc(order, 1)
                nc.vector.scalar_tensor_tensor(out=val["last"][c][:], in0=val["dst"][c][:], scalar=float(-SKIP),
                                               in1=nxt[c][:], op0=ALU.add, op1=ALU.mult).then_inc(order, 1)
                n += 2
            dve.wait_ge(order, n)
            for c in range(NC):
                nc.vector.tensor_scalar(val["last"][c][:], val["last"][c][:], float(SKIP), None,
                                        ALU.add).then_inc(order, 1)
                n += 1
            dve.wait_ge(order, n)
            nc.vector.memset(nxt[0][:, 0:1], 0.0).then_inc(values_ready, 1)
            at = 0
            for c, (t0, rows) in enumerate(chunks):
                for name in names:
                    dve.wait_ge(turned, at + 1)
                    where = {"src": [k["ci"][:, t0:t0 + rows, 0], k["li_src"][:, t0:t0 + rows, 0]],
                             "gather_dst": [k["ci"][:, t0:t0 + rows, 1]],
                             "last": [k["ci"][:, t0:t0 + rows, 2]],
                             "dst": [k["cf"][:, t0:t0 + rows, 0]],
                             "prev": [k["cf"][:, t0:t0 + rows, 1]],
                             "pen": [k["cf"][:, t0:t0 + rows, 2]],
                             "weight": [k["li_src"][:, t0:t0 + rows, 1]]}[name]
                    for q, w in enumerate(where):
                        ins = nc.vector.tensor_copy(w, tp[at % 2][:, 0:rows])
                        if q == len(where) - 1:
                            ins.then_inc(copied, 1)
                    at += 1

        @block.tensor
        def _(pe):
            pe.wait_ge(values_ready, 1)
            at = 0
            for c, (t0, rows) in enumerate(chunks):
                for name in names:
                    if at >= 2:
                        pe.wait_ge(copied, at - 1)
                    nc.tensor.transpose(tp[at % 2][:, 0:rows], val[name][c][0:rows, :],
                                        k["ident"][0:rows, 0:rows]).then_inc(turned, 1)
                    at += 1


def first_norm(nc, k, x, h0, x1, agg1, agg2):
    R = k["rows"]
    U = 3
    D = x.shape[1]
    with ExitStack() as ctx:
        ph = Phase(nc, ctx, "ln1")
        xs = [ph.sb(f"x{s}", [P, J, D]) for s in range(U)]
        hs = [ph.sb(f"h{s}", [P, J, D]) for s in range(U)]
        st = [ph.sb(f"st{s}", [P, J, 6]) for s in range(U)]
        mv = [ph.sb(f"mv{s}", [P, J, 2]) for s in range(U)]
        sd = [ph.sb(f"sd{s}", [P, J]) for s in range(U)]
        rs = [ph.sb(f"rs{s}", [P, J]) for s in range(U)]
        nm = [ph.sb(f"nm{s}", [P, J]) for s in range(U)]
        neutral = [ph.sb("neutral1", [P, agg1.shape[1]]), ph.sb("neutral2", [P, agg2.shape[1]])]
        loaded, stored_h, stored_x = ph.sems("loaded", U), ph.sems("stored_h", U), ph.sems("stored_x", U)
        dumped, neutral_ready, agg_cleared = ph.sem("dumped"), ph.sem("neutral_ready"), ph.sem("agg_cleared")
        stats, moments, root, inverse, shift = (ph.sem(n) for n in ("stats", "moments", "root", "inverse", "shift"))
        normed = ph.sem("normed")
        block = ctx.enter_context(nc.Block())

        @block.sync
        def _(sp):
            def load(t):
                if not (t.static and t.n < U):
                    sp.wait_ge(normed, (t.n - U + 1) * J)
                    settle(sp, k["passed"]["sp"])
                    sp.wait_ge(stored_x[t.slot], 16 * t.u)
                ap, p = R.dram(x, t)
                w = R.width(t)
                settle(sp, k["passed"]["sp"])
                sp.dma_start(xs[t.slot][0:p, 0:w, :], ap).then_inc(loaded[t.slot], 16)

            def store_x(t):
                sp.wait_ge(loaded[t.slot], 16 * (t.u + 1))
                ap, p = R.dram(x1, t)
                settle(sp, k["passed"]["sp"])
                sp.dma_start(ap, xs[t.slot][0:p, 0:R.width(t), :]).then_inc(stored_x[t.slot], 16)

            pipeline(sp, R.turns, U, [(0, load), (1, store_x)], R.supers)
            sp.dma_start(x1[R.n:R.n + P, :], xs[0][:, 0, :]).then_inc(dumped, 16)
            sp.wait_ge(dumped, 16)
            for s in range(U):
                sp.wait_ge(stored_x[s], 16 * ((R.turns - 1 - s) // U + 1))

        @block.vector
        def _(dve):
            for a, ag, hd in ((neutral[0], agg1, k["h1"]), (neutral[1], agg2, 1)):
                w = ag.shape[1]
                f = k["agg_m"][hd]
                nc.vector.memset(a[:, 0:f], 0.0).then_inc(neutral_ready, 1)
                nc.vector.memset(a[:, f:w], -BIG).then_inc(neutral_ready, 1)

            def statistics(t):
                dve.wait_ge(loaded[t.slot], 16 * (t.u + 1))
                wait_count(dve, moments, t.n - U + 1)
                for j in range(R.width(t)):
                    ins = nc.vector.bn_stats(st[t.slot][:, j, :], xs[t.slot][:, j, :])
                ins.then_inc(stats, 1)
                wait_count(dve, root, t.n - U + 1)
                wait_count(dve, shift, t.n - U + 1)
                dve.wait_ge(stats, t.n + 1)
                settle(dve, k["passed"]["dve"])
                for j in range(R.width(t)):
                    ins = nc.vector.bn_aggr(mv[t.slot][:, j, :], st[t.slot][:, j, :])
                ins.then_inc(moments, 1)

            def scales(t):
                dve.wait_ge(root, t.n + 1)
                wait_count(dve, normed, (t.n - U + 1) * J)
                nc.vector.reciprocal(rs[t.slot][:], sd[t.slot][:]).then_inc(inverse, 1)
                dve.wait_ge(inverse, t.n + 1)
                nc.vector.scalar_tensor_tensor(out=nm[t.slot][:], in0=mv[t.slot][:, :, 0], scalar=-1.0,
                                               in1=rs[t.slot][:], op0=ALU.mult, op1=ALU.mult).then_inc(shift, 1)

            pipeline(dve, R.turns, U, [(0, statistics), (1, scales)], R.supers)

        @block.scalar
        def _(act):
            def deviation(t):
                act.wait_ge(moments, t.n + 1)
                wait_count(act, inverse, t.n - U + 1)
                nc.scalar.activation(sd[t.slot][:], mv[t.slot][:, :, 1], ACT.Sqrt, bias=k["eps"][:, 0:1]).then_inc(root, 1)

            def normalise(t):
                act.wait_ge(shift, t.n + 1)
                wait_count(act, stored_h[t.slot], 16 * t.u)
                for j in range(R.width(t)):
                    nc.scalar.activation(hs[t.slot][:, j, :], xs[t.slot][:, j, :], ACT.Relu,
                                         bias=nm[t.slot][:, j:j + 1], scale=rs[t.slot][:, j:j + 1]).then_inc(normed, 1)

            pipeline(act, R.turns, U, [(0, deviation), (1, normalise)], R.supers)

        @block.gpsimd
        def _(pool):
            pool.wait_ge(neutral_ready, 4)

            def store_h(t):
                pool.wait_ge(normed, t.n * J + R.width(t))
                ap, p = R.dram(h0, t)
                settle(pool, k["passed"]["pool"])
                pool.dma_start(ap, hs[t.slot][0:p, 0:R.width(t), :]).then_inc(stored_h[t.slot], 16)

            def clear_agg(t):
                for a, ag in zip(neutral, (agg1, agg2)):
                    ap, p = R.dram(ag, t)
                    w = R.width(t)
                    settle(pool, k["passed"]["pool"])
                    pool.dma_start(ap, a[0:p, :].unsqueeze(1).to_broadcast([p, w, ag.shape[1]])).then_inc(agg_cleared, 16)

            pipeline(pool, R.turns, U, [(0, clear_agg), (1, store_h)], R.supers)
            pool.wait_ge(agg_cleared, 32 * R.turns)
            for s in range(U):
                pool.wait_ge(stored_h[s], 16 * ((R.turns - 1 - s) // U + 1))


def weighted_scatter(nc, k, h0, x1):
    T, U = k["t"], 4
    D = h0.shape[1]
    with ExitStack() as ctx:
        ph = Phase(nc, ctx, "l0")
        cols = [ph.sb(f"cols{s}", [P, 2]) for s in range(U)]
        gidx = [ph.sb(f"gidx{s}", [P, 1], I32) for s in range(U)]
        hd = [ph.sb(f"hd{s}", [P, D]) for s in range(U)]
        v = [ph.sb(f"v{s}", [P, D]) for s in range(U)]
        same = [ph.sb(f"same{s}", [P, P]) for s in range(U)]
        junk = ph.sb("junk", [P, P])
        before = [ph.sb(f"before{s}", [P, 1]) for s in range(U)]
        repeat = [ph.sb(f"repeat{s}", [P, 1]) for s in range(U)]
        way = [ph.sb(f"way{s}", [P, 1]) for s in range(U)]
        sidx = [ph.sb(f"sidx{s}", [P, 1], I32) for s in range(U)]
        sums = [ph.sb(f"sums{s}", [P, D]) for s in range(U)]
        row = [ph.ps(f"row{s}", [P, P]) for s in range(2)]
        acc = [ph.ps(f"acc{s}", [P, D]) for s in range(2)]
        gathered, added = ph.sems("gathered", U), ph.sem("added")
        names = ("cols_ready", "gidx_ready", "row_ready", "same_ready", "before_ready", "repeat_ready",
                 "way_ready", "sidx_ready", "v_ready", "acc_ready", "sums_ready")
        s = {n: ph.sem(n) for n in names}
        block = ctx.enter_context(nc.Block())

        @block.scalar
        def _(act):
            def stage(t):
                wait_count(act, gathered[t.slot], 16 * t.u)
                nc.scalar.copy(gidx[t.slot][:], k["ci"][:, bass.ds(t.n, 1), 1]).then_inc(s["gidx_ready"], 1)
                wait_count(act, s["sidx_ready"], t.n - U + 1)
                wait_count(act, s["v_ready"], t.n - U + 1)
                nc.scalar.copy(cols[t.slot][:], k["li_src"][:, bass.ds(t.n, 1), :].rearrange("p a b -> p (a b)")
                               ).then_inc(s["cols_ready"], 1)

            def weigh(t):
                act.wait_ge(gathered[t.slot], 16 * (t.u + 1))
                act.wait_ge(s["cols_ready"], t.n + 1)
                wait_count(act, s["acc_ready"], t.n - U + 1)
                nc.scalar.activation(v[t.slot][:], hd[t.slot][:], ACT.Copy,
                                     scale=cols[t.slot][:, 1:2]).then_inc(s["v_ready"], 1)

            pipeline(act, T, U, [(0, stage), (2, weigh)])

        @block.tensor
        def _(pe):
            def row_of(t):
                pe.wait_ge(s["cols_ready"], t.n + 1)
                wait_count(pe, s["same_ready"], t.n - 1)
                nc.tensor.transpose(row[t.slot % 2][:], cols[t.slot][:, 0:1].to_broadcast([P, P]),
                                    k["ident"][:]).then_inc(s["row_ready"], 1)

            def total(t):
                pe.wait_ge(s["v_ready"], t.n + 1)
                pe.wait_ge(s["same_ready"], t.n + 1)
                wait_count(pe, s["sums_ready"], t.n - 1)
                nc.tensor.matmul(acc[t.slot % 2][:], same[t.slot][:], v[t.slot][:], start=True,
                                 stop=True).then_inc(s["acc_ready"], 1)

            pipeline(pe, T, U, [(1, row_of), (2, total)])

        @block.vector
        def _(dve):
            def match(t):
                dve.wait_ge(s["row_ready"], t.n + 1)
                wait_count(dve, s["acc_ready"], t.n - U + 1)
                nc.vector.tensor_scalar(same[t.slot][:], row[t.slot % 2][:], cols[t.slot][:, 0:1], None,
                                        ALU.is_equal).then_inc(s["same_ready"], 1)
                dve.wait_ge(s["same_ready"], t.n + 1)
                wait_count(dve, s["repeat_ready"], t.n - U + 1)
                nc.vector.tensor_tensor_reduce(junk[:], same[t.slot][:], k["below"][:], 1.0, 0.0, ALU.mult, ALU.add,
                                               before[t.slot][:]).then_inc(s["before_ready"], 1)
                nc.vector.tensor_tensor(way[t.slot][:], k["dump"][:], cols[t.slot][:, 0:1],
                                        ALU.subtract).then_inc(s["way_ready"], 1)
                dve.wait_ge(s["before_ready"], t.n + 1)
                nc.vector.tensor_scalar(repeat[t.slot][:], before[t.slot][:], 1.0, None,
                                        ALU.min).then_inc(s["repeat_ready"], 1)
                wait_count(dve, added, 16 * (t.n - U + 1))
                dve.wait_ge(s["way_ready"], t.n + 1)
                dve.wait_ge(s["repeat_ready"], t.n + 1)
                nc.vector.scalar_tensor_tensor(out=sidx[t.slot][:], in0=way[t.slot][:], scalar=repeat[t.slot][:, 0:1],
                                               in1=cols[t.slot][:, 0:1], op0=ALU.mult,
                                               op1=ALU.add).then_inc(s["sidx_ready"], 1)

            def drain(t):
                dve.wait_ge(s["acc_ready"], t.n + 1)
                wait_count(dve, added, 16 * (t.n - U + 1))
                nc.vector.tensor_copy(sums[t.slot][:], acc[t.slot % 2][:]).then_inc(s["sums_ready"], 1)

            pipeline(dve, T, U, [(1, match), (2, drain)])

        @block.gpsimd
        def _(pool):
            def gather(t):
                pool.wait_ge(s["gidx_ready"], t.n + 1)
                wait_count(pool, s["v_ready"], t.n - U + 1)
                settle(pool, k["passed"]["pool"])
                pool.indirect_dma_start(hd[t.slot][:], None, h0, bass.IndirectOffsetOnAxis(gidx[t.slot][:], 0),
                                        bounds_check=k["n"] - 1).then_inc(gathered[t.slot], 16)

            def scatter(t):
                pool.wait_ge(s["sidx_ready"], t.n + 1)
                pool.wait_ge(s["sums_ready"], t.n + 1)
                wait_count(pool, added, 16 * t.n)
                settle(pool, k["passed"]["pool"])
                pool.indirect_dma_start(x1, bass.IndirectOffsetOnAxis(sidx[t.slot][:], 0), sums[t.slot][:], None,
                                        bounds_check=k["n"] + P - 1, compute_op=ALU.add).then_inc(added, 16)

            pipeline(pool, T, U, [(0, gather), (3, scatter)])
            pool.wait_ge(added, 16 * T)


def node_projections(nc, k, x1, wl, wr, xl, xr):
    R = k["rows"]
    U = 3
    D, F, H = x1.shape[1], wl.shape[1], k["h1"]
    C = F // H
    KC = D // P
    with ExitStack() as ctx:
        ph = Phase(nc, ctx, "np1")
        w_sb = ph.sb("w", [P, 2, KC, F])
        xs = [ph.sb(f"x{s}", [P, J, D]) for s in range(U)]
        hs = [ph.sb(f"h{s}", [P, J, D]) for s in range(2)] + [None]
        hs[2] = ph.sb("h2", [P, J, D])
        st = [ph.sb(f"st{s}", [P, J, 6]) for s in range(U)]
        mv = [ph.sb(f"mv{s}", [P, J, 2]) for s in range(U)]
        sd = [ph.sb(f"sd{s}", [P, J]) for s in range(U)]
        rs = [ph.sb(f"rs{s}", [P, J]) for s in range(U)]
        nm = [ph.sb(f"nm{s}", [P, J]) for s in range(U)]
        hT = [ph.sb(f"hT{s}", [P, D]) for s in range(2)]
        ls = [ph.sb(f"l{s}", [P, J, F]) for s in range(U)]
        rr = [ph.sb(f"r{s}", [P, J, F]) for s in range(U)]
        g = [ph.sb(f"g{s}", [P, F]) for s in range(2)]
        lk = ph.sb("lk", [P, F])
        junk = ph.sb("junk", [P, F])
        own = [ph.sb(f"own{s}", [P, J, H]) for s in range(U)]
        hp = [ph.ps(f"hp{s}", [P, D]) for s in range(2)]
        lp = [ph.ps(f"lp{s}", [P, F]) for s in range(2)]
        rp = [ph.ps(f"rp{s}", [P, F]) for s in range(2)]
        loaded, stored_l, stored_r = ph.sems("loaded", U), ph.sems("stored_l", U), ph.sems("stored_r", U)
        names = ("weights", "stats", "moments", "root", "inverse", "shift", "normed", "turned", "hT_ready",
                 "lp_ready", "rp_ready", "l_ready", "r_ready", "g_ready", "lk_ready", "own_ready", "own_kept")
        s = {n: ph.sem(n) for n in names}
        block = ctx.enter_context(nc.Block())
        sub = lambda t, j: t.n * J + j

        def half(j):
            return j % 2

        @block.sync
        def _(sp):
            for i, w in enumerate((wl, wr)):
                for c in range(KC):
                    sp.dma_start(w_sb[:, i, c, :], w[c * P:(c + 1) * P, :]).then_inc(s["weights"], 16)

            def load(t):
                wait_count(sp, s["normed"], (t.n - U + 1) * J)
                ap, p = R.dram(x1, t)
                settle(sp, k["passed"]["sp"])
                sp.dma_start(xs[t.slot][0:p, 0:R.width(t), :], ap).then_inc(loaded[t.slot], 16)

            def store(t):
                w = R.width(t)
                sp.wait_ge(s["l_ready"], t.n * J + w)
                ap, p = R.dram(xl, t)
                settle(sp, k["passed"]["sp"])
                sp.dma_start(ap, ls[t.slot][0:p, 0:w, :]).then_inc(stored_l[t.slot], 16)
                sp.wait_ge(s["r_ready"], t.n * J + w)
                ap, p = R.dram(xr, t)
                settle(sp, k["passed"]["sp"])
                sp.dma_start(ap, rr[t.slot][0:p, 0:w, :]).then_inc(stored_r[t.slot], 16)

            pipeline(sp, R.turns, U, [(0, load), (3, store)], R.supers)
            for q in range(U):
                sp.wait_ge(stored_l[q], 16 * ((R.turns - 1 - q) // U + 1))
                sp.wait_ge(stored_r[q], 16 * ((R.turns - 1 - q) // U + 1))

        @block.vector
        def _(dve):
            def statistics(t, j):
                if j == 0:
                    dve.wait_ge(loaded[t.slot], 16 * (t.u + 1))
                    wait_count(dve, s["moments"], t.n - U + 1)
                ins = nc.vector.bn_stats(st[t.slot][:, j, :], xs[t.slot][:, j, :])
                if j == R.width(t) - 1:
                    ins.then_inc(s["stats"], 1)

            def moments(t):
                wait_count(dve, s["root"], t.n - U + 1)
                wait_count(dve, s["shift"], t.n - U + 1)
                dve.wait_ge(s["stats"], t.n + 1)
                settle(dve, k["passed"]["dve"])
                for j in range(R.width(t)):
                    ins = nc.vector.bn_aggr(mv[t.slot][:, j, :], st[t.slot][:, j, :])
                ins.then_inc(s["moments"], 1)

            def scales(t):
                dve.wait_ge(s["root"], t.n + 1)
                wait_count(dve, s["normed"], (t.n - U + 1) * J)
                nc.vector.reciprocal(rs[t.slot][:], sd[t.slot][:]).then_inc(s["inverse"], 1)
                dve.wait_ge(s["inverse"], t.n + 1)
                nc.vector.scalar_tensor_tensor(out=nm[t.slot][:], in0=mv[t.slot][:, :, 0], scalar=-1.0,
                                               in1=rs[t.slot][:], op0=ALU.mult, op1=ALU.mult).then_inc(s["shift"], 1)

            def right(t, j):
                dve.wait_ge(s["rp_ready"], sub(t, j) + 1)
                if j == 0:
                    wait_count(dve, stored_r[t.slot], 16 * t.u)
                    wait_count(dve, s["g_ready"], (t.n - U + 1) * J)
                nc.vector.tensor_copy(rr[t.slot][:, j, :], rp[half(j)][:]).then_inc(s["r_ready"], 1)

            def own_score(t, j):
                dve.wait_ge(s["g_ready"], sub(t, j) + 1)
                if j == 0:
                    wait_count(dve, s["own_kept"], t.n - U + 1)
                wait_count(dve, s["own_ready"], sub(t, j))
                nc.vector.scalar_tensor_tensor(out=lk[:], in0=g[half(j)][:], scalar=SLOPE, in1=g[half(j)][:],
                                               op0=ALU.mult, op1=ALU.max).then_inc(s["lk_ready"], 1)
                dve.wait_ge(s["lk_ready"], sub(t, j) + 1)
                for h in range(H):
                    ins = nc.vector.tensor_tensor_reduce(junk[:, h * C:(h + 1) * C], lk[:, h * C:(h + 1) * C],
                                                         k["a1"][:, h * C:(h + 1) * C], 1.0, 0.0, ALU.mult, ALU.add,
                                                         own[t.slot][:, j, h:h + 1])
                ins.then_inc(s["own_ready"], 1)

            def keep(t):
                w = R.width(t)
                dve.wait_ge(s["own_ready"], t.n * J + w)
                nc.vector.tensor_copy(k["own1"][:, bass.ds(t.n * J, w), :],
                                      own[t.slot][:, 0:w, :]).then_inc(s["own_kept"], 1)

            steps = [(1, scales)] + staggered(R, [(0, 0, statistics), (1, 2, right), (2, 2, own_score)])
            pipeline(dve, R.turns, U, steps + [(0, moments), (2, keep)], R.supers)

        @block.scalar
        def _(act):
            def deviation(t):
                act.wait_ge(s["moments"], t.n + 1)
                wait_count(act, s["inverse"], t.n - U + 1)
                nc.scalar.activation(sd[t.slot][:], mv[t.slot][:, :, 1], ACT.Sqrt,
                                     bias=k["eps"][:, 0:1]).then_inc(s["root"], 1)

            def normalise(t, j):
                if j == 0:
                    act.wait_ge(s["shift"], t.n + 1)
                    wait_count(act, s["turned"], (t.n - U + 1) * J)
                nc.scalar.activation(hs[t.slot][:, j, :], xs[t.slot][:, j, :], ACT.Relu,
                                     bias=nm[t.slot][:, j:j + 1], scale=rs[t.slot][:, j:j + 1]).then_inc(s["normed"], 1)

            def turn(t, j):
                act.wait_ge(s["turned"], sub(t, j) + 1)
                wait_count(act, s["rp_ready"], sub(t, j) - 1)
                nc.scalar.copy(hT[half(j)][:], hp[half(j)][:]).then_inc(s["hT_ready"], 1)

            def left(t, j):
                act.wait_ge(s["lp_ready"], sub(t, j) + 1)
                if j == 0:
                    wait_count(act, stored_l[t.slot], 16 * t.u)
                    wait_count(act, s["g_ready"], (t.n - U + 1) * J)
                nc.scalar.copy(ls[t.slot][:, j, :], lp[half(j)][:]).then_inc(s["l_ready"], 1)

            steps = [(1, deviation)] + staggered(R, [(0, 2, turn), (0, 1, normalise), (1, 2, left)])
            pipeline(act, R.turns, U, steps, R.supers)

        @block.gpsimd
        def _(pool):
            def add(t, j):
                pool.wait_ge(s["l_ready"], sub(t, j) + 1)
                pool.wait_ge(s["r_ready"], sub(t, j) + 1)
                wait_count(pool, s["lk_ready"], sub(t, j) - 1)
                nc.gpsimd.tensor_tensor(g[half(j)][:], ls[t.slot][:, j, :], rr[t.slot][:, j, :],
                                        ALU.add).then_inc(s["g_ready"], 1)

            pipeline(pool, R.turns, U, staggered(R, [(0, 2, add)]), R.supers)

        @block.tensor
        def _(pe):
            pe.wait_ge(s["weights"], 16 * 2 * KC)

            def transposes(t, j):
                pe.wait_ge(s["normed"], sub(t, j) + 1)
                wait_count(pe, s["hT_ready"], sub(t, j) - 1)
                for c in range(KC):
                    ins = nc.tensor.transpose(hp[half(j)][:, c * P:(c + 1) * P], hs[t.slot][:, j, c * P:(c + 1) * P],
                                              k["ident"][:])
                ins.then_inc(s["turned"], 1)

            def products(t, j):
                pe.wait_ge(s["hT_ready"], sub(t, j) + 1)
                for i, (bank, ready, free) in enumerate(((lp, "lp_ready", "l_ready"), (rp, "rp_ready", "r_ready"))):
                    wait_count(pe, s[free], sub(t, j) - 1)
                    for c in range(KC):
                        ins = nc.tensor.matmul(bank[half(j)][:], hT[half(j)][:, c * P:(c + 1) * P], w_sb[:, i, c, :],
                                               start=(c == 0), stop=(c == KC - 1))
                    ins.then_inc(s[ready], 1)

            pipeline(pe, R.turns, U, staggered(R, [(0, 2, transposes), (1, 2, products)]), R.supers)


def edge_softmax(nc, k, name, xl, xr, agg, att, H):
    T, U = k["t"], 4
    F = xl.shape[1]
    C = F // H
    W = agg.shape[1]
    with ExitStack() as ctx:
        ph = Phase(nc, ctx, name)
        cols = [ph.sb(f"cols{q}", [P, 3]) for q in range(U)]
        idx = [ph.sb(f"idx{q}", [P, 3], I32) for q in range(U)]
        gl = [ph.sb(f"gl{q}", [P, F]) for q in range(U)]
        gr = [ph.sb(f"gr{q}", [P, F]) for q in range(U)]
        g = [ph.sb(f"g{q}", [P, F]) for q in range(2)]
        lk = [ph.sb(f"lk{q}", [P, F]) for q in range(2)]
        junk = ph.sb("junk", [P, F])
        junk2 = ph.sb("junk2", [P, H, P])
        e = [ph.sb(f"e{q}", [P, H]) for q in range(U)]
        same = [ph.sb(f"same{q}", [P, P]) for q in range(U)]
        away = [ph.sb(f"away{q}", [P, P]) for q in range(2)]
        link = [ph.sb(f"link{q}", [P, P]) for q in range(U)]
        here = [ph.sb(f"here{q}", [P, H]) for q in range(2)]
        past = [ph.sb(f"past{q}", [P, H]) for q in range(2)]
        m = [ph.sb(f"m{q}", [P, H]) for q in range(U)]
        dif = [ph.sb(f"dif{q}", [P, 2, H]) for q in range(2)]
        pf = [ph.sb(f"pf{q}", [P, 2, H]) for q in range(U)]
        v = [ph.sb(f"v{q}", [P, F]) for q in range(2)]
        old = [ph.sb(f"old{q}", [P, F]) for q in range(2)]
        oldd = [ph.sb(f"oldd{q}", [P, H]) for q in range(2)]
        f_sb = [ph.sb(f"f{q}", [P, H]) for q in range(2)]
        out = [ph.sb(f"out{q}", [P, W]) for q in range(U)]
        row = ph.ps("row", [P, P])
        eb = [ph.ps(f"eb{q}", [P, H, P]) for q in range(2)]
        acc = [ph.ps(f"acc{q}", [P, F]) for q in range(2)]
        mb = ph.ps("mb", [P, H])
        fb = ph.ps("fb", [P, H])
        den_all = ph.ps("den", [P, H])
        den = [den_all[:], den_all[:]]
        gl_in, gr_in, written = ph.sems("gl_in", U), ph.sems("gr_in", U), ph.sems("written", U)
        names = ("cols_ready", "idx_ready", "g_ready", "lk_ready", "e_ready", "row_ready", "same_ready", "away_ready",
                 "eb_ready", "here_ready", "mb_ready", "past_ready", "m_ready", "dif_ready", "pf_ready", "fb_ready",
                 "v_ready", "old_ready", "acc_ready", "out_ready", "outm_ready", "start_ready", "fs_ready")
        s = {n: ph.sem(n) for n in names}
        block = ctx.enter_context(nc.Block())

        @block.scalar
        def _(act):
            def stage(t):
                wait_count(act, gl_in[t.slot], 16 * t.u)
                wait_count(act, gr_in[t.slot], 16 * t.u)
                wait_count(act, written[t.slot], 16 * t.u)
                nc.scalar.copy(idx[t.slot][:], k["ci"][:, bass.ds(t.n, 1), :].rearrange("p a b -> p (a b)")
                               ).then_inc(s["idx_ready"], 1)
                wait_count(act, s["past_ready"], t.n - U + 1)
                nc.scalar.copy(cols[t.slot][:], k["cf"][:, bass.ds(t.n, 1), :].rearrange("p a b -> p (a b)")
                               ).then_inc(s["cols_ready"], 1)

            def exponent(t):
                act.wait_ge(s["dif_ready"], t.n + 1)
                wait_count(act, s["acc_ready"], t.n - U + 1)
                nc.scalar.activation(pf[t.slot][:], dif[t.slot % 2][:], ACT.Exp).then_inc(s["pf_ready"], 1)

            def weigh(t):
                act.wait_ge(s["pf_ready"], t.n + 1)
                act.wait_ge(gl_in[t.slot], 16 * (t.u + 1))
                wait_count(act, s["acc_ready"], t.n - 1)
                for h in range(H):
                    ins = nc.scalar.activation(v[t.slot % 2][:, h * C:(h + 1) * C], gl[t.slot][:, h * C:(h + 1) * C],
                                               ACT.Copy, scale=pf[t.slot][:, 0, h:h + 1])
                ins.then_inc(s["v_ready"], 1)

            def drain(t):
                act.wait_ge(s["acc_ready"], t.n + 1)
                wait_count(act, written[t.slot], 16 * t.u)
                nc.scalar.copy(out[t.slot][:, 0:F], acc[t.slot % 2][:])
                nc.scalar.copy(out[t.slot][:, F:F + H], den[t.slot % 2]).then_inc(s["out_ready"], 1)

            pipeline(act, T, U, [(0, stage), (2, exponent), (2, weigh), (3, drain)])

        @block.gpsimd
        def _(pool):
            def gather(t):
                pool.wait_ge(s["idx_ready"], t.n + 1)
                wait_count(pool, s["v_ready"], t.n - U + 1)
                settle(pool, k["passed"]["pool"])
                pool.indirect_dma_start(gl[t.slot][:], None, xl, bass.IndirectOffsetOnAxis(idx[t.slot][:, 0:1], 0),
                                        bounds_check=k["n"] - 1).then_inc(gl_in[t.slot], 16)
                wait_count(pool, s["g_ready"], t.n - U + 1)
                settle(pool, k["passed"]["pool"])
                pool.indirect_dma_start(gr[t.slot][:], None, xr, bass.IndirectOffsetOnAxis(idx[t.slot][:, 1:2], 0),
                                        bounds_check=k["n"] - 1).then_inc(gr_in[t.slot], 16)

            def write(t):
                pool.wait_ge(s["out_ready"], t.n + 1)
                pool.wait_ge(s["outm_ready"], t.n + 1)
                settle(pool, k["passed"]["pool"])
                pool.indirect_dma_start(agg, bass.IndirectOffsetOnAxis(idx[t.slot][:, 2:3], 0), out[t.slot][:], None,
                                        bounds_check=k["n"] - 1, oob_is_err=False).then_inc(written[t.slot], 16)

            pipeline(pool, T, U, [(0, gather), (3, write)])
            for q in range(U):
                pool.wait_ge(written[q], 16 * ((T - 1 - q) // U + 1))

        @block.vector
        def _(dve):
            nc.vector.memset(m[U - 1][:], 0.0).then_inc(s["start_ready"], 1)

            def score(t):
                q = t.slot % 2
                dve.wait_ge(gl_in[t.slot], 16 * (t.u + 1))
                dve.wait_ge(gr_in[t.slot], 16 * (t.u + 1))
                wait_count(dve, s["lk_ready"], t.n - 1)
                nc.vector.tensor_tensor(g[q][:], gl[t.slot][:], gr[t.slot][:], ALU.add).then_inc(s["g_ready"], 1)
                dve.wait_ge(s["g_ready"], t.n + 1)
                wait_count(dve, s["e_ready"], t.n - 1)
                nc.vector.scalar_tensor_tensor(out=lk[q][:], in0=g[q][:], scalar=SLOPE, in1=g[q][:], op0=ALU.mult,
                                               op1=ALU.max).then_inc(s["lk_ready"], 1)
                wait_count(dve, s["eb_ready"], t.n - U + 1)
                dve.wait_ge(s["lk_ready"], t.n + 1)
                for h in range(H):
                    ins = nc.vector.tensor_tensor_reduce(junk[:, h * C:(h + 1) * C], lk[q][:, h * C:(h + 1) * C],
                                                         att[:, h * C:(h + 1) * C], 1.0, 0.0, ALU.mult, ALU.add,
                                                         e[t.slot][:, h:h + 1])
                ins.then_inc(s["e_ready"], 1)

            def match(t):
                dve.wait_ge(s["row_ready"], t.n + 1)
                wait_count(dve, s["acc_ready"], t.n - U + 1)
                nc.vector.tensor_scalar(same[t.slot][:], row[:], cols[t.slot][:, 0:1], None, ALU.is_equal)
                nc.vector.tensor_scalar(link[t.slot][:], row[:], cols[t.slot][:, 1:2], None,
                                        ALU.is_equal).then_inc(s["same_ready"], 1)
                dve.wait_ge(s["same_ready"], t.n + 1)
                wait_count(dve, s["here_ready"], t.n - 1)
                nc.vector.tensor_scalar(away[t.slot % 2][:], same[t.slot][:], BIG, -BIG, ALU.mult,
                                        ALU.add).then_inc(s["away_ready"], 1)

            def maximum(t):
                q = t.slot % 2
                dve.wait_ge(s["eb_ready"], t.n + 1)
                wait_count(dve, s["m_ready"], t.n - 1)
                dve.wait_ge(s["away_ready"], t.n + 1)
                settle(dve, k["passed"]["dve"])
                for h in range(H):
                    ins = nc.vector.tensor_tensor_reduce(junk2[:, h, :], eb[q][:, h, :], away[q][:], 1.0, -3.0e38, ALU.add,
                                                         ALU.max, here[q][:, h:h + 1])
                ins.then_inc(s["here_ready"], 1)
                dve.wait_ge(s["mb_ready"], t.n + 1)
                wait_count(dve, s["dif_ready"], t.n - 1)
                nc.vector.tensor_scalar(past[q][:], mb[:], cols[t.slot][:, 2:3], None, ALU.add
                                        ).then_inc(s["past_ready"], 1)
                dve.wait_ge(s["past_ready"], t.n + 1)
                wait_count(dve, s["outm_ready"], t.n - U + 1)
                dve.wait_ge(s["here_ready"], t.n + 1)
                nc.vector.tensor_tensor(m[t.slot][:], past[q][:], here[q][:], ALU.max).then_inc(s["m_ready"], 1)
                dve.wait_ge(s["m_ready"], t.n + 1)
                wait_count(dve, s["pf_ready"], t.n - 1)
                nc.vector.tensor_tensor(dif[q][:, 0, :], e[t.slot][:], m[t.slot][:], ALU.subtract)
                nc.vector.tensor_tensor(dif[q][:, 1, :], past[q][:], m[t.slot][:],
                                        ALU.subtract).then_inc(s["dif_ready"], 1)
                wait_count(dve, written[t.slot], 16 * t.u)
                nc.vector.tensor_copy(out[t.slot][:, F + H:F + 2 * H], m[t.slot][:]).then_inc(s["outm_ready"], 1)

            def carry(t):
                if t.static and t.n == 0:
                    nc.vector.memset(old[0][:], 0.0)
                    nc.vector.memset(oldd[0][:], 0.0).then_inc(s["old_ready"], 1)
                    return
                q = t.slot % 2
                past_out = out[(t.slot - 1) % U]
                dve.wait_ge(s["fb_ready"], t.n + 1)
                nc.vector.tensor_copy(f_sb[q][:], fb[:]).then_inc(s["fs_ready"], 1)
                dve.wait_ge(s["out_ready"], t.n)
                dve.wait_ge(s["fs_ready"], t.n)
                nc.vector.tensor_tensor(oldd[q][:], past_out[:, F:F + H], f_sb[q][:], ALU.mult)
                nc.vector.tensor_tensor(old[q][:].rearrange("p (h c) -> p h c", h=H),
                                        past_out[:, 0:F].rearrange("p (h c) -> p h c", h=H),
                                        f_sb[q][:].unsqueeze(2).to_broadcast([P, H, C]),
                                        ALU.mult).then_inc(s["old_ready"], 1)

            pipeline(dve, T, U, [(2, maximum), (1, score), (1, match), (2, carry)])

        @block.tensor
        def _(pe):
            pe.wait_ge(s["start_ready"], 1)

            def row_of(t):
                pe.wait_ge(s["cols_ready"], t.n + 1)
                wait_count(pe, s["same_ready"], t.n)
                nc.tensor.transpose(row[:], cols[t.slot][:, 0:1].to_broadcast([P, P]),
                                    k["ident"][:]).then_inc(s["row_ready"], 1)

            def scores(t):
                pe.wait_ge(s["e_ready"], t.n + 1)
                wait_count(pe, s["here_ready"], t.n - 1)
                for h in range(H):
                    ins = nc.tensor.transpose(eb[t.slot % 2][:, h, :], e[t.slot][:, h:h + 1].to_broadcast([P, P]),
                                              k["ident"][:])
                ins.then_inc(s["eb_ready"], 1)

            def last_maximum(t):
                wait_count(pe, s["m_ready"], t.n)
                wait_count(pe, s["past_ready"], t.n)
                nc.tensor.matmul(mb[:], k["last_row"][:], m[(t.slot - 1) % U][:], start=True,
                                 stop=True).then_inc(s["mb_ready"], 1)

            def factor(t):
                pe.wait_ge(s["pf_ready"], t.n + 1)
                if not (t.static and t.n < 2):
                    wait_count(pe, s["fs_ready"], t.n - 1)
                nc.tensor.matmul(fb[:], k["first_row"][:], pf[t.slot][:, 1, :], start=True,
                                 stop=True).then_inc(s["fb_ready"], 1)

            def total(t):
                q = t.slot % 2
                pe.wait_ge(s["v_ready"], t.n + 1)
                pe.wait_ge(s["same_ready"], t.n + 1)
                wait_count(pe, s["out_ready"], t.n - 1)
                wait_count(pe, s["old_ready"], t.n)
                nc.tensor.matmul(acc[q][:], same[t.slot][:], v[q][:], start=True, stop=False)
                pe.wait_ge(s["old_ready"], t.n + 1)
                nc.tensor.matmul(acc[q][:], link[t.slot][:], old[q][:], start=False, stop=True)
                nc.tensor.matmul(den[q], same[t.slot][:], pf[t.slot][:, 0, :], start=True, stop=False)
                nc.tensor.matmul(den[q], link[t.slot][:], oldd[q][:], start=False, stop=True).then_inc(s["acc_ready"], 1)

            pipeline(pe, T, U, [(2, last_maximum), (1, row_of), (2, factor), (1, scores), (2, total)])



def combined(nc, dve, act, b, s, k, R, U, H, own_all, F):
    def differences(t):
        w = R.width(t)
        ag = b["agg"][t.slot]
        dve.wait_ge(b["agg_in"][t.slot], 16 * (t.u + 1))
        wait_count(dve, s["dif_ready"], t.n - U + 1)
        nc.vector.tensor_tensor(b["top"][t.slot][:, 0:w, :], ag[:, 0:w, F + H:F + 2 * H],
                                own_all[:, bass.ds(t.n * J, w), :], ALU.max).then_inc(s["top_ready"], 1)
        dve.wait_ge(s["top_ready"], t.n + 1)
        wait_count(dve, s["exp_ready"], t.n - U + 1)
        nc.vector.tensor_tensor(b["dif"][t.slot][:, 0, 0:w, :], ag[:, 0:w, F + H:F + 2 * H],
                                b["top"][t.slot][:, 0:w, :], ALU.subtract)
        nc.vector.tensor_tensor(b["dif"][t.slot][:, 1, 0:w, :], own_all[:, bass.ds(t.n * J, w), :],
                                b["top"][t.slot][:, 0:w, :], ALU.subtract).then_inc(s["dif_ready"], 1)

    def exponents(t):
        w = R.width(t)
        act.wait_ge(s["dif_ready"], t.n + 1)
        wait_count(act, s["fac_ready"], t.n - U + 1)
        nc.scalar.activation(b["ex"][t.slot][:, :, 0:w, :], b["dif"][t.slot][:, :, 0:w, :],
                             ACT.Exp).then_inc(s["exp_ready"], 1)

    def factors(t):
        w = R.width(t)
        ag, wh, ex = b["agg"][t.slot], b["whole"][t.slot], b["ex"][t.slot]
        dve.wait_ge(s["exp_ready"], t.n + 1)
        nc.vector.tensor_tensor(wh[:, 0:w, :], ag[:, 0:w, F:F + H], ex[:, 0, 0:w, :],
                                ALU.mult).then_inc(s["whole_ready"], 1)
        dve.wait_ge(s["whole_ready"], 3 * t.n + 1)
        nc.vector.tensor_tensor(wh[:, 0:w, :], wh[:, 0:w, :], ex[:, 1, 0:w, :], ALU.add).then_inc(s["whole_ready"], 1)
        dve.wait_ge(s["whole_ready"], 3 * t.n + 2)
        nc.vector.reciprocal(wh[:, 0:w, :], wh[:, 0:w, :]).then_inc(s["whole_ready"], 1)
        wait_count(dve, s["mixed"], (t.n - U + 1) * J)
        dve.wait_ge(s["whole_ready"], 3 * t.n + 3)
        nc.vector.tensor_tensor(b["fac"][t.slot][:, 0, 0:w, :], wh[:, 0:w, :], ex[:, 0, 0:w, :], ALU.mult)
        nc.vector.tensor_tensor(b["fac"][t.slot][:, 1, 0:w, :], wh[:, 0:w, :], ex[:, 1, 0:w, :],
                                ALU.mult).then_inc(s["fac_ready"], 1)

    return differences, exponents, factors


COMBINED = ("top_ready", "dif_ready", "exp_ready", "whole_ready", "fac_ready", "scaled", "mixed")


def combined_buffers(ph, U, H, W):
    b = {"agg": [ph.sb(f"agg{q}", [P, J, W]) for q in range(U)],
         "top": [ph.sb(f"top{q}", [P, J, H]) for q in range(U)],
         "dif": [ph.sb(f"dif{q}", [P, 2, J, H]) for q in range(U)],
         "ex": [ph.sb(f"ex{q}", [P, 2, J, H]) for q in range(U)],
         "whole": [ph.sb(f"whole{q}", [P, J, H]) for q in range(U)],
         "fac": [ph.sb(f"fac{q}", [P, 2, J, H]) for q in range(U)],
         "agg_in": ph.sems("agg_in", U)}
    return b


def node_hidden(nc, k, xl, agg, w2l, w2r, xl2, xr2):
    R = k["rows"]
    U = 3
    H, F, G = k["h1"], xl.shape[1], w2l.shape[1]
    C = F // H
    KC = F // P
    with ExitStack() as ctx:
        ph = Phase(nc, ctx, "np2")
        w_sb = ph.sb("w", [P, KC, 2 * G])
        b = combined_buffers(ph, U, H, agg.shape[1])
        ls = [ph.sb(f"l{q}", [P, J, F]) for q in range(U)]
        mix = [ph.sb(f"mix{q}", [P, F]) for q in range(2)]
        hT = [ph.sb(f"hT{q}", [P, F]) for q in range(2)]
        lr = [ph.sb(f"lr{q}", [P, J, 2 * G]) for q in range(2)]
        g = [ph.sb(f"g{q}", [P, G]) for q in range(2)]
        lk = ph.sb("lk", [P, G])
        junk = ph.sb("junk", [P, G])
        own = [ph.sb(f"own{q}", [P, J, 1]) for q in range(U)]
        hp = [ph.ps(f"hp{q}", [P, F]) for q in range(2)]
        op = [ph.ps(f"op{q}", [P, 2 * G]) for q in range(2)]
        l_in, stored = ph.sems("l_in", U), ph.sems("stored", 6)
        names = COMBINED + ("weights", "turned", "hT_ready", "op_ready", "lr_ready", "g_ready", "lk_ready",
                            "own_ready", "own_kept")
        s = {n: ph.sem(n) for n in names}
        block = ctx.enter_context(nc.Block())
        sub = lambda t, j: t.n * J + j
        half = lambda j: j % 2
        UU = 6

        @block.sync
        def _(sp):
            for i, w in enumerate((w2l, w2r)):
                for c in range(KC):
                    sp.dma_start(w_sb[:, c, i * G:(i + 1) * G], w[c * P:(c + 1) * P, :]).then_inc(s["weights"], 16)

            def load(t):
                q = t.slot % U
                ap, p = R.dram(agg, t)
                wait_count(sp, s["mixed"], (t.n - U + 1) * J)
                settle(sp, k["passed"]["sp"])
                sp.dma_start(b["agg"][q][0:p, 0:R.width(t), :], ap).then_inc(b["agg_in"][q], 16)
                ap, p = R.dram(xl, t)
                settle(sp, k["passed"]["sp"])
                sp.dma_start(ls[q][0:p, 0:R.width(t), :], ap).then_inc(l_in[q], 16)

            def store(t):
                w = R.width(t)
                sp.wait_ge(s["lr_ready"], t.n * J + w)
                for i, table in enumerate((xl2, xr2)):
                    ap, p = R.dram(table, t)
                    settle(sp, k["passed"]["sp"])
                    sp.dma_start(ap, lr[t.slot % 2][0:p, 0:w, i * G:(i + 1) * G]).then_inc(stored[t.slot], 16)

            pipeline(sp, R.turns, UU, [(0, load), (3, store)], R.supers)
            for q in range(UU):
                sp.wait_ge(stored[q], 32 * ((R.turns - 1 - q) // UU + 1))

        def thirds(fn):
            def run(t, *a):
                n = Tile(t.u * 2 + t.slot // U, t.slot % U, U, t.static)
                return fn(n, *a)
            return run


        @block.vector
        def _(dve):
            differences, _, factors = combined(nc, dve, None, b, s, k, R, U, H, k["own1"], F)

            def mixture(t, j):
                t3 = Tile(t.u * 2 + t.slot // U, t.slot % U, U, t.static)
                if j == 0:
                    dve.wait_ge(l_in[t3.slot], 16 * (t3.u + 1))
                dve.wait_ge(s["scaled"], sub(t, j) + 1)
                for h in range(H):
                    ins = nc.vector.scalar_tensor_tensor(out=mix[half(j)][:, h * C:(h + 1) * C],
                                                         in0=ls[t3.slot][:, j, h * C:(h + 1) * C],
                                                         scalar=b["fac"][t3.slot][:, 1, j, h:h + 1],
                                                         in1=mix[half(j)][:, h * C:(h + 1) * C],
                                                         op0=ALU.mult, op1=ALU.add)
                ins.then_inc(s["mixed"], 1)

            def out_copy(t, j):
                dve.wait_ge(s["op_ready"], sub(t, j) + 1)
                if j == 0:
                    wait_stored(dve, t)
                    wait_count(dve, s["g_ready"], (t.n - 1) * J)
                nc.vector.tensor_copy(lr[t.slot % 2][:, j, :], op[half(j)][:]).then_inc(s["lr_ready"], 1)

            def wait_stored(eng, t):
                c = t.slot - 2
                v = 32 * (t.u + (c // UU) + 1)
                wait_count(eng, stored[c % UU], v)

            def own_score(t, j):
                dve.wait_ge(s["g_ready"], sub(t, j) + 1)
                if j == 0:
                    wait_count(dve, s["own_kept"], t.n - U + 1)
                wait_count(dve, s["own_ready"], sub(t, j))
                nc.vector.scalar_tensor_tensor(out=lk[:], in0=g[half(j)][:], scalar=SLOPE, in1=g[half(j)][:],
                                               op0=ALU.mult, op1=ALU.max).then_inc(s["lk_ready"], 1)
                dve.wait_ge(s["lk_ready"], sub(t, j) + 1)
                nc.vector.tensor_tensor_reduce(junk[:], lk[:], k["a2"][:], 1.0, 0.0, ALU.mult, ALU.add,
                                               own[t.slot % U][:, j, 0:1]).then_inc(s["own_ready"], 1)

            def keep(t):
                w = R.width(t)
                dve.wait_ge(s["own_ready"], t.n * J + w)
                nc.vector.tensor_copy(k["own2"][:, bass.ds(t.n * J, w), :],
                                      own[t.slot % U][:, 0:w, :]).then_inc(s["own_kept"], 1)

            steps = [(1, thirds(factors))] + staggered(R, [(0, 1, mixture), (1, 1, out_copy), (2, 1, own_score)])
            pipeline(dve, R.turns, UU, steps + [(0, thirds(differences)), (1, keep)], R.supers)

        @block.scalar
        def _(act):
            _, exponents, _ = combined(nc, None, act, b, s, k, R, U, H, k["own1"], F)

            def scale(t, j):
                q = t.slot % U
                act.wait_ge(s["fac_ready"], t.n + 1)
                wait_count(act, s["turned"], sub(t, j) - 1)
                for h in range(H):
                    ins = nc.scalar.activation(mix[half(j)][:, h * C:(h + 1) * C],
                                               b["agg"][q][:, j, h * C:(h + 1) * C], ACT.Copy,
                                               scale=b["fac"][q][:, 0, j, h:h + 1])
                ins.then_inc(s["scaled"], 1)

            def turn(t, j):
                act.wait_ge(s["turned"], sub(t, j) + 1)
                wait_count(act, s["op_ready"], sub(t, j) - 1)
                for c in range(KC):
                    ins = nc.scalar.activation(hT[half(j)][:, c * P:(c + 1) * P], hp[half(j)][:, c * P:(c + 1) * P],
                                               ACT.Relu, bias=k["b1"][:, c:c + 1])
                ins.then_inc(s["hT_ready"], 1)

            steps = staggered(R, [(0, 1, scale), (1, 1, turn)])
            pipeline(act, R.turns, UU, steps + [(0, thirds(exponents))], R.supers)

        @block.gpsimd
        def _(pool):
            def add(t, j):
                pool.wait_ge(s["lr_ready"], sub(t, j) + 1)
                wait_count(pool, s["lk_ready"], sub(t, j) - 1)
                x = lr[t.slot % 2]
                nc.gpsimd.tensor_tensor(g[half(j)][:], x[:, j, 0:G], x[:, j, G:2 * G], ALU.add).then_inc(s["g_ready"], 1)

            pipeline(pool, R.turns, UU, staggered(R, [(0, 1, add)]), R.supers)

        @block.tensor
        def _(pe):
            pe.wait_ge(s["weights"], 16 * 2 * KC)

            def transposes(t, j):
                pe.wait_ge(s["mixed"], sub(t, j) + 1)
                wait_count(pe, s["hT_ready"], sub(t, j) - 1)
                for c in range(KC):
                    ins = nc.tensor.transpose(hp[half(j)][:, c * P:(c + 1) * P], mix[half(j)][:, c * P:(c + 1) * P],
                                              k["ident"][:])
                ins.then_inc(s["turned"], 1)

            def products(t, j):
                pe.wait_ge(s["hT_ready"], sub(t, j) + 1)
                wait_count(pe, s["lr_ready"], sub(t, j) - 1)
                for c in range(KC):
                    ins = nc.tensor.matmul(op[half(j)][:], hT[half(j)][:, c * P:(c + 1) * P], w_sb[:, c, :],
                                           start=(c == 0), stop=(c == KC - 1))
                ins.then_inc(s["op_ready"], 1)

            pipeline(pe, R.turns, UU, staggered(R, [(0, 1, transposes), (1, 1, products)]), R.supers)


def node_output(nc, k, xl2, agg2, x1, out):
    R = k["rows"]
    U = 3
    F = xl2.shape[1]
    with ExitStack() as ctx:
        ph = Phase(nc, ctx, "out")
        b = combined_buffers(ph, U, 1, agg2.shape[1])
        ls = [ph.sb(f"l{q}", [P, J, F]) for q in range(U)]
        xs = [ph.sb(f"x{q}", [P, J, F]) for q in range(U)]
        mix = [ph.sb(f"mix{q}", [P, J, F]) for q in range(U)]
        ys = [ph.sb(f"y{q}", [P, J, F]) for q in range(U)]
        l_in, x_in, stored = ph.sems("l_in", U), ph.sems("x_in", U), ph.sems("stored", U)
        names = COMBINED + ("y_ready", "biased")
        s = {n: ph.sem(n) for n in names}
        block = ctx.enter_context(nc.Block())
        sub = lambda t, j: t.n * J + j

        @block.sync
        def _(sp):
            def load(t):
                q = t.slot
                w = R.width(t)
                wait_count(sp, s["mixed"], (t.n - U + 1) * J)
                ap, p = R.dram(agg2, t)
                settle(sp, k["passed"]["sp"])
                sp.dma_start(b["agg"][q][0:p, 0:w, :], ap).then_inc(b["agg_in"][q], 16)
                ap, p = R.dram(xl2, t)
                settle(sp, k["passed"]["sp"])
                sp.dma_start(ls[q][0:p, 0:w, :], ap).then_inc(l_in[q], 16)
                wait_count(sp, s["y_ready"], t.n - U + 1)
                ap, p = R.dram(x1, t)
                settle(sp, k["passed"]["sp"])
                sp.dma_start(xs[q][0:p, 0:w, :], ap).then_inc(x_in[q], 16)

            pipeline(sp, R.turns, U, [(0, load)], R.supers)

        @block.vector
        def _(dve):
            differences, _, factors = combined(nc, dve, None, b, s, k, R, U, 1, k["own2"], F)

            def mixture(t, j):
                if j == 0:
                    dve.wait_ge(l_in[t.slot], 16 * (t.u + 1))
                dve.wait_ge(s["scaled"], sub(t, j) + 1)
                nc.vector.scalar_tensor_tensor(out=mix[t.slot][:, j, :], in0=ls[t.slot][:, j, :],
                                               scalar=b["fac"][t.slot][:, 1, j, 0:1], in1=mix[t.slot][:, j, :],
                                               op0=ALU.mult, op1=ALU.add).then_inc(s["mixed"], 1)

            def result(t):
                w = R.width(t)
                dve.wait_ge(s["biased"], t.n + 1)
                wait_count(dve, stored[t.slot], 16 * t.u)
                dve.wait_ge(s["mixed"], t.n * J + w)
                nc.vector.tensor_tensor(ys[t.slot][:, 0:w, :], mix[t.slot][:, 0:w, :], xs[t.slot][:, 0:w, :],
                                        ALU.add).then_inc(s["y_ready"], 1)

            steps = [(1, factors)] + staggered(R, [(0, 1, mixture)]) + [(1, result), (0, differences)]
            pipeline(dve, R.turns, U, steps, R.supers)

        @block.scalar
        def _(act):
            _, exponents, _ = combined(nc, None, act, b, s, k, R, U, 1, k["own2"], F)

            def scale(t, j):
                act.wait_ge(s["fac_ready"], t.n + 1)
                if j == 0:
                    wait_count(act, s["y_ready"], t.n - U + 1)
                nc.scalar.activation(mix[t.slot][:, j, :], b["agg"][t.slot][:, j, 0:F], ACT.Copy,
                                     scale=b["fac"][t.slot][:, 0, j, 0:1]).then_inc(s["scaled"], 1)

            def store(t):
                act.wait_ge(s["y_ready"], t.n + 1)
                ap, p = R.dram(out, t)
                settle(act, k["passed"]["act"])
                act.dma_start(ap, ys[t.slot][0:p, 0:R.width(t), :]).then_inc(stored[t.slot], 16)

            steps = staggered(R, [(0, 1, scale)]) + [(0, exponents), (2, store)]
            pipeline(act, R.turns, U, steps, R.supers)
            for q in range(U):
                act.wait_ge(stored[q], 16 * ((R.turns - 1 - q) // U + 1))

        @block.gpsimd
        def _(pool):
            def bias(t):
                w = R.width(t)
                pool.wait_ge(x_in[t.slot], 16 * (t.u + 1))
                nc.gpsimd.tensor_tensor(xs[t.slot][:, 0:w, :], xs[t.slot][:, 0:w, :],
                                        k["b2"][:].unsqueeze(1).to_broadcast([P, w, F]), ALU.add
                                        ).then_inc(s["biased"], 1)

            pipeline(pool, R.turns, U, [(0, bias)], R.supers)


def gnn(nc, x, src, dst, edge_weight, W1l, W1r, a1, b1, W2l, W2r, a2, b2, out):
    N, D = x.shape
    E = src.shape[0]
    H, C = a1.shape
    F1, F2 = H * C, W2l.shape[1]
    T = (E + P - 1) // P
    dram = lambda name, shape, dt=F32: nc.dram_tensor(name, shape, dt).ap()
    h0 = dram("h0", (N, D))
    x1 = dram("x1", (N + P, D))
    xl1, xr1 = dram("xl1", (N, F1)), dram("xr1", (N, F1))
    agg1, agg2 = dram("agg1", (N, F1 + 2 * H)), dram("agg2", (N, F2 + 2))
    xl2, xr2 = dram("xl2", (N, F2)), dram("xr2", (N, F2))
    with ExitStack() as ctx:
        ph = Phase(nc, ctx, "kept", last=True)
        rows = Rows(N)
        k = {"n": N, "e": E, "t": T, "rows": rows, "h1": H, "agg_m": {H: F1 + H, 1: F2 + 1},
             "ident": ph.sb("ident", [P, P]), "last_row": ph.sb("last_row", [P, P]),
             "first_row": ph.sb("first_row", [P, P]), "below": ph.sb("below", [P, P]),
             "dump_i": ph.sb("dump_i", [P, 1], I32), "dump": ph.sb("dump", [P, 1]), "eps": ph.sb("eps", [P, 1]),
             "ci": ph.sb("ci", [P, T, 3], I32), "cf": ph.sb("cf", [P, T, 3]), "li_src": ph.sb("li_src", [P, T, 2]),
             "own1": ph.sb("own1", [P, rows.tiles, H]), "own2": ph.sb("own2", [P, rows.tiles, 1]),
             "a1": ph.sb("a1", [P, F1]), "a2": ph.sb("a2", [P, F2]), "b1": ph.sb("b1", [P, F1 // P]),
             "b2": ph.sb("b2", [P, F2]), "ready": ph.sem("ready"),
             "passed": {e: ph.sem(f"passed_{e}") for e in ("sp", "act", "pool", "dve")}}
        constants(nc, k)
        with nc.Block() as block:
            @block.sync
            def _(sp):
                sp.dma_start(k["a1"][:], a1.rearrange("h c -> (h c)").partition_broadcast(P)).then_inc(k["ready"], 16)
                sp.dma_start(k["a2"][:], a2.rearrange("h c -> (h c)").partition_broadcast(P)).then_inc(k["ready"], 16)
                sp.dma_start(k["b2"][:], b2.partition_broadcast(P)).then_inc(k["ready"], 16)
                sp.dma_start(k["b1"][:], b1.rearrange("(c p) -> p c", p=P),
                             allow_slow_non_contiguous=True).then_inc(k["ready"], 16)
                sp.wait_ge(k["ready"], 64)
        edge_columns(nc, k, src, dst, edge_weight, dst[1:E])
        first_norm(nc, k, x, h0, x1, agg1, agg2)
        weighted_scatter(nc, k, h0, x1)
        node_projections(nc, k, x1, W1l, W1r, xl1, xr1)
        edge_softmax(nc, k, "ed1", xl1, xr1, agg1, k["a1"], H)
        node_hidden(nc, k, xl1, agg1, W2l, W2r, xl2, xr2)
        edge_softmax(nc, k, "ed2", xl2, xr2, agg2, k["a2"], 1)
        node_output(nc, k, xl2, agg2, x1, out)


_INS = ["x", "src", "dst", "edge_weight", "L1_gnn_W1l", "L1_gnn_W1r", "L1_gnn_a1", "L1_gnn_b1", "L1_gnn_W2l",
        "L1_gnn_W2r", "L1_gnn_a2", "L1_gnn_b2"]


def kernel(**inputs):
    import numpy as _np
    import concourse.bacc as _bacc
    from concourse import mybir as _mybir
    from concourse.bass_utils import run_bass_kernel_spmd as _run

    nc = _bacc.Bacc("TRN2", target_bir_lowering=False, num_devices=1)
    arrays, args = {}, []
    for name in _INS:
        a = _np.ascontiguousarray(inputs[name])
        arrays[f"in_{name}_dram"] = a
        args.append(nc.dram_tensor(f"in_{name}_dram", a.shape, _mybir.dt.from_np(a.dtype), kind="ExternalInput").ap())
    out = nc.dram_tensor("out_0_dram", inputs["x"].shape, _mybir.dt.float32, kind="ExternalOutput").ap()
    gnn(nc, *args, out)
    r = _run(nc, [arrays], core_ids=[0])
    return r.results[0]["out_0_dram"]
```

```python
from contextlib import ExitStack

import concourse.bass as bass
from concourse import mybir

ALU = mybir.AluOpType
ACT = mybir.ActivationFunctionType
F32 = mybir.dt.float32
F32R = mybir.dt.float32r
I32 = mybir.dt.int32

P = 128
BIG = 1.0e30
EPS = 1e-5
SLOPE = 0.2
LINEAR = (1 + SLOPE) / 2
SKIP = 60000


class Tile:

    def __init__(self, u, slot, unroll, static):
        self.u, self.slot, self.static = u, slot, static
        self.n = u * unroll + slot


def pipeline(eng, count, unroll, steps, rolled_to=None):
    rolled_to = count if rolled_to is None else rolled_to
    longest = max(lag for lag, _ in steps)
    start = longest + unroll
    loops = max(0, (rolled_to - start) // unroll)

    def beat(base, offset, static):
        for lag, fn in steps:
            c = offset - lag
            if static:
                n = base * unroll + c
                if 0 <= n < count:
                    fn(Tile(n // unroll, n % unroll, unroll, True))
            else:
                fn(Tile(base + c // unroll, c % unroll, unroll, False))

    for i in range(min(start, count + longest)):
        beat(0, i, True)
    if loops > 0:
        with eng.Fori(0, loops) as r:
            for k in range(unroll):
                beat(r, start + k, False)
    for i in range(start + loops * unroll, count + longest):
        beat(0, i, True)


def wait_count(eng, semaphore, value):
    if isinstance(value, int) and value <= 0:
        return
    eng.wait_ge(semaphore, value)


def settle(eng, passed):
    eng.sem_inc(passed, 1)


class Phase:

    def __init__(self, nc, ctx, name, last=False):
        self.nc, self.ctx, self.name, self.taken = nc, ctx, name, []
        if not last:
            ctx.callback(self.end)

    def end(self):
        self.nc.clear_and_free_semaphores(self.taken)
        self.nc.all_engine_barrier()

    def sb(self, name, shape, dt=F32):
        return self.ctx.enter_context(self.nc.sbuf_tensor(f"{self.name}_{name}", shape, dt))

    def ps(self, name, shape, dt=F32):
        return self.ctx.enter_context(self.nc.psum_tensor(f"{self.name}_{name}", shape, dt))

    def sem(self, name):
        self.taken.append(self.nc.alloc_semaphore(f"{self.name}_{name}"))
        return self.taken[-1]

    def sems(self, name, n):
        return [self.sem(f"{name}{k}") for k in range(n)]


J = 6


UNROLL = 3 * J


class Rows:
    def __init__(self, n):
        self.n = n
        self.supers = n // (P * J)
        self.rest = n - self.supers * P * J
        assert 0 < self.rest <= P and self.rest % 16 == 0
        self.tiles = self.supers * J + 1

    def tail(self, tile):
        return tile.static and tile.n == self.tiles - 1

    def width(self, tile):
        return 1 if self.tail(tile) else J

    def dram(self, table, tile, cols=None):
        d = table.shape[1] if cols is None else cols
        if self.tail(tile):
            return table[self.supers * P * J:self.n, 0:d].rearrange("(p j) d -> p j d", j=1), self.rest
        return table[bass.ds(Super(tile).n * (P * J), P * J), 0:d].rearrange("(p j) d -> p j d", j=J), P

    def first(self, fn):
        return lambda t: fn(t) if t.slot % J == 0 else None

    def final(self, fn):
        return lambda t: fn(t) if t.slot % J == J - 1 or self.tail(t) else None


class Super:

    def __init__(self, tile):
        self.q, self.u = tile.slot // J, tile.u
        self.n = tile.u * (UNROLL // J) + self.q
        self.start = self.n * J


def constants(nc, k):
    with ExitStack() as ctx:
        ph = Phase(nc, ctx, "consts")
        filled = ph.sem("filled")
        block = ctx.enter_context(nc.Block())

        @block.gpsimd
        def _(pool):
            nc.gpsimd.memset(k["ident"][:], 0.0).then_inc(filled, 1)
            nc.gpsimd.memset(k["row_one"][:], 0.0).then_inc(filled, 1)
            nc.gpsimd.memset(k["below"][:], 1.0).then_inc(filled, 1)
            nc.gpsimd.iota(k["dump_i"][:], [[P, 2]], base=k["n"], channel_multiplier=1).then_inc(filled, 1)
            pool.wait_ge(filled, 4)
            nc.gpsimd.affine_select(out=k["ident"][:], in_=k["ident"][:], compare_op=ALU.not_equal, fill=1.0,
                                    base=0, pattern=[[-1, P]], channel_multiplier=1).then_inc(filled, 1)
            nc.gpsimd.affine_select(out=k["row_one"][:], in_=k["row_one"][:], compare_op=ALU.not_equal, fill=1.0,
                                    base=-1, pattern=[[0, P]], channel_multiplier=1).then_inc(filled, 1)
            nc.gpsimd.affine_select(out=k["below"][:], in_=k["below"][:], compare_op=ALU.is_gt, fill=0.0,
                                    base=0, pattern=[[-1, P]], channel_multiplier=1).then_inc(filled, 1)
            nc.gpsimd.tensor_copy(k["dump"][:], k["dump_i"][:]).then_inc(filled, 1)
            nc.gpsimd.memset(k["eps"][:], EPS).then_inc(filled, 1)
            pool.wait_ge(filled, 9)


Q = P - 1


def edge_columns(nc, k, src, dst, weight, next_dst):
    E, N, T = k["e"], k["n"], k["t"]
    full = E // Q
    rest = E - full * Q
    chunks = [(c * P, min(P, T - c * P)) for c in range((T + P - 1) // P)]
    with ExitStack() as ctx:
        ph = Phase(nc, ctx, "cols")
        NC = len(chunks)
        raw_src = [ph.sb(f"raw_src{c}", [P, P], I32) for c in range(NC)]
        raw_dst = [ph.sb(f"raw_dst{c}", [P, P], I32) for c in range(NC)]
        raw_nxt = [ph.sb(f"raw_nxt{c}", [P, P], I32) for c in range(NC)]
        wt = [ph.sb(f"wt{c}", [P, P]) for c in range(NC)]
        names = ["src", "dst", "out_dst", "gather_dst", "last", "weight"]
        val = {n: [ph.sb(f"v_{n}{c}", [P, P]) if n != "weight" else wt[c] for c in range(NC)] for n in names}
        nxt = [ph.sb(f"nxt{c}", [P, P]) for c in range(NC)]
        tp = [ph.ps(f"tp{b}", [P, P]) for b in range(2)]
        padded, loaded, order = ph.sem("padded"), ph.sem("loaded"), ph.sem("order")
        values_ready, turned, copied = ph.sem("values_ready"), ph.sem("turned"), ph.sem("copied")
        loads = []
        for c, (t0, rows) in enumerate(chunks):
            f = min(rows, full - t0)
            lists = ((raw_src, src, rest), (raw_dst, dst, rest), (wt, weight, rest), (raw_nxt, next_dst, rest - 1))
            for buf, a, _ in lists:
                loads.append((buf[c][0:f, 1:P], a[t0 * Q:(t0 + f) * Q].rearrange("(t p) -> t p", p=Q)))
            if f < rows and rest:
                for buf, a, n in lists:
                    loads.append((buf[c][f:f + 1, 1:1 + n], a[full * Q:full * Q + n].rearrange("(t p) -> t p", t=1)))
            first = 1 if c == 0 else 0
            a0 = (t0 + first) * Q - 1
            loads.append((raw_dst[c][first:rows, 0:1],
                          dst[a0:a0 + (rows - first - 1) * Q + 1:Q].rearrange("(t o) -> t o", o=1)))
        block = ctx.enter_context(nc.Block())

        @block.gpsimd
        def _(pool):
            for c in range(NC):
                nc.gpsimd.memset(raw_src[c][:], 0).then_inc(padded, 1)
                nc.gpsimd.memset(raw_dst[c][:], N).then_inc(padded, 1)
                nc.gpsimd.memset(raw_nxt[c][:], N + 1).then_inc(padded, 1)
                nc.gpsimd.memset(wt[c][:], 0.0).then_inc(padded, 1)
            pool.wait_ge(padded, 4 * NC)
            nc.gpsimd.memset(raw_dst[0][0:1, 0:1], -5).then_inc(padded, 1)

        @block.sync
        def _(sp):
            sp.wait_ge(padded, 4 * NC + 1)
            for to, frm in loads:
                sp.dma_start(to, frm, allow_slow_non_contiguous=True).then_inc(loaded, 16)

        @block.vector
        def _(dve):
            dve.wait_ge(padded, 4 * NC + 1)
            dve.wait_ge(loaded, 16 * len(loads))
            n = 0
            for c in range(NC):
                nc.vector.tensor_copy(val["src"][c][:], raw_src[c][:]).then_inc(order, 1)
                nc.vector.tensor_copy(val["dst"][c][:], raw_dst[c][:]).then_inc(order, 1)
                nc.vector.tensor_copy(val["out_dst"][c][:], raw_dst[c][:]).then_inc(order, 1)
                nc.vector.tensor_copy(nxt[c][:], raw_nxt[c][:]).then_inc(order, 1)
                n += 4
            dve.wait_ge(order, n)
            for c in range(NC):
                d = val["dst"][c]
                nc.vector.tensor_scalar(val["gather_dst"][c][:], d[:], float(N - 1), 0.0, ALU.min,
                                        ALU.max).then_inc(order, 1)
                nc.vector.tensor_copy(val["out_dst"][c][:, 0:1], d[:, P - 1:P]).then_inc(order, 1)
                nc.vector.tensor_tensor(nxt[c][:], d[:], nxt[c][:], ALU.not_equal).then_inc(order, 1)
                n += 3
            dve.wait_ge(order, n)
            for c in range(NC):
                nc.vector.scalar_tensor_tensor(out=val["last"][c][:], in0=val["dst"][c][:], scalar=float(-SKIP),
                                               in1=nxt[c][:], op0=ALU.add, op1=ALU.mult).then_inc(order, 1)
                n += 1
            dve.wait_ge(order, n)
            for c in range(NC):
                nc.vector.tensor_scalar(val["last"][c][:], val["last"][c][:], float(SKIP), None,
                                        ALU.add).then_inc(order, 1)
                n += 1
            dve.wait_ge(order, n)
            for c in range(NC):
                ins = nc.vector.memset(val["last"][c][:, 0:1], float(SKIP))
            ins.then_inc(values_ready, 1)
            at = 0
            for c, (t0, rows) in enumerate(chunks):
                for name in names:
                    dve.wait_ge(turned, at + 1)
                    where = {"src": [k["ci"][:, t0:t0 + rows, 0], k["li_src"][:, t0:t0 + rows, 0]],
                             "gather_dst": [k["ci"][:, t0:t0 + rows, 1]],
                             "last": [k["ci"][:, t0:t0 + rows, 2]],
                             "dst": [k["cf"][:, t0:t0 + rows, 0]],
                             "out_dst": [k["cf"][:, t0:t0 + rows, 1]],
                             "weight": [k["li_src"][:, t0:t0 + rows, 1]]}[name]
                    for w in where:
                        ins = nc.vector.tensor_copy(w, tp[at % 2][:, 0:rows])
                    ins.then_inc(copied, 1)
                    at += 1

        @block.tensor
        def _(pe):
            pe.wait_ge(values_ready, 1)
            at = 0
            for c, (t0, rows) in enumerate(chunks):
                for name in names:
                    if at >= 2:
                        pe.wait_ge(copied, at - 1)
                    nc.tensor.transpose(tp[at % 2][:, 0:rows], val[name][c][0:rows, :],
                                        k["ident"][0:rows, 0:rows]).then_inc(turned, 1)
                    at += 1


def weighted_scatter(nc, k, x, x1, agg1, agg2):
    T, U = k["t"], 8
    assert T % 2 == 0
    COPIES = x.shape[0] // 400 // 25 + 1
    D = x.shape[1]
    R = k["rows"]
    with ExitStack() as ctx:
        ph = Phase(nc, ctx, "l0")
        cols = [ph.sb(f"cols{q}", [P, 2]) for q in range(U)]
        gidx = [ph.sb(f"gidx{q}", [P, 1], I32) for q in range(U)]
        xd = [ph.sb(f"xd{q}", [P, D]) for q in range(U)]
        hd = [ph.sb(f"hd{q}", [P, D]) for q in range(2)]
        v = [ph.sb(f"v{q}", [P, D]) for q in range(U)]
        st = [ph.sb(f"st{q}", [P, 6]) for q in range(U)]
        mv = [ph.sb(f"mv{q}", [P, 2]) for q in range(U)]
        sd = [ph.sb(f"sd{q}", [P, 1]) for q in range(U)]
        rs = [ph.sb(f"rs{q}", [P, 1]) for q in range(U)]
        nm = [ph.sb(f"nm{q}", [P, 1]) for q in range(U)]
        same = [ph.sb(f"same{q}", [P, P]) for q in range(U)]
        across = [ph.sb(f"across{q}", [P, P]) for q in range(U)]
        junk = [ph.sb(f"junk{q}", [P, P]) for q in range(U)]
        junk2 = [ph.sb(f"junkb{q}", [P, P]) for q in range(U)]
        before = [ph.sb(f"before{q}", [P, 2]) for q in range(U)]
        repeat = [ph.sb(f"repeat{q}", [P, 1]) for q in range(U)]
        way = [ph.sb(f"way{q}", [P, 1]) for q in range(U)]
        sidx = [ph.sb(f"sidx{q}", [P, 1], I32) for q in range(U)]
        sums = [ph.sb(f"sums{q}", [P, D]) for q in range(U)]
        neutral = [ph.sb("neutral1", [P, agg1.shape[1]]), ph.sb("neutral2", [P, agg2.shape[1]])]
        row = [ph.ps(f"row{q}", [P, 512]) for q in range(2)]
        acc = [ph.ps(f"acc{q}", [P, 512]) for q in range(2)]
        gathered, added = ph.sems("gathered", U), ph.sem("added")
        copied, agg_cleared = ph.sem("copied"), ph.sem("agg_cleared")
        names = ("neutral_ready", "cols_ready", "gidx_ready", "row_ready", "same_ready", "before_ready", "both_ready",
                 "repeat_ready", "way_ready", "sidx_ready", "stats", "moments", "root", "inverse", "shift", "normed",
                 "v_ready", "acc_ready", "sums_ready")
        s = {n: ph.sem(n) for n in names}
        block = ctx.enter_context(nc.Block())

        @block.sync
        def _(sp):
            whole = lambda table: table[0:R.n, :].rearrange("(a b e) d -> a b (e d)", a=80, e=5)
            for i in range(0, R.n // 400, 25):
                sp.dma_start(whole(x1)[:, i:i + 25, :], whole(x)[:, i:i + 25, :]).then_inc(copied, 16)
            sp.dma_start(x1[R.n:R.n + 2 * P, :], x[0:2 * P, :]).then_inc(copied, 16)
            sp.wait_ge(s["neutral_ready"], 4)
            sp.wait_ge(copied, 16 * COPIES)

            def clear_agg(t):
                for a, table in zip(neutral, (agg1, agg2)):
                    ap, p = R.dram(table, t)
                    w = R.width(t)
                    sp.dma_start(ap, a[0:p, :].unsqueeze(1).to_broadcast([p, w, table.shape[1]])
                                 ).then_inc(agg_cleared, 16)

            pipeline(sp, R.tiles, UNROLL, [(0, R.first(clear_agg))], R.tiles - 1)
            sp.wait_ge(agg_cleared, 32 * (R.supers + 1))

        @block.scalar
        def _(act):
            def deviation(t):
                act.wait_ge(s["moments"], t.n + 1)
                wait_count(act, s["inverse"], t.n - U + 1)
                nc.scalar.activation(sd[t.slot][:], mv[t.slot][:, 1:2], ACT.Sqrt,
                                     bias=k["eps"][:, 0:1]).then_inc(s["root"], 1)

            def normalise(t):
                act.wait_ge(s["shift"], t.n + 1)
                wait_count(act, s["v_ready"], t.n - 1)
                nc.scalar.activation(hd[t.slot % 2][:], xd[t.slot][:], ACT.Relu, bias=nm[t.slot][:, 0:1],
                                     scale=rs[t.slot][:, 0:1]).then_inc(s["normed"], 1)

            def drain(t):
                act.wait_ge(s["acc_ready"], t.n + 1)
                wait_count(act, added, 16 * (t.n - U + 2 - t.slot % 2))
                nc.scalar.copy(sums[t.slot][:], acc[t.slot % 2][:, 0:D]).then_inc(s["sums_ready"], 1)

            pipeline(act, T, U, [(3, deviation), (4, normalise), (7, drain)])

        @block.tensor
        def _(pe):
            def row_of(t):
                pe.wait_ge(s["cols_ready"], t.n + 1)
                wait_count(pe, s["same_ready"], t.n - t.slot % 2)
                nc.tensor.transpose(row[t.slot % 2][:, 0:P], cols[t.slot][:, 0:1].to_broadcast([P, P]),
                                    k["ident"][:]).then_inc(s["row_ready"], 1)

            def total(t):
                if t.slot % 2 == 0:
                    return
                a, b = t.slot - 1, t.slot
                pe.wait_ge(s["v_ready"], t.n + 1)
                pe.wait_ge(s["same_ready"], t.n + 1)
                wait_count(pe, s["sums_ready"], t.n - 1)
                nc.tensor.matmul(acc[0][:, 0:D], same[a][:], v[a][:], start=True, stop=False)
                nc.tensor.matmul(acc[0][:, 0:D], across[b][:], v[b][:], start=False,
                                 stop=True).then_inc(s["acc_ready"], 1)
                nc.tensor.matmul(acc[1][:, 0:D], same[b][:], v[b][:], start=True,
                                 stop=True).then_inc(s["acc_ready"], 1)

            pipeline(pe, T, U, [(1, row_of), (6, total)])

        @block.vector
        def _(dve):
            for a, w, f in ((neutral[0], agg1.shape[1], k["agg_m"][k["h1"]]), (neutral[1], agg2.shape[1], k["agg_m"][1])):
                nc.vector.memset(a[:, 0:f], 0.0).then_inc(s["neutral_ready"], 1)
                nc.vector.memset(a[:, f:w], -BIG).then_inc(s["neutral_ready"], 1)

            def stage(t):
                wait_count(dve, gathered[t.slot], 16 * t.u)
                nc.vector.tensor_copy(gidx[t.slot][:], k["ci"][:, bass.ds(t.n, 1), 1]).then_inc(s["gidx_ready"], 1)
                wait_count(dve, s["sidx_ready"], t.n - U + 1)
                wait_count(dve, s["row_ready"], t.n - U + 1)
                nc.vector.tensor_copy(cols[t.slot][:], k["li_src"][:, bass.ds(t.n, 1), :].rearrange("p a b -> p (a b)")
                                      ).then_inc(s["cols_ready"], 1)

            def match(t):
                c = t.slot
                dve.wait_ge(s["row_ready"], t.n + 1)
                wait_count(dve, s["acc_ready"], t.n - U + 1)
                if c % 2 == 1:
                    nc.vector.tensor_scalar(across[c][:], row[0][:, 0:P], cols[c][:, 0:1], None, ALU.is_equal)
                nc.vector.tensor_scalar(same[c][:], row[c % 2][:, 0:P], cols[c][:, 0:1], None,
                                        ALU.is_equal).then_inc(s["same_ready"], 1)

            def index(t):
                c = t.slot
                dve.wait_ge(s["same_ready"], t.n + 1)
                wait_count(dve, s["sidx_ready"], t.n - U + 1)
                nc.vector.tensor_tensor_reduce(junk[c][:], same[c][:], k["below"][:], 1.0, 0.0, ALU.mult, ALU.add,
                                               before[c][:, 0:1]).then_inc(s["before_ready"], 1)
                nc.vector.tensor_tensor(way[c][:], k["dump"][:, c % 2:c % 2 + 1], cols[c][:, 0:1],
                                        ALU.subtract).then_inc(s["way_ready"], 1)
                dve.wait_ge(s["before_ready"], t.n + 1)
                if c % 2 == 1:
                    nc.vector.tensor_tensor_reduce(junk2[c][:], across[c][:], across[c][:], 1.0,
                                                   before[c][:, 0:1], ALU.mult, ALU.add,
                                                   before[c][:, 1:2]).then_inc(s["both_ready"], 1)
                    dve.wait_ge(s["both_ready"], t.u * (U // 2) + c // 2 + 1)
                nc.vector.tensor_scalar(repeat[c][:], before[c][:, c % 2:c % 2 + 1], 1.0, None,
                                        ALU.min).then_inc(s["repeat_ready"], 1)
                wait_count(dve, added, 16 * (t.n - U + 2 - t.slot % 2))
                dve.wait_ge(s["way_ready"], t.n + 1)
                dve.wait_ge(s["repeat_ready"], t.n + 1)
                nc.vector.scalar_tensor_tensor(out=sidx[c][:], in0=way[c][:], scalar=repeat[c][:, 0:1],
                                               in1=cols[c][:, 0:1], op0=ALU.mult, op1=ALU.add
                                               ).then_inc(s["sidx_ready"], 1)

            def statistics(t):
                dve.wait_ge(gathered[t.slot], 16 * (t.u + 1))
                wait_count(dve, s["moments"], t.n - U + 1)
                nc.vector.bn_stats(st[t.slot][:], xd[t.slot][:]).then_inc(s["stats"], 1)
                wait_count(dve, s["root"], t.n - U + 1)
                wait_count(dve, s["shift"], t.n - U + 1)
                dve.wait_ge(s["stats"], t.n + 1)
                settle(dve, k["passed"]["dve"])
                nc.vector.bn_aggr(mv[t.slot][:], st[t.slot][:]).then_inc(s["moments"], 1)

            def scales(t):
                c = t.slot
                dve.wait_ge(s["root"], t.n + 1)
                wait_count(dve, s["normed"], t.n - U + 1)
                nc.vector.reciprocal(rs[c][:], sd[c][:]).then_inc(s["inverse"], 1)
                dve.wait_ge(s["inverse"], t.n + 1)
                nc.vector.tensor_scalar(nm[c][:], mv[c][:, 0:1], rs[c][:, 0:1], -1.0, ALU.mult,
                                        ALU.mult).then_inc(s["shift"], 1)

            def weigh(t):
                dve.wait_ge(s["normed"], t.n + 1)
                wait_count(dve, s["acc_ready"], t.n - U + 1)
                nc.vector.tensor_scalar(v[t.slot][:], hd[t.slot % 2][:], cols[t.slot][:, 1:2], None,
                                        ALU.mult).then_inc(s["v_ready"], 1)

            pipeline(dve, T, U, [(4, scales), (0, stage), (2, match), (5, weigh), (5, index), (3, statistics)])

        @block.gpsimd
        def _(pool):
            def gather(t):
                pool.wait_ge(s["gidx_ready"], t.n + 1)
                wait_count(pool, s["normed"], t.n - U + 1)
                settle(pool, k["passed"]["pool"])
                pool.indirect_dma_start(xd[t.slot][:], None, x, bass.IndirectOffsetOnAxis(gidx[t.slot][:], 0),
                                        bounds_check=k["n"] - 1).then_inc(gathered[t.slot], 16)

            def scatter(t):
                if t.slot % 2 == 0:
                    return
                pool.wait_ge(s["sidx_ready"], t.n + 1)
                pool.wait_ge(s["sums_ready"], t.n + 1)
                wait_count(pool, added, 16 * (t.n - 1))
                settle(pool, k["passed"]["pool"])
                for q in (t.slot - 1, t.slot):
                    pool.indirect_dma_start(x1, bass.IndirectOffsetOnAxis(sidx[q][:], 0), sums[q][:], None,
                                            bounds_check=k["n"] + 2 * P - 1, compute_op=ALU.add).then_inc(added, 16)

            def begin(t):
                if t.static and t.n == 1:
                    pool.wait_ge(copied, 16 * COPIES)

            pipeline(pool, T, U, [(1, gather), (8, begin), (8, scatter)])
            pool.wait_ge(added, 16 * T)


def split_weights(nc, dve, w, parts, folded, att, H, junk, order, n=0):
    KC, F2 = w.shape[1], w.shape[2]
    F = F2 // 2
    C = F // H
    hi, lo = parts
    fold, fhi, flo = folded
    for c in range(KC):
        for i in range(2):
            for h in range(H):
                a = i * F + h * C
                ins = nc.vector.tensor_tensor_reduce(junk[:, a:a + C], w[:, c, a:a + C], att[:, h * C:(h + 1) * C],
                                                     LINEAR, 0.0, ALU.mult, ALU.add,
                                                     fold[:, c, i * H + h:i * H + h + 1])
        ins.then_inc(order, 1)
        n += 1
        dve.wait_ge(order, n)
    nc.vector.tensor_copy(hi[:], w[:]).then_inc(order, 1)
    nc.vector.tensor_copy(fhi[:], fold[:]).then_inc(order, 1)
    n += 2
    dve.wait_ge(order, n)
    nc.vector.tensor_tensor(lo[:], w[:], hi[:].bitcast(F32), ALU.subtract).then_inc(order, 1)
    nc.vector.tensor_tensor(flo[:], fold[:], fhi[:].bitcast(F32), ALU.subtract).then_inc(order, 1)
    return n + 2


def node_projections(nc, k, x1, wl, wr, xl, xr):
    R = k["rows"]
    U = 3
    D, F, H = x1.shape[1], wl.shape[1], k["h1"]
    C = F // H
    KC = D // P
    with ExitStack() as ctx:
        ph = Phase(nc, ctx, "np1")
        w_sb = ph.sb("w", [P, KC, 2 * F])
        w_parts = [ph.sb(f"w_part{i}", [P, KC, 2 * F], F32R) for i in range(2)]
        fold = [ph.sb("fold", [P, KC, 2 * H])] + [ph.sb(f"fold{i}", [P, KC, 2 * H], F32R) for i in range(2)]
        xs = [ph.sb(f"x{q}", [P, J, D]) for q in range(U)]
        hs = [ph.sb(f"h{q}", [P, D]) for q in range(3)]
        st = [ph.sb(f"st{q}", [P, J, 6]) for q in range(U)]
        mv = [ph.sb(f"mv{q}", [P, J, 2]) for q in range(U)]
        sd = [ph.sb(f"sd{q}", [P, J]) for q in range(U)]
        rs = [ph.sb(f"rs{q}", [P, J]) for q in range(U)]
        nm = [ph.sb(f"nm{q}", [P, J]) for q in range(U)]
        hT1 = [ph.sb(f"hTa{q}", [P, D], F32R) for q in range(3)]
        hT2 = [ph.sb(f"hTb{q}", [P, D], F32R) for q in range(3)]
        ls = [ph.sb(f"l{q}", [P, J, F + H]) for q in range(U)]
        rr = [ph.sb(f"r{q}", [P, J, F + H]) for q in range(U)]
        g = [ph.sb(f"g{q}", [P, F + H]) for q in range(3)]
        ab = [ph.sb(f"ab{q}", [P, F]) for q in range(2)]
        junk = ph.sb("junk", [P, 2 * F])
        own = [ph.sb(f"own{q}", [P, J, H]) for q in range(U)]
        hp = [ph.ps(f"hp{q}", [P, 512]) for q in range(2)]
        lp = [ph.ps(f"lp{q}", [P, F]) for q in range(2)]
        rp = [ph.ps(f"rp{q}", [P, F]) for q in range(2)]
        fp = [ph.ps(f"fp{q}", [P, 512]) for q in range(2)]
        loaded, stored = ph.sems("loaded", U), ph.sems("stored", U)
        names = ("weights", "order", "split", "stats", "moments", "root", "inverse", "shift", "normed", "turned",
                 "hT1_ready", "hT2_ready", "lp_ready", "rp_ready", "l_ready", "r_ready", "g_ready", "ab_ready",
                 "own_ready", "own_kept")
        s = {n: ph.sem(n) for n in names}
        block = ctx.enter_context(nc.Block())

        @block.sync
        def _(sp):
            for i, w in enumerate((wl, wr)):
                for c in range(KC):
                    sp.dma_start(w_sb[:, c, i * F:(i + 1) * F], w[c * P:(c + 1) * P, :]).then_inc(s["weights"], 16)

            def load(t):
                S = Super(t)
                wait_count(sp, s["normed"], S.start - (U - 1) * J)
                ap, p = R.dram(x1, t)
                settle(sp, k["passed"]["sp"])
                sp.dma_start(xs[S.q][0:p, 0:R.width(t), :], ap).then_inc(loaded[S.q], 16)

            def store(t):
                S = Super(t)
                w = R.width(t)
                sp.wait_ge(s["l_ready"], S.start + w)
                settle(sp, k["passed"]["sp"])
                sp.wait_ge(s["r_ready"], S.start + w)
                for table, buf in ((xl, ls), (xr, rr)):
                    ap, p = R.dram(table, t)
                    settle(sp, k["passed"]["sp"])
                    sp.dma_start(ap, buf[S.q][0:p, 0:w, :]).then_inc(stored[S.q], 16)

            pipeline(sp, R.tiles, UNROLL, [(0, R.first(load)), (19, R.final(store))], R.tiles - 1)
            for q in range(U):
                sp.wait_ge(stored[q], 32 * ((R.supers - q) // U + 1))

        @block.vector
        def _(dve):
            dve.wait_ge(s["weights"], 16 * 2 * KC)
            n = split_weights(nc, dve, w_sb, w_parts, fold, k["a1"], H, junk, s["order"])
            dve.wait_ge(s["order"], n)
            nc.vector.memset(junk[:, 0:1], 0.0).then_inc(s["split"], 1)

            def statistics(t):
                S, j = Super(t), t.slot % J
                if j == 0:
                    dve.wait_ge(loaded[S.q], 16 * (S.u + 1))
                    wait_count(dve, s["moments"], S.n - U + 1)
                nc.vector.bn_stats(st[S.q][:, j, :], xs[S.q][:, j, :]).then_inc(s["stats"], 1)

            def moments(t):
                S = Super(t)
                wait_count(dve, s["root"], S.n - U + 1)
                wait_count(dve, s["shift"], S.n - U + 1)
                dve.wait_ge(s["stats"], S.start + R.width(t))
                settle(dve, k["passed"]["dve"])
                for j in range(R.width(t)):
                    ins = nc.vector.bn_aggr(mv[S.q][:, j, :], st[S.q][:, j, :])
                ins.then_inc(s["moments"], 1)

            def scales(t):
                S = Super(t)
                dve.wait_ge(s["root"], S.n + 1)
                wait_count(dve, s["normed"], S.start - (U - 1) * J)
                nc.vector.reciprocal(rs[S.q][:], sd[S.q][:]).then_inc(s["inverse"], 1)
                dve.wait_ge(s["inverse"], S.n + 1)
                nc.vector.scalar_tensor_tensor(out=nm[S.q][:], in0=mv[S.q][:, :, 0], scalar=-1.0,
                                               in1=rs[S.q][:], op0=ALU.mult, op1=ALU.mult).then_inc(s["shift"], 1)

            def rest(t):
                dve.wait_ge(s["hT1_ready"], t.n + 1)
                wait_count(dve, s["rp_ready"], t.n - 2)
                nc.vector.tensor_tensor(hT2[t.slot % 3][:], hp[t.slot % 2][:, 0:D], hT1[t.slot % 3][:].bitcast(F32),
                                        ALU.subtract).then_inc(s["hT2_ready"], 1)

            def right(t):
                S, j, b = Super(t), t.slot % J, t.slot % 2
                dve.wait_ge(s["rp_ready"], t.n + 1)
                if j == 0:
                    wait_count(dve, stored[S.q], 32 * S.u)
                    wait_count(dve, s["g_ready"], S.start - (U - 1) * J)
                nc.vector.tensor_copy(ls[S.q][:, j, F:F + H], fp[b][:, 0:H])
                nc.vector.tensor_copy(rr[S.q][:, j, F:F + H], fp[b][:, H:2 * H])
                nc.vector.tensor_copy(rr[S.q][:, j, 0:F], rp[b][:]).then_inc(s["r_ready"], 1)

            def own_score(t):
                S, j, b = Super(t), t.slot % J, t.slot % 2
                dve.wait_ge(s["ab_ready"], t.n + 1)
                if j == 0:
                    wait_count(dve, s["own_kept"], S.n - U + 1)
                for h in range(H):
                    ins = nc.vector.tensor_tensor_reduce(ab[b][:, h * C:(h + 1) * C], ab[b][:, h * C:(h + 1) * C],
                                                         k["a1"][:, h * C:(h + 1) * C], 1.0,
                                                         g[t.slot % 3][:, F + h:F + h + 1], ALU.mult, ALU.add,
                                                         own[S.q][:, j, h:h + 1])
                ins.then_inc(s["own_ready"], 1)

            def keep(t):
                S, w = Super(t), R.width(t)
                dve.wait_ge(s["own_ready"], S.start + w)
                nc.vector.tensor_copy(k["own1"][:, bass.ds(S.start, w), :],
                                      own[S.q][:, 0:w, :]).then_inc(s["own_kept"], 1)

            pipeline(dve, R.tiles, UNROLL,
                     [(16, rest), (18, right), (21, own_score), (6, statistics), (6, R.final(moments)),
                      (8, R.final(scales)), (22, R.final(keep))], R.tiles - 1)

        @block.scalar
        def _(act):
            def deviation(t):
                S = Super(t)
                act.wait_ge(s["moments"], S.n + 1)
                wait_count(act, s["inverse"], S.n - U + 1)
                nc.scalar.activation(sd[S.q][:], mv[S.q][:, :, 1], ACT.Sqrt,
                                     bias=k["eps"][:, 0:1]).then_inc(s["root"], 1)

            def normalise(t):
                S, j = Super(t), t.slot % J
                if j == 0:
                    act.wait_ge(s["shift"], S.n + 1)
                wait_count(act, s["turned"], t.n - 2)
                nc.scalar.activation(hs[t.slot % 3][:], xs[S.q][:, j, :], ACT.Relu,
                                     bias=nm[S.q][:, j:j + 1], scale=rs[S.q][:, j:j + 1]).then_inc(s["normed"], 1)

            def turn(t):
                act.wait_ge(s["turned"], t.n + 1)
                wait_count(act, s["rp_ready"], t.n - 2)
                nc.scalar.copy(hT1[t.slot % 3][:], hp[t.slot % 2][:, 0:D]).then_inc(s["hT1_ready"], 1)

            def left(t):
                S, j = Super(t), t.slot % J
                act.wait_ge(s["lp_ready"], t.n + 1)
                if j == 0:
                    wait_count(act, stored[S.q], 32 * S.u)
                    wait_count(act, s["g_ready"], S.start - (U - 1) * J)
                nc.scalar.copy(ls[S.q][:, j, 0:F], lp[t.slot % 2][:]).then_inc(s["l_ready"], 1)

            def magnitude(t):
                act.wait_ge(s["g_ready"], t.n + 1)
                wait_count(act, s["own_ready"], t.n - 1)
                nc.scalar.activation(ab[t.slot % 2][:], g[t.slot % 3][:, 0:F], ACT.Abs,
                                     scale=1.0 - LINEAR).then_inc(s["ab_ready"], 1)

            pipeline(act, R.tiles, UNROLL,
                     [(15, turn), (18, left), (20, magnitude), (13, normalise), (7, R.final(deviation))], R.tiles - 1)

        @block.gpsimd
        def _(pool):
            def add(t):
                S, j = Super(t), t.slot % J
                pool.wait_ge(s["l_ready"], t.n + 1)
                pool.wait_ge(s["r_ready"], t.n + 1)
                wait_count(pool, s["own_ready"], t.n - 2)
                nc.gpsimd.tensor_tensor(g[t.slot % 3][:], ls[S.q][:, j, :], rr[S.q][:, j, :],
                                        ALU.add).then_inc(s["g_ready"], 1)

            pipeline(pool, R.tiles, UNROLL, [(19, add)], R.tiles - 1)

        @block.tensor
        def _(pe):
            pe.wait_ge(s["split"], 1)

            def transposes(t):
                pe.wait_ge(s["normed"], t.n + 1)
                wait_count(pe, s["hT2_ready"], t.n - 1)
                for c in range(KC):
                    ins = nc.tensor.transpose(hp[t.slot % 2][:, c * P:(c + 1) * P],
                                              hs[t.slot % 3][:, c * P:(c + 1) * P], k["ident"][:])
                ins.then_inc(s["turned"], 1)

            def products(t):
                b, h1, h2 = t.slot % 2, hT1[t.slot % 3], hT2[t.slot % 3]
                passes = [(h1, 0), (h1, 1), (h2, 0)]
                pe.wait_ge(s["hT2_ready"], t.n + 1)
                wait_count(pe, s["l_ready"], t.n - 1)
                wait_count(pe, s["r_ready"], t.n - 1)
                for out, weights, lo, hi, ready in ((fp[b][:, 0:2 * H], fold[1:], 0, 2 * H, None),
                                                    (lp[b][:], w_parts, 0, F, "lp_ready"),
                                                    (rp[b][:], w_parts, F, 2 * F, "rp_ready")):
                    for n, (c, (h, part)) in enumerate([(c, q) for c in range(KC) for q in passes]):
                        ins = nc.tensor.matmul(out, h[:, c * P:(c + 1) * P], weights[part][:, c, lo:hi],
                                               start=(n == 0), stop=(n == 3 * KC - 1))
                    if ready:
                        ins.then_inc(s[ready], 1)

            pipeline(pe, R.tiles, UNROLL, [(17, products), (14, transposes)], R.tiles - 1)


def edge_softmax(nc, k, name, xl, xr, agg, att, H):
    T, U = k["t"], 8
    F = agg.shape[1] - 2 * H
    C = F // H
    W = agg.shape[1]
    with ExitStack() as ctx:
        ph = Phase(nc, ctx, name)
        cols = [ph.sb(f"cols{q}", [P, 2]) for q in range(U)]
        idx = [ph.sb(f"idx{q}", [P, 2], I32) for q in range(U)]
        last = [ph.sb(f"last{q}", [P, 1], I32) for q in range(U)]
        gl = [ph.sb(f"gl{q}", [P, F + H]) for q in range(U)]
        gr = [ph.sb(f"gr{q}", [P, F + H]) for q in range(U)]
        g = [ph.sb(f"g{q}", [P, F + H]) for q in range(2)]
        ab = [ph.sb(f"ab{q}", [P, F]) for q in range(2)]
        junk2 = ph.sb("junk2", [P, H, P])
        e = [ph.sb(f"e{q}", [P, H]) for q in range(U)]
        same = [ph.sb(f"same{q}", [P, P]) for q in range(U)]
        away = [ph.sb(f"away{q}", [P, P]) for q in range(U)]
        m = [ph.sb(f"m{q}", [P, H]) for q in range(U)]
        dif = [ph.sb(f"dif{q}", [P, H]) for q in range(U)]
        p = [ph.sb(f"p{q}", [P, H]) for q in range(U)]
        pd = [ph.sb(f"pd{q}", [P, H]) for q in range(U)]
        v = [ph.sb(f"v{q}", [P, F]) for q in range(2)]
        out = [ph.sb(f"out{q}", [P, W]) for q in range(U)]
        row = ph.ps("row", [P, 2, P])
        eb = [ph.ps(f"eb{q}", [P, H, P] if H > 1 else [P, 4, P]) for q in range(2)]
        acc = [ph.ps(f"acc{q}", [P, 512]) for q in range(2)]
        den = [ph.ps(f"den{q}", [P, 512]) for q in range(2)]
        mb = ph.ps("mb", [P, 512])
        gl_in, gr_in, written = ph.sems("gl_in", U), ph.sems("gr_in", U), ph.sems("written", U)
        names = ("cols_ready", "idx_ready", "last_ready", "g_ready", "ab_ready", "e_ready", "row_ready",
                 "match_ready", "joined", "eb_ready", "m_ready", "mb_ready", "dif0_ready", "dif_ready", "clamped",
                 "p_ready", "v_ready", "pd_ready", "taken_over", "acc_ready", "out_ready", "outm_ready")
        s = {n: ph.sem(n) for n in names}
        block = ctx.enter_context(nc.Block())

        @block.gpsimd
        def _(pool):
            def gather(t):
                pool.wait_ge(s["idx_ready"], t.n + 1)
                wait_count(pool, s["v_ready"], t.n - U + 1)
                settle(pool, k["passed"]["pool"])
                pool.indirect_dma_start(gl[t.slot][:], None, xl, bass.IndirectOffsetOnAxis(idx[t.slot][:, 0:1], 0),
                                        bounds_check=k["n"] - 1).then_inc(gl_in[t.slot], 16)
                pool.indirect_dma_start(gr[t.slot][:], None, xr, bass.IndirectOffsetOnAxis(idx[t.slot][:, 1:2], 0),
                                        bounds_check=k["n"] - 1).then_inc(gr_in[t.slot], 16)

            def write(t):
                pool.wait_ge(s["out_ready"], t.n + 1)
                pool.wait_ge(s["outm_ready"], t.n + 1)
                pool.wait_ge(s["last_ready"], t.n + 1)
                settle(pool, k["passed"]["pool"])
                pool.indirect_dma_start(agg, bass.IndirectOffsetOnAxis(last[t.slot][:], 0), out[t.slot][:], None,
                                        bounds_check=k["n"] - 1, oob_is_err=False).then_inc(written[t.slot], 16)

            pipeline(pool, T, U, [(1, gather), (10, write)])
            for q in range(U):
                pool.wait_ge(written[q], 16 * ((T - 1 - q) // U + 1))

        @block.scalar
        def _(act):
            def weigh(t):
                act.wait_ge(s["p_ready"], t.n + 1)
                act.wait_ge(gl_in[t.slot], 16 * (t.u + 1))
                wait_count(act, s["acc_ready"], t.n - 1)
                for h in range(H):
                    ins = nc.scalar.activation(v[t.slot % 2][:, h * C:(h + 1) * C], gl[t.slot][:, h * C:(h + 1) * C],
                                               ACT.Copy, scale=p[t.slot][:, h:h + 1])
                ins.then_inc(s["v_ready"], 1)

            def magnitude(t):
                act.wait_ge(s["g_ready"], t.n + 1)
                wait_count(act, s["e_ready"], t.n - 1)
                nc.scalar.activation(ab[t.slot % 2][:], g[t.slot % 2][:, 0:F], ACT.Abs,
                                     scale=1.0 - LINEAR).then_inc(s["ab_ready"], 1)

            def exponent(t):
                act.wait_ge(s["clamped"], t.n + 1)
                wait_count(act, s["taken_over"], t.n - U + 1)
                nc.scalar.activation(p[t.slot][:], dif[t.slot][:], ACT.Exp).then_inc(s["p_ready"], 1)

            def drain(t):
                if not (t.static and t.n == T - 1):
                    act.wait_ge(s["taken_over"], t.n + 2)
                act.wait_ge(s["acc_ready"], t.n + 1)
                wait_count(act, written[t.slot], 16 * t.u)
                nc.scalar.copy(out[t.slot][:, 0:F], acc[t.slot % 2][:, 0:F])
                nc.scalar.copy(out[t.slot][:, F:F + H], den[t.slot % 2][:, 0:H]).then_inc(s["out_ready"], 1)

            pipeline(act, T, U, [(6, exponent), (7, weigh), (4, magnitude), (9, drain)])

        @block.vector
        def _(dve):
            def stage(t):
                wait_count(dve, gl_in[t.slot], 16 * t.u)
                wait_count(dve, gr_in[t.slot], 16 * t.u)
                nc.vector.tensor_copy(idx[t.slot][:], k["ci"][:, bass.ds(t.n, 1), 0:2].rearrange("p a b -> p (a b)")
                                      ).then_inc(s["idx_ready"], 1)
                wait_count(dve, s["row_ready"], t.n - U + 1)
                nc.vector.tensor_copy(cols[t.slot][:], k["cf"][:, bass.ds(t.n, 1), :].rearrange("p a b -> p (a b)")
                                      ).then_inc(s["cols_ready"], 1)

            def join(t):
                dve.wait_ge(s["e_ready"], t.n + 1)
                if t.static and t.n == 0:
                    nc.vector.memset(e[0][0:1, :], 0.0).then_inc(s["joined"], 1)
                    return
                dve.wait_ge(s["m_ready"], t.n)
                nc.vector.tensor_copy(e[t.slot][0:1, :], m[(t.slot - 1) % U][0:1, :]).then_inc(s["joined"], 1)

            def take_over(t):
                q, before = t.slot % 2, (t.slot + 1) % 2
                dve.wait_ge(s["p_ready"], t.n + 1)
                wait_count(dve, s["acc_ready"], t.n - U + 1)
                nc.vector.tensor_copy(pd[t.slot][:], p[t.slot][:]).then_inc(s["pd_ready"], 1)
                dve.wait_ge(s["pd_ready"], t.n + 1)
                if t.static and t.n == 0:
                    nc.vector.memset(pd[0][0:1, :], 0.0)
                    dve.wait_ge(s["v_ready"], 1)
                    nc.vector.memset(v[0][0:1, :], 0.0).then_inc(s["taken_over"], 1)
                    return
                dve.wait_ge(s["acc_ready"], t.n)
                nc.vector.tensor_tensor(pd[t.slot][0:1, :], den[before][0:1, 0:H], p[t.slot][0:1, :], ALU.mult)
                dve.wait_ge(s["v_ready"], t.n + 1)
                nc.vector.tensor_tensor(v[q][0:1, :].rearrange("p (h c) -> p h c", h=H),
                                        acc[before][0:1, 0:F].rearrange("p (h c) -> p h c", h=H),
                                        p[t.slot][0:1, :].unsqueeze(2).to_broadcast([1, H, C]),
                                        ALU.mult).then_inc(s["taken_over"], 1)

            def add(t):
                q = t.slot % 2
                dve.wait_ge(gl_in[t.slot], 16 * (t.u + 1))
                dve.wait_ge(gr_in[t.slot], 16 * (t.u + 1))
                wait_count(dve, s["ab_ready"], t.n - 1)
                wait_count(dve, s["e_ready"], t.n - 1)
                nc.vector.tensor_tensor(g[q][:], gl[t.slot][:], gr[t.slot][:], ALU.add).then_inc(s["g_ready"], 1)

            def match(t):
                dve.wait_ge(s["row_ready"], t.n + 1)
                wait_count(dve, s["acc_ready"], t.n - U + 1)
                nc.vector.tensor_scalar(same[t.slot][:], row[:, 1, :], cols[t.slot][:, 0:1], None, ALU.is_equal)
                wait_count(dve, s["m_ready"], t.n - U + 1)
                nc.vector.tensor_scalar(away[t.slot][:], row[:, 0, :], cols[t.slot][:, 1:2], -BIG, ALU.not_equal,
                                        ALU.mult).then_inc(s["match_ready"], 1)

            def maximum(t):
                dve.wait_ge(s["eb_ready"], t.n + 1)
                dve.wait_ge(s["match_ready"], t.n + 1)
                wait_count(dve, s["outm_ready"], t.n - U + 1)
                settle(dve, k["passed"]["dve"])
                for h in range(H):
                    ins = nc.vector.tensor_tensor_reduce(junk2[:, h, :], eb[t.slot % 2][:, h, :], away[t.slot][:],
                                                         1.0, -3.0e38, ALU.add, ALU.max, m[t.slot][:, h:h + 1])
                ins.then_inc(s["m_ready"], 1)

            def score(t):
                q = t.slot % 2
                dve.wait_ge(s["ab_ready"], t.n + 1)
                dve.wait_ge(s["g_ready"], t.n + 1)
                wait_count(dve, s["eb_ready"], t.n - U + 1)
                for h in range(H):
                    ins = nc.vector.tensor_tensor_reduce(ab[q][:, h * C:(h + 1) * C], ab[q][:, h * C:(h + 1) * C],
                                                         att[:, h * C:(h + 1) * C], 1.0, g[q][:, F + h:F + h + 1],
                                                         ALU.mult, ALU.add, e[t.slot][:, h:h + 1])
                ins.then_inc(s["e_ready"], 1)

            def difference(t):
                dve.wait_ge(s["m_ready"], t.n + 1)
                wait_count(dve, s["p_ready"], t.n - U + 1)
                nc.vector.tensor_tensor(dif[t.slot][:], e[t.slot][:], m[t.slot][:],
                                        ALU.subtract).then_inc(s["dif_ready"], 1)

            def carried(t):
                dve.wait_ge(s["mb_ready"], t.n + 1)
                dve.wait_ge(s["dif_ready"], t.n + 1)
                nc.vector.tensor_tensor(dif[t.slot][0:1, :], e[t.slot][0:1, :], mb[0:1, 0:H],
                                        ALU.subtract).then_inc(s["dif0_ready"], 1)
                dve.wait_ge(s["dif0_ready"], t.n + 1)
                nc.vector.tensor_scalar(dif[t.slot][0:1, :], dif[t.slot][0:1, :], 0.0, None,
                                        ALU.min).then_inc(s["clamped"], 1)

            def result(t):
                wait_count(dve, written[t.slot], 16 * t.u)
                nc.vector.tensor_copy(out[t.slot][:, F + H:F + 2 * H], m[t.slot][:]).then_inc(s["outm_ready"], 1)
                nc.vector.tensor_copy(last[t.slot][:], k["ci"][:, bass.ds(t.n, 1), 2]).then_inc(s["last_ready"], 1)

            pipeline(dve, T, U, [(6, carried), (5, join), (8, take_over), (4, add), (4, match), (5, maximum), (4, score),
                                 (5, difference), (6, result), (0, stage)])

        @block.tensor
        def _(pe):
            def rows_of(t):
                pe.wait_ge(s["cols_ready"], t.n + 1)
                wait_count(pe, s["match_ready"], t.n)
                for c in range(2):
                    ins = nc.tensor.transpose(row[:, c, :], cols[t.slot][:, c:c + 1].to_broadcast([P, P]),
                                              k["ident"][:])
                ins.then_inc(s["row_ready"], 1)

            def scores(t):
                pe.wait_ge(s["joined"], t.n + 1)
                wait_count(pe, s["m_ready"], t.n - 1)
                for h in range(H):
                    ins = nc.tensor.transpose(eb[t.slot % 2][:, h, :], e[t.slot][:, h:h + 1].to_broadcast([P, P]),
                                              k["ident"][:])
                ins.then_inc(s["eb_ready"], 1)

            def next_maximum(t):
                pe.wait_ge(s["m_ready"], t.n + 1)
                wait_count(pe, s["dif0_ready"], t.n)
                nc.tensor.matmul(mb[:, 0:H], k["row_one"][:], m[t.slot][:], start=True, stop=True
                                 ).then_inc(s["mb_ready"], 1)

            def total(t):
                q = t.slot % 2
                pe.wait_ge(s["taken_over"], t.n + 1)
                pe.wait_ge(s["match_ready"], t.n + 1)
                wait_count(pe, s["out_ready"], t.n - 1)
                nc.tensor.matmul(den[q][:, 0:H], same[t.slot][:], pd[t.slot][:], start=True, stop=True)
                nc.tensor.matmul(acc[q][:, 0:F], same[t.slot][:], v[q][:], start=True,
                                 stop=True).then_inc(s["acc_ready"], 1)

            pipeline(pe, T, U, [(5, scores), (8, total), (3, rows_of), (5, next_maximum)])


def combined(nc, dve, act, b, s, k, R, U, H, own_all, F):
    def differences(t):
        S, w = Super(t), R.width(t)
        ag, top, dif = (b[n][S.q] for n in ("agg", "top", "dif"))
        dve.wait_ge(b["agg_in"][S.q], 16 * (S.u + 1))
        wait_count(dve, s["dif_ready"], S.n - U + 1)
        nc.vector.tensor_tensor(top[:, 0:w, :], ag[:, 0:w, F + H:F + 2 * H], own_all[:, bass.ds(S.start, w), :],
                                ALU.max).then_inc(s["top_ready"], 1)
        dve.wait_ge(s["top_ready"], S.n + 1)
        wait_count(dve, s["exp_ready"], S.n - U + 1)
        nc.vector.tensor_tensor(dif[:, 0, 0:w, :], ag[:, 0:w, F + H:F + 2 * H], top[:, 0:w, :], ALU.subtract)
        nc.vector.tensor_tensor(dif[:, 1, 0:w, :], own_all[:, bass.ds(S.start, w), :], top[:, 0:w, :],
                                ALU.subtract).then_inc(s["dif_ready"], 1)

    def exponents(t):
        S, w = Super(t), R.width(t)
        act.wait_ge(s["dif_ready"], S.n + 1)
        wait_count(act, s["fac_ready"], S.n - U + 1)
        nc.scalar.activation(b["ex"][S.q][:, :, 0:w, :], b["dif"][S.q][:, :, 0:w, :], ACT.Exp
                             ).then_inc(s["exp_ready"], 1)

    def factors(t):
        S, w = Super(t), R.width(t)
        ag, wh, ex, fac = (b[n][S.q] for n in ("agg", "whole", "ex", "fac"))
        dve.wait_ge(s["exp_ready"], S.n + 1)
        nc.vector.tensor_tensor(wh[:, 0:w, :], ag[:, 0:w, F:F + H], ex[:, 0, 0:w, :],
                                ALU.mult).then_inc(s["whole_ready"], 1)
        dve.wait_ge(s["whole_ready"], 3 * S.n + 1)
        nc.vector.tensor_tensor(wh[:, 0:w, :], wh[:, 0:w, :], ex[:, 1, 0:w, :], ALU.add).then_inc(s["whole_ready"], 1)
        dve.wait_ge(s["whole_ready"], 3 * S.n + 2)
        nc.vector.reciprocal(wh[:, 0:w, :], wh[:, 0:w, :]).then_inc(s["whole_ready"], 1)
        wait_count(dve, s["mixed"], S.start - (U - 1) * J)
        dve.wait_ge(s["whole_ready"], 3 * S.n + 3)
        nc.vector.tensor_tensor(fac[:, 0, 0:w, :], wh[:, 0:w, :], ex[:, 0, 0:w, :], ALU.mult)
        nc.vector.tensor_tensor(fac[:, 1, 0:w, :], wh[:, 0:w, :], ex[:, 1, 0:w, :], ALU.mult
                                ).then_inc(s["fac_ready"], 1)

    return differences, exponents, factors


COMBINED = ("top_ready", "dif_ready", "exp_ready", "whole_ready", "fac_ready", "scaled", "mixed")


def combined_buffers(ph, U, H, W):
    b = {"agg": [ph.sb(f"agg{q}", [P, J, W]) for q in range(U)],
         "top": [ph.sb(f"top{q}", [P, J, H]) for q in range(U)],
         "dif": [ph.sb(f"dif{q}", [P, 2, J, H]) for q in range(U)],
         "ex": [ph.sb(f"ex{q}", [P, 2, J, H]) for q in range(U)],
         "whole": [ph.sb(f"whole{q}", [P, J, H]) for q in range(U)],
         "fac": [ph.sb(f"fac{q}", [P, 2, J, H]) for q in range(U)],
         "agg_in": ph.sems("agg_in", U)}
    return b


def node_hidden(nc, k, xl, agg, w2l, w2r, xl2, xr2):
    R = k["rows"]
    U = 3
    H, G = k["h1"], w2l.shape[1]
    F = w2l.shape[0]
    C = F // H
    KC = F // P
    with ExitStack() as ctx:
        ph = Phase(nc, ctx, "np2")
        w_sb = ph.sb("w", [P, KC, 2 * G])
        w_parts = [ph.sb(f"w_part{i}", [P, KC, 2 * G], F32R) for i in range(2)]
        fold = [ph.sb("fold", [P, KC, 2])] + [ph.sb(f"fold{i}", [P, KC, 2], F32R) for i in range(2)]
        b = combined_buffers(ph, U, H, agg.shape[1])
        ls = [ph.sb(f"l{q}", [P, J, F]) for q in range(U)]
        mix = [ph.sb(f"mix{q}", [P, F]) for q in range(3)]
        hT = [ph.sb(f"hT{q}", [P, F]) for q in range(2)]
        hT1 = [ph.sb(f"hTa{q}", [P, F], F32R) for q in range(3)]
        hT2 = [ph.sb(f"hTb{q}", [P, F], F32R) for q in range(3)]
        lr = [ph.sb(f"lr{q}", [P, 2, J, G + 1]) for q in range(U)]
        g = [ph.sb(f"g{q}", [P, G + 1]) for q in range(3)]
        ab = [ph.sb(f"ab{q}", [P, G]) for q in range(2)]
        junk = ph.sb("junk", [P, 2 * G])
        own = [ph.sb(f"own{q}", [P, J, 1]) for q in range(U)]
        hp = [ph.ps(f"hp{q}", [P, F]) for q in range(2)]
        op = [ph.ps(f"op{q}", [P, 2 * G]) for q in range(2)]
        fp = [ph.ps(f"fp{q}", [P, 512]) for q in range(2)]
        l_in, stored = ph.sems("l_in", U), ph.sems("stored", U)
        names = COMBINED + ("weights", "order", "split", "turned", "hT_ready", "hT1_ready", "hT2_ready", "op_ready",
                            "lr_ready", "g_ready", "ab_ready", "own_ready", "own_kept")
        s = {n: ph.sem(n) for n in names}
        block = ctx.enter_context(nc.Block())

        @block.sync
        def _(sp):
            for i, w in enumerate((w2l, w2r)):
                for c in range(KC):
                    sp.dma_start(w_sb[:, c, i * G:(i + 1) * G], w[c * P:(c + 1) * P, :]).then_inc(s["weights"], 16)

            def load(t):
                S, w = Super(t), R.width(t)
                wait_count(sp, s["mixed"], S.start - (U - 1) * J)
                ap, p = R.dram(agg, t)
                settle(sp, k["passed"]["sp"])
                sp.dma_start(b["agg"][S.q][0:p, 0:w, :], ap).then_inc(b["agg_in"][S.q], 16)
                ap, p = R.dram(xl, t, F)
                sp.dma_start(ls[S.q][0:p, 0:w, :], ap).then_inc(l_in[S.q], 16)

            def store(t):
                S, w = Super(t), R.width(t)
                sp.wait_ge(s["lr_ready"], S.start + w)
                for i, table in enumerate((xl2, xr2)):
                    ap, p = R.dram(table, t)
                    settle(sp, k["passed"]["sp"])
                    sp.dma_start(ap, lr[S.q][0:p, i, 0:w, :]).then_inc(stored[S.q], 16)

            pipeline(sp, R.tiles, UNROLL, [(0, R.first(load)), (17, R.final(store))], R.tiles - 1)
            for q in range(U):
                sp.wait_ge(stored[q], 32 * ((R.supers - q) // U + 1))

        @block.vector
        def _(dve):
            dve.wait_ge(s["weights"], 16 * 2 * KC)
            n = split_weights(nc, dve, w_sb, w_parts, fold, k["a2"], 1, junk, s["order"])
            dve.wait_ge(s["order"], n)
            nc.vector.memset(junk[:, 0:1], 0.0).then_inc(s["split"], 1)
            differences, _, factors = combined(nc, dve, None, b, s, k, R, U, H, k["own1"], F)

            def mixture(t):
                S, j, m = Super(t), t.slot % J, mix[t.slot % 3]
                if j == 0:
                    dve.wait_ge(l_in[S.q], 16 * (S.u + 1))
                dve.wait_ge(s["scaled"], t.n + 1)
                for h in range(H):
                    ins = nc.vector.scalar_tensor_tensor(out=m[:, h * C:(h + 1) * C],
                                                         in0=ls[S.q][:, j, h * C:(h + 1) * C],
                                                         scalar=b["fac"][S.q][:, 1, j, h:h + 1],
                                                         in1=m[:, h * C:(h + 1) * C], op0=ALU.mult, op1=ALU.add)
                ins.then_inc(s["mixed"], 1)

            def rest(t):
                dve.wait_ge(s["hT1_ready"], t.n + 1)
                wait_count(dve, s["op_ready"], t.n - 2)
                nc.vector.tensor_tensor(hT2[t.slot % 3][:], hT[t.slot % 2][:], hT1[t.slot % 3][:].bitcast(F32),
                                        ALU.subtract).then_inc(s["hT2_ready"], 1)

            def out_copy(t):
                S, j, c = Super(t), t.slot % J, t.slot % 2
                dve.wait_ge(s["op_ready"], t.n + 1)
                if j == 0:
                    wait_count(dve, stored[S.q], 32 * S.u)
                    wait_count(dve, s["g_ready"], S.start - (U - 1) * J)
                nc.vector.tensor_copy(lr[S.q][:, :, j, G], fp[c][:, 0:2])
                nc.vector.tensor_copy(lr[S.q][:, :, j, 0:G], op[c][:].rearrange("p (i g) -> p i g", i=2)
                                      ).then_inc(s["lr_ready"], 1)

            def own_score(t):
                S, j, c = Super(t), t.slot % J, t.slot % 2
                dve.wait_ge(s["ab_ready"], t.n + 1)
                if j == 0:
                    wait_count(dve, s["own_kept"], S.n - U + 1)
                nc.vector.tensor_tensor_reduce(ab[c][:], ab[c][:], k["a2"][:], 1.0, g[t.slot % 3][:, G:G + 1],
                                               ALU.mult, ALU.add, own[S.q][:, j, 0:1]).then_inc(s["own_ready"], 1)

            def keep(t):
                S, w = Super(t), R.width(t)
                dve.wait_ge(s["own_ready"], S.start + w)
                nc.vector.tensor_copy(k["own2"][:, bass.ds(S.start, w), :],
                                      own[S.q][:, 0:w, :]).then_inc(s["own_kept"], 1)

            pipeline(dve, R.tiles, UNROLL,
                     [(11, mixture), (14, rest), (16, out_copy), (19, own_score), (6, R.first(differences)),
                      (8, R.first(factors)), (20, R.final(keep))], R.tiles - 1)

        @block.scalar
        def _(act):
            _, exponents, _ = combined(nc, None, act, b, s, k, R, U, H, k["own1"], F)

            def scale(t):
                S, j, m = Super(t), t.slot % J, mix[t.slot % 3]
                if j == 0:
                    act.wait_ge(s["fac_ready"], S.n + 1)
                wait_count(act, s["turned"], t.n - 2)
                for h in range(H):
                    ins = nc.scalar.activation(m[:, h * C:(h + 1) * C], b["agg"][S.q][:, j, h * C:(h + 1) * C],
                                               ACT.Copy, scale=b["fac"][S.q][:, 0, j, h:h + 1])
                ins.then_inc(s["scaled"], 1)

            def turn(t):
                c = t.slot % 2
                act.wait_ge(s["turned"], t.n + 1)
                wait_count(act, s["hT2_ready"], t.n - 1)
                for q in range(KC):
                    ins = nc.scalar.activation(hT[c][:, q * P:(q + 1) * P], hp[c][:, q * P:(q + 1) * P], ACT.Relu,
                                               bias=k["b1"][:, q:q + 1])
                ins.then_inc(s["hT_ready"], 1)
                act.wait_ge(s["hT_ready"], t.n + 1)
                wait_count(act, s["op_ready"], t.n - 2)
                nc.scalar.copy(hT1[t.slot % 3][:], hT[c][:]).then_inc(s["hT1_ready"], 1)

            def magnitude(t):
                act.wait_ge(s["g_ready"], t.n + 1)
                wait_count(act, s["own_ready"], t.n - 1)
                nc.scalar.activation(ab[t.slot % 2][:], g[t.slot % 3][:, 0:G], ACT.Abs,
                                     scale=1.0 - LINEAR).then_inc(s["ab_ready"], 1)

            pipeline(act, R.tiles, UNROLL,
                     [(13, turn), (10, scale), (18, magnitude), (7, R.first(exponents))], R.tiles - 1)

        @block.gpsimd
        def _(pool):
            def add(t):
                S, j = Super(t), t.slot % J
                pool.wait_ge(s["lr_ready"], t.n + 1)
                wait_count(pool, s["own_ready"], t.n - 2)
                nc.gpsimd.tensor_tensor(g[t.slot % 3][:], lr[S.q][:, 0, j, :], lr[S.q][:, 1, j, :],
                                        ALU.add).then_inc(s["g_ready"], 1)

            pipeline(pool, R.tiles, UNROLL, [(17, add)], R.tiles - 1)

        @block.tensor
        def _(pe):
            pe.wait_ge(s["split"], 1)

            def transposes(t):
                pe.wait_ge(s["mixed"], t.n + 1)
                wait_count(pe, s["hT_ready"], t.n - 1)
                for c in range(KC):
                    ins = nc.tensor.transpose(hp[t.slot % 2][:, c * P:(c + 1) * P],
                                              mix[t.slot % 3][:, c * P:(c + 1) * P], k["ident"][:])
                ins.then_inc(s["turned"], 1)

            def products(t):
                q, h1, h2 = t.slot % 2, hT1[t.slot % 3], hT2[t.slot % 3]
                passes = [(h1, 0), (h1, 1), (h2, 0)]
                pe.wait_ge(s["hT2_ready"], t.n + 1)
                wait_count(pe, s["lr_ready"], t.n - 1)
                for out, weights in ((fp[q][:, 0:2], fold[1:]), (op[q][:], w_parts)):
                    for n, (c, (h, part)) in enumerate([(c, x) for c in range(KC) for x in passes]):
                        ins = nc.tensor.matmul(out, h[:, c * P:(c + 1) * P], weights[part][:, c, :],
                                               start=(n == 0), stop=(n == 3 * KC - 1))
                ins.then_inc(s["op_ready"], 1)

            pipeline(pe, R.tiles, UNROLL, [(15, products), (12, transposes)], R.tiles - 1)


def node_output(nc, k, xl2, agg2, x1, out):
    R = k["rows"]
    U = 3
    F = out.shape[1]
    with ExitStack() as ctx:
        ph = Phase(nc, ctx, "out")
        b = combined_buffers(ph, U, 1, agg2.shape[1])
        ls = [ph.sb(f"l{q}", [P, J, F]) for q in range(U)]
        xs = [ph.sb(f"x{q}", [P, J, F]) for q in range(U)]
        mix = [ph.sb(f"mix{q}", [P, J, F]) for q in range(U)]
        ys = [ph.sb(f"y{q}", [P, J, F]) for q in range(U)]
        l_in, x_in, stored = ph.sems("l_in", U), ph.sems("x_in", U), ph.sems("stored", U)
        names = COMBINED + ("y_ready", "biased")
        s = {n: ph.sem(n) for n in names}
        block = ctx.enter_context(nc.Block())

        @block.sync
        def _(sp):
            def load(t):
                S, w = Super(t), R.width(t)
                wait_count(sp, s["mixed"], S.start - (U - 1) * J)
                ap, p = R.dram(agg2, t)
                settle(sp, k["passed"]["sp"])
                sp.dma_start(b["agg"][S.q][0:p, 0:w, :], ap).then_inc(b["agg_in"][S.q], 16)
                ap, p = R.dram(xl2, t, F)
                sp.dma_start(ls[S.q][0:p, 0:w, :], ap).then_inc(l_in[S.q], 16)
                wait_count(sp, s["y_ready"], S.n - U + 1)
                ap, p = R.dram(x1, t, F)
                settle(sp, k["passed"]["sp"])
                sp.dma_start(xs[S.q][0:p, 0:w, :], ap).then_inc(x_in[S.q], 16)

            pipeline(sp, R.tiles, UNROLL, [(0, R.first(load))], R.tiles - 1)

        @block.vector
        def _(dve):
            differences, _, factors = combined(nc, dve, None, b, s, k, R, U, 1, k["own2"], F)

            def mixture(t):
                S, j = Super(t), t.slot % J
                if j == 0:
                    dve.wait_ge(l_in[S.q], 16 * (S.u + 1))
                dve.wait_ge(s["scaled"], t.n + 1)
                nc.vector.scalar_tensor_tensor(out=mix[S.q][:, j, :], in0=ls[S.q][:, j, :],
                                               scalar=b["fac"][S.q][:, 1, j, 0:1], in1=mix[S.q][:, j, :],
                                               op0=ALU.mult, op1=ALU.add).then_inc(s["mixed"], 1)

            def result(t):
                S, w = Super(t), R.width(t)
                dve.wait_ge(s["biased"], S.n + 1)
                wait_count(dve, stored[S.q], 16 * S.u)
                dve.wait_ge(s["mixed"], S.start + w)
                nc.vector.tensor_tensor(ys[S.q][:, 0:w, :], mix[S.q][:, 0:w, :], xs[S.q][:, 0:w, :],
                                        ALU.add).then_inc(s["y_ready"], 1)

            pipeline(dve, R.tiles, UNROLL, [(10, mixture), (10, R.final(result)), (6, R.first(differences)),
                                            (8, R.first(factors))], R.tiles - 1)

        @block.scalar
        def _(act):
            _, exponents, _ = combined(nc, None, act, b, s, k, R, U, 1, k["own2"], F)

            def scale(t):
                S, j = Super(t), t.slot % J
                if j == 0:
                    act.wait_ge(s["fac_ready"], S.n + 1)
                    wait_count(act, s["y_ready"], S.n - U + 1)
                nc.scalar.activation(mix[S.q][:, j, :], b["agg"][S.q][:, j, 0:F], ACT.Copy,
                                     scale=b["fac"][S.q][:, 0, j, 0:1]).then_inc(s["scaled"], 1)

            def store(t):
                S = Super(t)
                act.wait_ge(s["y_ready"], S.n + 1)
                ap, p = R.dram(out, t)
                settle(act, k["passed"]["act"])
                act.dma_start(ap, ys[S.q][0:p, 0:R.width(t), :]).then_inc(stored[S.q], 16)

            pipeline(act, R.tiles, UNROLL, [(9, scale), (7, R.first(exponents)), (11, R.final(store))], R.tiles - 1)
            for q in range(U):
                act.wait_ge(stored[q], 16 * ((R.supers - q) // U + 1))

        @block.gpsimd
        def _(pool):
            def bias(t):
                S, w = Super(t), R.width(t)
                pool.wait_ge(x_in[S.q], 16 * (S.u + 1))
                nc.gpsimd.tensor_tensor(xs[S.q][:, 0:w, :], xs[S.q][:, 0:w, :],
                                        k["b2"][:].unsqueeze(1).to_broadcast([P, w, F]), ALU.add
                                        ).then_inc(s["biased"], 1)

            pipeline(pool, R.tiles, UNROLL, [(6, R.first(bias))], R.tiles - 1)


def gnn(nc, x, src, dst, edge_weight, W1l, W1r, a1, b1, W2l, W2r, a2, b2, out):
    N, D = x.shape
    E = src.shape[0]
    H, C = a1.shape
    F1, F2 = H * C, W2l.shape[1]
    T = (E + Q - 1) // Q
    dram = lambda name, shape, dt=F32: nc.dram_tensor(name, shape, dt).ap()
    x1 = dram("x1", (N + 2 * P, D))
    xl1, xr1 = dram("xl1", (N, F1 + H)), dram("xr1", (N, F1 + H))
    agg1, agg2 = dram("agg1", (N, F1 + 2 * H)), dram("agg2", (N, F2 + 2))
    xl2, xr2 = dram("xl2", (N, F2 + 1)), dram("xr2", (N, F2 + 1))
    with ExitStack() as ctx:
        ph = Phase(nc, ctx, "kept", last=True)
        rows = Rows(N)
        k = {"n": N, "e": E, "t": T, "rows": rows, "h1": H, "agg_m": {H: F1 + H, 1: F2 + 1},
             "ident": ph.sb("ident", [P, P]), "row_one": ph.sb("row_one", [P, P]),
             "below": ph.sb("below", [P, P]),
             "dump_i": ph.sb("dump_i", [P, 2], I32), "dump": ph.sb("dump", [P, 2]), "eps": ph.sb("eps", [P, 1]),
             "ci": ph.sb("ci", [P, T, 3], I32), "cf": ph.sb("cf", [P, T, 2]), "li_src": ph.sb("li_src", [P, T, 2]),
             "own1": ph.sb("own1", [P, rows.tiles, H]), "own2": ph.sb("own2", [P, rows.tiles, 1]),
             "a1": ph.sb("a1", [P, F1]), "a2": ph.sb("a2", [P, F2]), "b1": ph.sb("b1", [P, F1 // P]),
             "b2": ph.sb("b2", [P, F2]), "ready": ph.sem("ready"),
             "passed": {e: ph.sem(f"passed_{e}") for e in ("sp", "act", "pool", "dve")}}
        constants(nc, k)
        with nc.Block() as block:
            @block.sync
            def _(sp):
                sp.dma_start(k["a1"][:], a1.rearrange("h c -> (h c)").partition_broadcast(P)).then_inc(k["ready"], 16)
                sp.dma_start(k["a2"][:], a2.rearrange("h c -> (h c)").partition_broadcast(P)).then_inc(k["ready"], 16)
                sp.dma_start(k["b2"][:], b2.partition_broadcast(P)).then_inc(k["ready"], 16)
                sp.dma_start(k["b1"][:], b1.rearrange("(c p) -> p c", p=P),
                             allow_slow_non_contiguous=True).then_inc(k["ready"], 16)
                sp.wait_ge(k["ready"], 64)
        edge_columns(nc, k, src, dst, edge_weight, dst[1:E])
        weighted_scatter(nc, k, x, x1, agg1, agg2)
        node_projections(nc, k, x1, W1l, W1r, xl1, xr1)
        edge_softmax(nc, k, "ed1", xl1, xr1, agg1, k["a1"], H)
        node_hidden(nc, k, xl1, agg1, W2l, W2r, xl2, xr2)
        edge_softmax(nc, k, "ed2", xl2, xr2, agg2, k["a2"], 1)
        node_output(nc, k, xl2, agg2, x1, out)


_INS = ["x", "src", "dst", "edge_weight", "L1_gnn_W1l", "L1_gnn_W1r", "L1_gnn_a1", "L1_gnn_b1", "L1_gnn_W2l",
        "L1_gnn_W2r", "L1_gnn_a2", "L1_gnn_b2"]


def kernel(**inputs):
    import numpy as _np
    import concourse.bacc as _bacc
    from concourse import mybir as _mybir
    from concourse.bass_utils import run_bass_kernel_spmd as _run

    nc = _bacc.Bacc("TRN2", target_bir_lowering=False, num_devices=1)
    arrays, args = {}, []
    for name in _INS:
        a = _np.ascontiguousarray(inputs[name])
        arrays[f"in_{name}_dram"] = a
        args.append(nc.dram_tensor(f"in_{name}_dram", a.shape, _mybir.dt.from_np(a.dtype), kind="ExternalInput").ap())
    out = nc.dram_tensor("out_0_dram", inputs["x"].shape, _mybir.dt.float32, kind="ExternalOutput").ap()
    gnn(nc, *args, out)
    r = _run(nc, [arrays], core_ids=[0])
    return r.results[0]["out_0_dram"]
```

```python
from contextlib import ExitStack

import concourse.bass as bass
from concourse import mybir

ALU = mybir.AluOpType
ACT = mybir.ActivationFunctionType
F32 = mybir.dt.float32
F32R = mybir.dt.float32r
I32 = mybir.dt.int32

P = 128
BIG = 1.0e30
EPS = 1e-5
SLOPE = 0.2
LINEAR = (1 + SLOPE) / 2
SKIP = 60000


class Tile:

    def __init__(self, u, slot, unroll, static):
        self.u, self.slot, self.static = u, slot, static
        self.n = u * unroll + slot


def pipeline(eng, count, unroll, steps, rolled_to=None):
    rolled_to = count if rolled_to is None else rolled_to
    longest = max(lag for lag, _ in steps)
    start = longest + unroll
    loops = max(0, (rolled_to - start) // unroll)

    def beat(base, offset, static):
        for lag, fn in steps:
            c = offset - lag
            if static:
                n = base * unroll + c
                if 0 <= n < count:
                    fn(Tile(n // unroll, n % unroll, unroll, True))
            else:
                fn(Tile(base + c // unroll, c % unroll, unroll, False))

    for i in range(min(start, count + longest)):
        beat(0, i, True)
    if loops > 0:
        with eng.Fori(0, loops) as r:
            for k in range(unroll):
                beat(r, start + k, False)
    for i in range(start + loops * unroll, count + longest):
        beat(0, i, True)


def wait_count(eng, semaphore, value):
    if isinstance(value, int) and value <= 0:
        return
    eng.wait_ge(semaphore, value)


def settle(eng, passed):
    eng.sem_inc(passed, 1)


class Phase:

    def __init__(self, nc, ctx, name, last=False):
        self.nc, self.ctx, self.name, self.taken = nc, ctx, name, []
        if not last:
            ctx.callback(self.end)

    def end(self):
        self.nc.clear_and_free_semaphores(self.taken)
        self.nc.all_engine_barrier()

    def sb(self, name, shape, dt=F32):
        return self.ctx.enter_context(self.nc.sbuf_tensor(f"{self.name}_{name}", shape, dt))

    def ps(self, name, shape, dt=F32):
        return self.ctx.enter_context(self.nc.psum_tensor(f"{self.name}_{name}", shape, dt))

    def sem(self, name):
        self.taken.append(self.nc.alloc_semaphore(f"{self.name}_{name}"))
        return self.taken[-1]

    def sems(self, name, n):
        return [self.sem(f"{name}{k}") for k in range(n)]


J = 6


UNROLL = 3 * J


class Rows:
    def __init__(self, n):
        self.n = n
        self.supers = n // (P * J)
        self.rest = n - self.supers * P * J
        assert 0 < self.rest <= P and self.rest % 16 == 0
        self.tiles = self.supers * J + 1

    def tail(self, tile):
        return tile.static and tile.n == self.tiles - 1

    def width(self, tile):
        return 1 if self.tail(tile) else J

    def dram(self, table, tile, cols=None):
        d = table.shape[1] if cols is None else cols
        if self.tail(tile):
            return table[self.supers * P * J:self.n, 0:d].rearrange("(p j) d -> p j d", j=1), self.rest
        return table[bass.ds(Super(tile).n * (P * J), P * J), 0:d].rearrange("(p j) d -> p j d", j=J), P

    def first(self, fn):
        return lambda t: fn(t) if t.slot % J == 0 else None

    def final(self, fn):
        return lambda t: fn(t) if t.slot % J == J - 1 or self.tail(t) else None


class Super:

    def __init__(self, tile):
        self.q, self.u = tile.slot // J, tile.u
        self.n = tile.u * (UNROLL // J) + self.q
        self.start = self.n * J


def constants(nc, k):
    with ExitStack() as ctx:
        ph = Phase(nc, ctx, "consts")
        filled = ph.sem("filled")
        block = ctx.enter_context(nc.Block())

        @block.gpsimd
        def _(pool):
            nc.gpsimd.memset(k["ident"][:], 0.0).then_inc(filled, 1)
            nc.gpsimd.memset(k["row_one"][:], 0.0).then_inc(filled, 1)
            nc.gpsimd.memset(k["before"][:], 1.0).then_inc(filled, 1)
            nc.gpsimd.iota(k["dump_i"][:], [[P, 2]], base=k["n"], channel_multiplier=1).then_inc(filled, 1)
            pool.wait_ge(filled, 4)
            nc.gpsimd.affine_select(out=k["ident"][:], in_=k["ident"][:], compare_op=ALU.not_equal, fill=1.0,
                                    base=0, pattern=[[-1, P]], channel_multiplier=1).then_inc(filled, 1)
            nc.gpsimd.affine_select(out=k["row_one"][:], in_=k["row_one"][:], compare_op=ALU.not_equal, fill=1.0,
                                    base=-1, pattern=[[0, P]], channel_multiplier=1).then_inc(filled, 1)
            nc.gpsimd.affine_select(out=k["before"][:, P:2 * P], in_=k["before"][:, P:2 * P],
                                    compare_op=ALU.is_gt, fill=0.0,
                                    base=0, pattern=[[-1, P]], channel_multiplier=1).then_inc(filled, 1)
            nc.gpsimd.tensor_copy(k["dump"][:], k["dump_i"][:]).then_inc(filled, 1)
            nc.gpsimd.memset(k["eps"][:], EPS).then_inc(filled, 1)
            pool.wait_ge(filled, 9)


Q = P - 1


def order_edges(nc, k, lists, ordered):
    E, N = k["e"], k["n"]
    PE = P - 3
    TC = E // PE
    NH = (N + P - 1) // P
    CH = [(c * P, min(P, NH - c * P)) for c in range((NH + P - 1) // P)]
    assert PE * TC == E and NH <= 512 and TC % 2 == 0
    U = 2
    src, dst, weight = lists
    with ExitStack() as ctx:
        ph = Phase(nc, ctx, "sort")
        raw_src, raw_dst = ph.sb("raw_src", [PE, TC], I32), ph.sb("raw_dst", [PE, TC], I32)
        raw_next, w = ph.sb("raw_next", [PE, TC], I32), ph.sb("w", [PE, TC])
        d, nxt, above = ph.sb("d", [PE, TC]), ph.sb("nxt", [PE, TC]), ph.sb("above", [PE, TC])
        falls, ones = ph.sb("falls", [PE, 1]), ph.sb("ones", [P, P])
        flag = ph.sb("flag", [1, 1], I32)
        count = ph.ps("count", [P, 512])
        padded, loaded, order, flagged = ph.sem("padded"), ph.sem("loaded"), ph.sem("order"), ph.sem("flagged")
        summed = ph.sem("summed")
        with nc.Block() as block:
            @block.sync
            def _(sp):
                for to, a in zip(ordered, lists):
                    sp.dma_start(to, a).then_inc(loaded, 16)
                grid = lambda a: a.rearrange("(p t) -> p t", p=PE)
                sp.dma_start(raw_src[:], grid(src)).then_inc(loaded, 16)
                sp.dma_start(raw_dst[:], grid(dst)).then_inc(loaded, 16)
                sp.dma_start(w[:], grid(weight)).then_inc(loaded, 16)
                sp.wait_ge(padded, 1)
                sp.dma_start(raw_next[0:PE - 1, :], dst[1:1 + (PE - 1) * TC].rearrange("(p t) -> p t", p=PE - 1)
                             ).then_inc(loaded, 16)
                sp.dma_start(raw_next[PE - 1:PE, 0:TC - 1],
                             dst[1 + (PE - 1) * TC:E].rearrange("(p t) -> p t", p=1)).then_inc(loaded, 16)
                sp.wait_ge(loaded, 16 * 8)

            @block.vector
            def _(dve):
                nc.vector.memset(raw_next[:], N).then_inc(padded, 1)
                nc.vector.memset(ones[:], 1.0)
                dve.wait_ge(loaded, 16 * 8)
                nc.vector.tensor_copy(d[:], raw_dst[:]).then_inc(order, 1)
                nc.vector.tensor_copy(nxt[:], raw_next[:]).then_inc(order, 1)
                dve.wait_ge(order, 2)
                nc.vector.scalar_tensor_tensor(out=above[:], in0=d[:], scalar=0.0, in1=nxt[:], op0=ALU.add,
                                               op1=ALU.is_gt, accum_out=falls[:]).then_inc(order, 1)
                dve.wait_ge(summed, 1)
                nc.vector.tensor_copy(flag[:], count[0:1, 0:1]).then_inc(flagged, 1)

            @block.tensor
            def _(pe):
                pe.wait_ge(order, 3)
                nc.tensor.matmul(count[0:1, 0:1], falls[:], ones[0:PE, 0:1], start=True, stop=True).then_inc(summed, 1)

        out_of_order = nc.values_load(flag[0:1, 0:1], min_val=0, max_val=E,
                                      skip_runtime_bounds_check_because="it counts some of the edges")
        step, step_f = ph.sb("step", [P, 512], I32), ph.sb("step_f", [P, 512])
        part, part_f = ph.sb("part", [P, 1], I32), ph.sb("part_f", [P, len(CH)])
        cut, rounded = ph.sb("cut", [PE, TC]), ph.sb("rounded", [PE, TC])
        keys = ph.sb("keys", [PE, TC, 3])
        beyond = [ph.sb(f"beyond{c}", [P, 512]) for c in range(len(CH))]
        counts, run = ph.sb("counts", [P, 512]), ph.sb("run", [P, 512])
        totals = [ph.sb(f"totals{c}", [P, P]) for c in range(len(CH))]
        col = [ph.sb(f"col{q}", [PE, 3]) for q in range(U)]
        at_lo = [ph.sb(f"at_lo{q}", [PE, P]) for q in range(U)]
        at_hi = [ph.sb(f"at_hi{q}", [PE, 512]) for q in range(U)]
        lo_rows, found = ph.sb("lo_rows", [P, PE]), ph.sb("found", [PE, 512])
        met, base, rank = ph.sb("met", [PE, PE]), ph.sb("base", [PE, 1]), ph.sb("rank", [PE, 1])
        place = [ph.sb(f"place{q}", [PE, 1], I32) for q in range(U)]
        moved = [[ph.sb(f"moved_{n}{q}", [PE, 1], t) for n, t in (("src", I32), ("dst", I32), ("w", F32))]
                 for q in range(U)]
        total_ps, lo_ps, row_ps = ph.ps("total", [P, 512]), ph.ps("lo", [P, 512]), ph.ps("row", [P, 512])
        found_ps, more_ps = ph.ps("found_ps", [P, 512]), ph.ps("more", [P, 512])
        names = ("steps", "ready", "hist_col", "hist_hot", "counted", "copied", "total_ready", "total_copied",
                 "based", "run_ready", "col_ready", "hot_ready", "turned", "lo_copied", "found_ready", "ranked",
                 "placed")
        s = {n: ph.sem(n) for n in names}
        scattered = ph.sems("scattered", U)
        block = ctx.enter_context(nc.Block())

        @block.gpsimd
        def _(pool):
            with pool.If(out_of_order > 0):
                nc.gpsimd.iota(step[:], [[1, 512]], base=0, channel_multiplier=0).then_inc(s["steps"], 1)
                nc.gpsimd.iota(part[:], [[1, 1]], base=0, channel_multiplier=1).then_inc(s["steps"], 1)

                def scatter(t):
                    pool.wait_ge(s["placed"], t.n + 1)
                    settle(pool, k["passed"]["pool"])
                    for a, to in zip(moved[t.slot], ordered):
                        pool.indirect_dma_start(to.rearrange("(e o) -> e o", o=1),
                                                bass.IndirectOffsetOnAxis(place[t.slot][:], 0), a[:], None,
                                                bounds_check=E - 1).then_inc(scattered[t.slot], 16)

                pipeline(pool, TC, U, [(1, scatter)])
                for q in range(U):
                    pool.wait_ge(scattered[q], 48 * (TC // U))

        @block.scalar
        def _(act):
            with act.If(out_of_order > 0):
                def copy_lo(t):
                    act.wait_ge(s["turned"], t.n + 1)
                    wait_count(act, s["found_ready"], t.n)
                    nc.scalar.copy(lo_rows[:], lo_ps[:, 0:PE]).then_inc(s["lo_copied"], 1)

                pipeline(act, TC, U, [(1, copy_lo)])

        def one_hot(dve, t, staged, hot, free):
            c = t.slot
            free(t)
            nc.vector.tensor_copy(col[c][:], keys[:, bass.ds(t.n, 1), :].rearrange("p a b -> p (a b)")
                                  ).then_inc(staged, 1)
            dve.wait_ge(staged, t.n + 1)
            nc.vector.tensor_scalar(at_lo[c][:], step_f[0:PE, 0:P], col[c][:, 0:1], None, ALU.is_equal)
            nc.vector.tensor_scalar(at_hi[c][:, 0:NH], step_f[0:PE, 0:NH], col[c][:, 1:2], None,
                                    ALU.is_equal).then_inc(hot, 1)

        @block.vector
        def _(dve):
            with dve.If(out_of_order > 0):
                dve.wait_ge(s["steps"], 2)
                n = 0
                done = lambda ins: ins.then_inc(s["ready"], 1)
                done(nc.vector.tensor_scalar(cut[:], d[:], 1.0 / P, -(P - 1) / (2.0 * P), ALU.mult, ALU.add))
                done(nc.vector.tensor_copy(step_f[:], step[:]))
                done(nc.vector.tensor_copy(part_f[:, 0:1], part[:]))
                dve.wait_ge(s["ready"], 3)
                done(nc.vector.tensor_scalar(rounded[:], cut[:], 12582912.0, None, ALU.add))
                for c in range(1, len(CH)):
                    ins = nc.vector.tensor_scalar(part_f[:, c:c + 1], part_f[:, 0:1], float(c * P), None, ALU.add)
                done(ins)
                dve.wait_ge(s["ready"], 5)
                done(nc.vector.tensor_scalar(keys[:, :, 1], rounded[:], -12582912.0, None, ALU.add))
                for c in range(len(CH)):
                    ins = nc.vector.tensor_scalar(beyond[c][:], step_f[:], part_f[:, c:c + 1], None, ALU.is_gt)
                done(ins)
                dve.wait_ge(s["ready"], 7)
                nc.vector.tensor_copy(keys[:, :, 2], d[:])
                done(nc.vector.scalar_tensor_tensor(out=keys[:, :, 0], in0=keys[:, :, 1], scalar=float(-P), in1=d[:],
                                                    op0=ALU.mult, op1=ALU.add))
                dve.wait_ge(s["ready"], 8)

                def counted(t):
                    wait_count(dve, s["counted"], t.n - U + 1)
                pipeline(dve, TC, U, [(0, lambda t: one_hot(dve, t, s["hist_col"], s["hist_hot"], counted))])
                dve.wait_ge(s["counted"], TC)
                nc.vector.tensor_copy(counts[:, 0:NH], count[:, 0:NH]).then_inc(s["copied"], 1)
                for c, (_, width) in enumerate(CH):
                    dve.wait_ge(s["total_ready"], c + 1)
                    nc.vector.tensor_copy(totals[c][0:width, :], total_ps[0:width, 0:P]).then_inc(s["total_copied"], 1)
                dve.wait_ge(s["based"], 1)
                nc.vector.tensor_copy(run[:, 0:NH], count[:, 0:NH]).then_inc(s["run_ready"], 1)

                def placed_before(t):
                    wait_count(dve, s["found_ready"], t.n - U + 1)

                def place_tile(t):
                    c = t.slot
                    dve.wait_ge(s["turned"], t.n + 1)
                    dve.wait_ge(s["found_ready"], t.n + 1)
                    wait_count(dve, s["placed"], t.n)
                    nc.vector.scalar_tensor_tensor(out=met[:], in0=row_ps[0:PE, 0:PE], scalar=col[c][:, 2:3],
                                                   in1=k["before"][0:PE, P:P + PE], op0=ALU.is_equal, op1=ALU.mult,
                                                   accum_out=rank[:])
                    nc.vector.tensor_tensor(run[:, 0:NH], run[:, 0:NH], more_ps[:, 0:NH],
                                            ALU.add).then_inc(s["run_ready"], 1)
                    nc.vector.tensor_tensor_reduce(found[:, 0:NH], found_ps[0:PE, 0:NH], at_hi[c][:, 0:NH], 1.0, 0.0,
                                                   ALU.mult, ALU.add, base[:]).then_inc(s["ranked"], 1)
                    dve.wait_ge(s["ranked"], t.n + 1)
                    wait_count(dve, scattered[c], 48 * t.u)
                    nc.vector.tensor_copy(moved[c][0][:], raw_src[:, bass.ds(t.n, 1)])
                    nc.vector.tensor_copy(moved[c][1][:], raw_dst[:, bass.ds(t.n, 1)])
                    nc.vector.tensor_copy(moved[c][2][:], w[:, bass.ds(t.n, 1)])
                    nc.vector.tensor_tensor(place[c][:], base[:], rank[:], ALU.add).then_inc(s["placed"], 1)

                pipeline(dve, TC, U, [(0, lambda t: one_hot(dve, t, s["col_ready"], s["hot_ready"], placed_before)),
                                      (1, place_tile)])

        @block.tensor
        def _(pe):
            with pe.If(out_of_order > 0):
                def histogram(t):
                    pe.wait_ge(s["hist_hot"], t.n + 1)
                    nc.tensor.matmul(count[:, 0:NH], at_lo[t.slot][:], at_hi[t.slot][:, 0:NH],
                                     start=(t.static and t.n == 0), stop=(t.static and t.n == TC - 1)
                                     ).then_inc(s["counted"], 1)

                pipeline(pe, TC, U, [(0, histogram)], TC - 1)
                pe.wait_ge(s["copied"], 1)
                for c, (first, width) in enumerate(CH):
                    if c:
                        pe.wait_ge(s["total_copied"], c)
                    nc.tensor.matmul(total_ps[0:width, 0:P], counts[:, first:first + width], ones[:], start=True,
                                     stop=True).then_inc(s["total_ready"], 1)
                pe.wait_ge(s["total_copied"], len(CH))
                nc.tensor.matmul(count[:, 0:NH], beyond[0][:, 0:P], counts[:, 0:NH], start=True, stop=False)
                for c, (_, width) in enumerate(CH):
                    ins = nc.tensor.matmul(count[:, 0:NH], totals[c][0:width, :], beyond[c][0:width, 0:NH],
                                           start=False, stop=(c == len(CH) - 1))
                ins.then_inc(s["based"], 1)

                def turn(t):
                    pe.wait_ge(s["hot_ready"], t.n + 1)
                    wait_count(pe, s["lo_copied"], t.n)
                    wait_count(pe, s["ranked"], t.n)
                    nc.tensor.transpose(row_ps[0:PE, 0:PE], col[t.slot][:, 2:3].to_broadcast([PE, PE]),
                                        k["ident"][0:PE, 0:PE])
                    nc.tensor.transpose(lo_ps[:, 0:PE], at_lo[t.slot][:], k["ident"][0:PE, 0:PE]
                                        ).then_inc(s["turned"], 1)

                def find(t):
                    pe.wait_ge(s["lo_copied"], t.n + 1)
                    pe.wait_ge(s["run_ready"], t.n + 1)
                    wait_count(pe, s["ranked"], t.n)
                    nc.tensor.matmul(found_ps[0:PE, 0:NH], lo_rows[:], run[:, 0:NH], start=True, stop=True)
                    nc.tensor.matmul(more_ps[:, 0:NH], at_lo[t.slot][:], at_hi[t.slot][:, 0:NH], start=True,
                                     stop=True).then_inc(s["found_ready"], 1)

                pipeline(pe, TC, U, [(1, turn), (1, find)])


def edge_columns(nc, k, src, dst, weight, next_dst, x, x1):
    E, N, T = k["e"], k["n"], k["t"]
    full = E // Q
    rest = E - full * Q
    chunks = [(c * P, min(P, T - c * P)) for c in range((T + P - 1) // P)]
    with ExitStack() as ctx:
        ph = Phase(nc, ctx, "cols")
        NC = len(chunks)
        raw_src = [ph.sb(f"raw_src{c}", [P, P], I32) for c in range(NC)]
        raw_dst = [ph.sb(f"raw_dst{c}", [P, P], I32) for c in range(NC)]
        raw_nxt = [ph.sb(f"raw_nxt{c}", [P, P], I32) for c in range(NC)]
        wt = [ph.sb(f"wt{c}", [P, P]) for c in range(NC)]
        names = ["src", "dst", "out_dst", "gather_dst", "last", "weight"]
        val = {n: [ph.sb(f"v_{n}{c}", [P, P]) if n != "weight" else wt[c] for c in range(NC)] for n in names}
        nxt = [ph.sb(f"nxt{c}", [P, P]) for c in range(NC)]
        tp = [ph.ps(f"tp{b}", [P, P]) for b in range(2)]
        padded, loaded, order = ph.sem("padded"), ph.sem("loaded"), ph.sem("order")
        values_ready, turned, copied = ph.sem("values_ready"), ph.sem("turned"), ph.sem("copied")
        loads = []
        for c, (t0, rows) in enumerate(chunks):
            f = min(rows, full - t0)
            lists = ((raw_src, src, rest), (raw_dst, dst, rest), (wt, weight, rest), (raw_nxt, next_dst, rest - 1))
            for buf, a, _ in lists:
                loads.append((buf[c][0:f, 1:P], a[t0 * Q:(t0 + f) * Q].rearrange("(t p) -> t p", p=Q)))
            if f < rows and rest:
                for buf, a, n in lists:
                    loads.append((buf[c][f:f + 1, 1:1 + n], a[full * Q:full * Q + n].rearrange("(t p) -> t p", t=1)))
            first = 1 if c == 0 else 0
            a0 = (t0 + first) * Q - 1
            loads.append((raw_dst[c][first:rows, 0:1],
                          dst[a0:a0 + (rows - first - 1) * Q + 1:Q].rearrange("(t o) -> t o", o=1)))
        block = ctx.enter_context(nc.Block())

        @block.gpsimd
        def _(pool):
            for c in range(NC):
                nc.gpsimd.memset(raw_src[c][:], 0).then_inc(padded, 1)
                nc.gpsimd.memset(raw_dst[c][:], N).then_inc(padded, 1)
                nc.gpsimd.memset(raw_nxt[c][:], N + 1).then_inc(padded, 1)
                nc.gpsimd.memset(wt[c][:], 0.0).then_inc(padded, 1)
            pool.wait_ge(padded, 4 * NC)
            nc.gpsimd.memset(raw_dst[0][0:1, 0:1], -5).then_inc(padded, 1)

        @block.sync
        def _(sp):
            sp.wait_ge(padded, 4 * NC + 1)
            for to, frm in loads:
                sp.dma_start(to, frm, allow_slow_non_contiguous=True).then_inc(loaded, 16)
            whole = lambda table: table[0:N, :].rearrange("(a b e) d -> a b (e d)", a=80, e=5)
            for i in range(0, N // 400, 25):
                    sp.dma_start(whole(x1)[:, i:i + 25, :], whole(x)[:, i:i + 25, :]).then_inc(k["x1_copied"], 16)
            sp.dma_start(x1[N:N + 2 * P, :], x[0:2 * P, :]).then_inc(k["x1_copied"], 16)

        @block.vector
        def _(dve):
            dve.wait_ge(padded, 4 * NC + 1)
            dve.wait_ge(loaded, 16 * len(loads))
            n = 0
            for c in range(NC):
                nc.vector.tensor_copy(val["src"][c][:], raw_src[c][:]).then_inc(order, 1)
                nc.vector.tensor_copy(val["dst"][c][:], raw_dst[c][:]).then_inc(order, 1)
                nc.vector.tensor_copy(val["out_dst"][c][:], raw_dst[c][:]).then_inc(order, 1)
                nc.vector.tensor_copy(nxt[c][:], raw_nxt[c][:]).then_inc(order, 1)
                n += 4
            dve.wait_ge(order, n)
            for c in range(NC):
                d = val["dst"][c]
                nc.vector.tensor_scalar(val["gather_dst"][c][:], d[:], float(N - 1), 0.0, ALU.min,
                                        ALU.max).then_inc(order, 1)
                nc.vector.tensor_copy(val["out_dst"][c][:, 0:1], d[:, P - 1:P]).then_inc(order, 1)
                nc.vector.tensor_tensor(nxt[c][:], d[:], nxt[c][:], ALU.not_equal).then_inc(order, 1)
                n += 3
            dve.wait_ge(order, n)
            for c in range(NC):
                nc.vector.scalar_tensor_tensor(out=val["last"][c][:], in0=val["dst"][c][:], scalar=float(-SKIP),
                                               in1=nxt[c][:], op0=ALU.add, op1=ALU.mult).then_inc(order, 1)
                n += 1
            dve.wait_ge(order, n)
            for c in range(NC):
                nc.vector.tensor_scalar(val["last"][c][:], val["last"][c][:], float(SKIP), None,
                                        ALU.add).then_inc(order, 1)
                n += 1
            dve.wait_ge(order, n)
            for c in range(NC):
                ins = nc.vector.memset(val["last"][c][:, 0:1], float(SKIP))
            ins.then_inc(values_ready, 1)
            at = 0
            for c, (t0, rows) in enumerate(chunks):
                for name in names:
                    dve.wait_ge(turned, at + 1)
                    where = {"src": [k["ci"][:, t0:t0 + rows, 0], k["li_src"][:, t0:t0 + rows, 0]],
                             "gather_dst": [k["ci"][:, t0:t0 + rows, 1]],
                             "last": [k["ci"][:, t0:t0 + rows, 2]],
                             "dst": [k["cf"][:, t0:t0 + rows, 0]],
                             "out_dst": [k["cf"][:, t0:t0 + rows, 1]],
                             "weight": [k["li_src"][:, t0:t0 + rows, 1]]}[name]
                    for w in where:
                        ins = nc.vector.tensor_copy(w, tp[at % 2][:, 0:rows])
                    ins.then_inc(copied, 1)
                    at += 1

        @block.tensor
        def _(pe):
            pe.wait_ge(values_ready, 1)
            at = 0
            for c, (t0, rows) in enumerate(chunks):
                for name in names:
                    if at >= 2:
                        pe.wait_ge(copied, at - 1)
                    nc.tensor.transpose(tp[at % 2][:, 0:rows], val[name][c][0:rows, :],
                                        k["ident"][0:rows, 0:rows]).then_inc(turned, 1)
                    at += 1


def clear_rows(sp, k, neutral, table, cleared):
    R = k["rows"]

    def clear(t):
        ap, p = R.dram(table, t)
        sp.dma_start(ap, neutral[0:p, :].unsqueeze(1).to_broadcast([p, R.width(t), table.shape[1]])
                     ).then_inc(cleared, 16)
    return R.first(clear)


def fill_neutral(nc, k, neutral, H, ready):
    f = k["agg_m"][H]
    nc.vector.memset(neutral[:, 0:f], 0.0).then_inc(ready, 1)
    nc.vector.memset(neutral[:, f:neutral.shape[1]], -BIG).then_inc(ready, 1)


def weighted_scatter(nc, k, x, x1):
    T, U = k["t"], 6
    assert T % 2 == 0
    PAIRS = T // 2
    D = x.shape[1]
    with ExitStack() as ctx:
        ph = Phase(nc, ctx, "l0")
        cols = [ph.sb(f"cols{q}", [P, 2, 2]) for q in range(U)]
        gidx = [ph.sb(f"gidx{q}", [P, 2], I32) for q in range(U)]
        xd = [ph.sb(f"xd{q}", [P, 2, D]) for q in range(U)]
        hd = [ph.sb(f"hd{q}", [P, 2, D]) for q in range(2)]
        st = [ph.sb(f"st{q}", [P, 2, 6]) for q in range(U)]
        mv = [ph.sb(f"mv{q}", [P, 2, 2]) for q in range(U)]
        sd = [ph.sb(f"sd{q}", [P, 2]) for q in range(U)]
        rs = [ph.sb(f"rs{q}", [P, 2]) for q in range(U)]
        nm = [ph.sb(f"nm{q}", [P, 2]) for q in range(U)]
        one = [ph.sb(f"one{q}", [P, P]) for q in range(U)]
        two = [ph.sb(f"two{q}", [P, 2 * P]) for q in range(U)]
        met = [ph.sb(f"met{q}", [P, 3 * P]) for q in range(U)]
        before = [ph.sb(f"before{q}", [P, 2]) for q in range(U)]
        way = [ph.sb(f"way{q}", [P, 2]) for q in range(U)]
        off = [ph.sb(f"off{q}", [P, 2]) for q in range(U)]
        sidx = [ph.sb(f"sidx{q}", [P, 2], I32) for q in range(U)]
        sums = [ph.sb(f"sums{q}", [P, 2, D]) for q in range(U)]
        row = [ph.ps(f"row{q}", [P, 512]) for q in range(2)]
        acc = [ph.ps(f"acc{q}", [P, 2 * D]) for q in range(2)]
        gathered, added = ph.sems("gathered", U), ph.sem("added")
        names = ("cols_ready", "gidx_ready", "row_ready", "same_ready", "way_ready", "off_ready", "sidx_ready",
                 "stats", "moments", "root", "inverse", "shift", "normed", "acc_ready", "sums_ready")
        s = {n: ph.sem(n) for n in names}
        block = ctx.enter_context(nc.Block())

        @block.scalar
        def _(act):
            def deviation(t):
                act.wait_ge(s["moments"], t.n + 1)
                wait_count(act, s["inverse"], t.n - U + 1)
                nc.scalar.activation(sd[t.slot][:], mv[t.slot][:, :, 1], ACT.Sqrt,
                                     bias=k["eps"][:, 0:1]).then_inc(s["root"], 1)

            def normalise(t):
                act.wait_ge(s["shift"], t.n + 1)
                wait_count(act, s["acc_ready"], t.n - 1)
                for i in range(2):
                    ins = nc.scalar.activation(hd[t.slot % 2][:, i, :], xd[t.slot][:, i, :], ACT.Relu,
                                               bias=nm[t.slot][:, i:i + 1], scale=rs[t.slot][:, i:i + 1])
                ins.then_inc(s["normed"], 1)

            def drain(t):
                act.wait_ge(s["acc_ready"], t.n + 1)
                wait_count(act, added, 32 * (t.n - U + 1))
                nc.scalar.copy(sums[t.slot][:], acc[t.slot % 2][:].rearrange("p (i d) -> p i d", i=2)
                               ).then_inc(s["sums_ready"], 1)

            pipeline(act, PAIRS, U, [(8, drain), (6, normalise), (5, deviation)])

        @block.tensor
        def _(pe):
            def row_of(t):
                pe.wait_ge(s["cols_ready"], t.n + 1)
                wait_count(pe, s["same_ready"], t.n - 1)
                for i in range(2):
                    ins = nc.tensor.transpose(row[t.slot % 2][:, i * P:(i + 1) * P],
                                              cols[t.slot][:, i, 0:1].to_broadcast([P, P]), k["ident"][:])
                ins.then_inc(s["row_ready"], 1)

            def total(t):
                c, a, h = t.slot, acc[t.slot % 2], hd[t.slot % 2]
                pe.wait_ge(s["normed"], t.n + 1)
                pe.wait_ge(s["same_ready"], t.n + 1)
                wait_count(pe, s["sums_ready"], t.n - 1)
                nc.tensor.matmul(a[:, 0:D], one[c][:], h[:, 0, :], start=True, stop=False)
                nc.tensor.matmul(a[:, 0:D], two[c][:, 0:P], h[:, 1, :], start=False, stop=True)
                nc.tensor.matmul(a[:, D:2 * D], two[c][:, P:2 * P], h[:, 1, :], start=True,
                                 stop=True).then_inc(s["acc_ready"], 1)

            pipeline(pe, PAIRS, U, [(1, row_of), (7, total)])

        @block.vector
        def _(dve):
            def stage(t):
                wait_count(dve, gathered[t.slot], 32 * t.u)
                nc.vector.tensor_copy(gidx[t.slot][:], k["ci"][:, bass.ds(2 * t.n, 2), 1]).then_inc(s["gidx_ready"], 1)
                wait_count(dve, s["sidx_ready"], t.n - U + 1)
                wait_count(dve, s["row_ready"], t.n - U + 1)
                nc.vector.tensor_copy(cols[t.slot][:], k["li_src"][:, bass.ds(2 * t.n, 2), :]
                                      ).then_inc(s["cols_ready"], 1)

            def match(t):
                c, r = t.slot, row[t.slot % 2]
                dve.wait_ge(s["row_ready"], t.n + 1)
                wait_count(dve, s["acc_ready"], t.n - U + 1)
                wait_count(dve, s["sidx_ready"], t.n - U + 1)
                src, w = (lambda i: cols[c][:, i, 0:1]), (lambda i: cols[c][:, i, 1:2])
                nc.vector.tensor_scalar(one[c][:], r[:, 0:P], src(0), w(0), ALU.is_equal, ALU.mult)
                nc.vector.tensor_scalar(two[c][:], r[:, 0:2 * P], src(1), w(1), ALU.is_equal, ALU.mult)
                nc.vector.scalar_tensor_tensor(out=met[c][:, 0:P], in0=r[:, 0:P], scalar=src(0),
                                               in1=k["before"][:, P:2 * P], op0=ALU.is_equal, op1=ALU.mult,
                                               accum_out=before[c][:, 0:1])
                nc.vector.scalar_tensor_tensor(out=met[c][:, P:3 * P], in0=r[:, 0:2 * P], scalar=src(1),
                                               in1=k["before"][:], op0=ALU.is_equal, op1=ALU.mult,
                                               accum_out=before[c][:, 1:2]).then_inc(s["same_ready"], 1)
                nc.vector.tensor_tensor(way[c][:], k["dump"][:], cols[c][:, :, 0],
                                        ALU.subtract).then_inc(s["way_ready"], 1)

            def offset(t):
                c = t.slot
                dve.wait_ge(s["way_ready"], t.n + 1)
                dve.wait_ge(s["same_ready"], t.n + 1)
                nc.vector.scalar_tensor_tensor(out=off[c][:], in0=before[c][:], scalar=1.0, in1=way[c][:],
                                               op0=ALU.min, op1=ALU.mult).then_inc(s["off_ready"], 1)

            def index(t):
                c = t.slot
                dve.wait_ge(s["off_ready"], t.n + 1)
                wait_count(dve, added, 32 * (t.n - U + 1))
                nc.vector.tensor_tensor(sidx[c][:], off[c][:], cols[c][:, :, 0], ALU.add).then_inc(s["sidx_ready"], 1)

            def statistics(t):
                dve.wait_ge(gathered[t.slot], 32 * (t.u + 1))
                wait_count(dve, s["moments"], t.n - U + 1)
                for i in range(2):
                    ins = nc.vector.bn_stats(st[t.slot][:, i, :], xd[t.slot][:, i, :])
                ins.then_inc(s["stats"], 1)

            def moments(t):
                wait_count(dve, s["root"], t.n - U + 1)
                wait_count(dve, s["shift"], t.n - U + 1)
                dve.wait_ge(s["stats"], t.n + 1)
                settle(dve, k["passed"]["dve"])
                for i in range(2):
                    ins = nc.vector.bn_aggr(mv[t.slot][:, i, :], st[t.slot][:, i, :])
                ins.then_inc(s["moments"], 1)

            def inverse(t):
                dve.wait_ge(s["root"], t.n + 1)
                wait_count(dve, s["normed"], t.n - U + 1)
                nc.vector.reciprocal(rs[t.slot][:], sd[t.slot][:]).then_inc(s["inverse"], 1)

            def shift(t):
                dve.wait_ge(s["inverse"], t.n + 1)
                wait_count(dve, s["normed"], t.n - U + 1)
                nc.vector.scalar_tensor_tensor(out=nm[t.slot][:], in0=mv[t.slot][:, :, 0], scalar=-1.0,
                                               in1=rs[t.slot][:], op0=ALU.mult, op1=ALU.mult
                                               ).then_inc(s["shift"], 1)

            pipeline(dve, PAIRS, U, [(4, moments), (0, stage), (3, offset), (2, match), (4, index), (5, inverse),
                                     (3, statistics), (5, shift)])

        @block.gpsimd
        def _(pool):
            def gather(t):
                pool.wait_ge(s["gidx_ready"], t.n + 1)
                wait_count(pool, s["normed"], t.n - U + 1)
                settle(pool, k["passed"]["pool"])
                for i in range(2):
                    pool.indirect_dma_start(xd[t.slot][:, i, :], None, x,
                                            bass.IndirectOffsetOnAxis(gidx[t.slot][:, i:i + 1], 0),
                                            bounds_check=k["n"] - 1).then_inc(gathered[t.slot], 16)

            def scatter(t):
                if t.static and t.n == 0:
                    pool.wait_ge(k["x1_copied"], 16 * k["x1_copies"])
                pool.wait_ge(s["sidx_ready"], t.n + 1)
                pool.wait_ge(s["sums_ready"], t.n + 1)
                wait_count(pool, added, 32 * t.n)
                settle(pool, k["passed"]["pool"])
                for i in range(2):
                    pool.indirect_dma_start(x1, bass.IndirectOffsetOnAxis(sidx[t.slot][:, i:i + 1], 0),
                                            sums[t.slot][:, i, :], None, bounds_check=k["n"] + 2 * P - 1,
                                            compute_op=ALU.add).then_inc(added, 16)

            pipeline(pool, PAIRS, U, [(9, scatter), (1, gather)])
            pool.wait_ge(added, 32 * PAIRS)


def split_weights(nc, dve, w, parts, folded, att, H, junk, order, n=0):
    KC, F2 = w.shape[1], w.shape[2]
    F = F2 // 2
    C = F // H
    hi, lo = parts
    fold, fhi, flo = folded
    for c in range(KC):
        for i in range(2):
            for h in range(H):
                a = i * F + h * C
                ins = nc.vector.tensor_tensor_reduce(junk[:, a:a + C], w[:, c, a:a + C], att[:, h * C:(h + 1) * C],
                                                     LINEAR, 0.0, ALU.mult, ALU.add,
                                                     fold[:, c, i * H + h:i * H + h + 1])
        ins.then_inc(order, 1)
        n += 1
        dve.wait_ge(order, n)
    w = w[:].rearrange("p k (i f) -> p k i f", i=2)
    nc.vector.tensor_copy(hi[:], w).then_inc(order, 1)
    fold = fold[:].rearrange("p k (i h) -> p k i h", i=2)
    if H == 1:
        fold = fold.to_broadcast(list(fhi.shape))
    nc.vector.tensor_copy(fhi[:], fold).then_inc(order, 1)
    n += 2
    dve.wait_ge(order, n)
    nc.vector.tensor_tensor(lo[:], w, hi[:].bitcast(F32), ALU.subtract).then_inc(order, 1)
    nc.vector.tensor_tensor(flo[:], fold, fhi[:].bitcast(F32), ALU.subtract).then_inc(order, 1)
    return n + 2


def node_projections(nc, k, x1, wl, wr, xl, xr, agg):
    R = k["rows"]
    U = 3
    D, F, H = x1.shape[1], wl.shape[1], k["h1"]
    C = F // H
    KC = D // P
    with ExitStack() as ctx:
        ph = Phase(nc, ctx, "np1")
        w_sb = ph.sb("w", [P, KC, 2 * F])
        w_parts = [ph.sb(f"w_part{i}", [P, KC, 2, F + H], F32R) for i in range(2)]
        B = 2 * (F + H) // 3
        assert 3 * B == 2 * (F + H) and B % 2 == 0 and B <= 512
        fold = ph.sb("fold", [P, KC, 2 * H])
        xs = [ph.sb(f"x{q}", [P, J, D]) for q in range(U)]
        hs = [ph.sb(f"h{q}", [P, D]) for q in range(3)]
        st = [ph.sb(f"st{q}", [P, J, 6]) for q in range(U)]
        mv = [ph.sb(f"mv{q}", [P, J, 2]) for q in range(U)]
        sd = [ph.sb(f"sd{q}", [P, J]) for q in range(U)]
        rs = [ph.sb(f"rs{q}", [P, J]) for q in range(U)]
        nm = [ph.sb(f"nm{q}", [P, J]) for q in range(U)]
        hT1 = [ph.sb(f"hTa{q}", [P, D], F32R) for q in range(3)]
        hT2 = [ph.sb(f"hTb{q}", [P, D], F32R) for q in range(3)]
        lr = [ph.sb(f"lr{q}", [P, J, 2 * (F + H)]) for q in range(U)]
        g = [ph.sb(f"g{q}", [P, F + H]) for q in range(3)]
        ab = [ph.sb(f"ab{q}", [P, F]) for q in range(2)]
        junk = ph.sb("junk", [P, 2 * F])
        own = [ph.sb(f"own{q}", [P, J, H]) for q in range(U)]
        hp = [ph.ps(f"hp{q}", [P, 512]) for q in range(2)]
        lp = [ph.ps(f"lp{q}", [P, 2, 512]) for q in range(2)]
        rp = [ph.ps(f"rp{q}", [P, 512]) for q in range(2)]
        loaded, stored = ph.sems("loaded", U), ph.sems("stored", U)
        neutral, cleared = ph.sb("neutral", [P, agg.shape[1]]), ph.sem("cleared")
        names = ("neutral_ready", "weights", "order", "split", "stats", "moments", "root", "inverse", "shift", "normed", "turned",
                 "hT1_ready", "hT2_ready", "lp_ready", "rp_ready", "l_ready", "r_ready", "g_ready", "ab_ready",
                 "own_ready", "own_kept")
        s = {n: ph.sem(n) for n in names}
        block = ctx.enter_context(nc.Block())

        @block.sync
        def _(sp):
            for i, w in enumerate((wl, wr)):
                for c in range(KC):
                    sp.dma_start(w_sb[:, c, i * F:(i + 1) * F], w[c * P:(c + 1) * P, :]).then_inc(s["weights"], 16)

            def load(t):
                S = Super(t)
                wait_count(sp, s["normed"], S.start - (U - 1) * J)
                ap, p = R.dram(x1, t)
                settle(sp, k["passed"]["sp"])
                sp.dma_start(xs[S.q][0:p, 0:R.width(t), :], ap).then_inc(loaded[S.q], 16)

            def store(t):
                S = Super(t)
                w = R.width(t)
                sp.wait_ge(s["l_ready"], S.start + w)
                settle(sp, k["passed"]["sp"])
                sp.wait_ge(s["r_ready"], S.start + w)
                for i, table in enumerate((xl, xr)):
                    ap, p = R.dram(table, t)
                    settle(sp, k["passed"]["sp"])
                    sp.dma_start(ap, lr[S.q][0:p, 0:w, i * (F + H):(i + 1) * (F + H)]).then_inc(stored[S.q], 16)

            sp.wait_ge(s["neutral_ready"], 2)
            clear = clear_rows(sp, k, neutral, agg, cleared)
            pipeline(sp, R.tiles, UNROLL, [(0, R.first(load)), (3, clear), (19, R.final(store))], R.tiles - 1)
            sp.wait_ge(cleared, 16 * (R.supers + 1))
            for q in range(U):
                sp.wait_ge(stored[q], 32 * ((R.supers - q) // U + 1))

        @block.vector
        def _(dve):
            fill_neutral(nc, k, neutral, H, s["neutral_ready"])
            dve.wait_ge(s["weights"], 16 * 2 * KC)
            n = split_weights(nc, dve, w_sb, [a[:, :, :, 0:F] for a in w_parts],
                              [fold] + [a[:, :, :, F:F + H] for a in w_parts], k["a1"], H, junk, s["order"])
            dve.wait_ge(s["order"], n)
            nc.vector.memset(junk[:, 0:1], 0.0).then_inc(s["split"], 1)

            def statistics(t):
                S, j = Super(t), t.slot % J
                if j == 0:
                    dve.wait_ge(loaded[S.q], 16 * (S.u + 1))
                    wait_count(dve, s["moments"], S.n - U + 1)
                nc.vector.bn_stats(st[S.q][:, j, :], xs[S.q][:, j, :]).then_inc(s["stats"], 1)

            def moments(t):
                S = Super(t)
                wait_count(dve, s["root"], S.n - U + 1)
                wait_count(dve, s["shift"], S.n - U + 1)
                dve.wait_ge(s["stats"], S.start + R.width(t))
                settle(dve, k["passed"]["dve"])
                for j in range(R.width(t)):
                    ins = nc.vector.bn_aggr(mv[S.q][:, j, :], st[S.q][:, j, :])
                ins.then_inc(s["moments"], 1)

            def scales(t):
                S = Super(t)
                dve.wait_ge(s["root"], S.n + 1)
                wait_count(dve, s["normed"], S.start - (U - 1) * J)
                nc.vector.reciprocal(rs[S.q][:], sd[S.q][:]).then_inc(s["inverse"], 1)
                dve.wait_ge(s["inverse"], S.n + 1)
                nc.vector.scalar_tensor_tensor(out=nm[S.q][:], in0=mv[S.q][:, :, 0], scalar=-1.0,
                                               in1=rs[S.q][:], op0=ALU.mult, op1=ALU.mult).then_inc(s["shift"], 1)

            def rest(t):
                dve.wait_ge(s["hT1_ready"], t.n + 1)
                wait_count(dve, s["rp_ready"], t.n - 2)
                nc.vector.tensor_tensor(hT2[t.slot % 3][:], hp[t.slot % 2][:, 0:D], hT1[t.slot % 3][:].bitcast(F32),
                                        ALU.subtract).then_inc(s["hT2_ready"], 1)

            def right(t):
                S, j, b = Super(t), t.slot % J, t.slot % 2
                dve.wait_ge(s["rp_ready"], t.n + 1)
                if j == 0:
                    wait_count(dve, stored[S.q], 32 * S.u)
                    wait_count(dve, s["g_ready"], S.start - (U - 1) * J)
                nc.vector.tensor_copy(lr[S.q][:, j, 2 * B:3 * B], rp[b][:, 0:B]).then_inc(s["r_ready"], 1)

            def own_score(t):
                S, j, b = Super(t), t.slot % J, t.slot % 2
                dve.wait_ge(s["ab_ready"], t.n + 1)
                if j == 0:
                    wait_count(dve, s["own_kept"], S.n - U + 1)
                for h in range(H):
                    ins = nc.vector.tensor_tensor_reduce(ab[b][:, h * C:(h + 1) * C], ab[b][:, h * C:(h + 1) * C],
                                                         k["a1"][:, h * C:(h + 1) * C], 1.0,
                                                         g[t.slot % 3][:, F + h:F + h + 1], ALU.mult, ALU.add,
                                                         own[S.q][:, j, h:h + 1])
                ins.then_inc(s["own_ready"], 1)

            def keep(t):
                S, w = Super(t), R.width(t)
                dve.wait_ge(s["own_ready"], S.start + w)
                nc.vector.tensor_copy(k["own1"][:, bass.ds(S.start, w), :],
                                      own[S.q][:, 0:w, :]).then_inc(s["own_kept"], 1)

            pipeline(dve, R.tiles, UNROLL,
                     [(16, rest), (18, right), (21, own_score), (6, statistics), (6, R.final(moments)),
                      (8, R.final(scales)), (22, R.final(keep))], R.tiles - 1)

        @block.scalar
        def _(act):
            def deviation(t):
                S = Super(t)
                act.wait_ge(s["moments"], S.n + 1)
                wait_count(act, s["inverse"], S.n - U + 1)
                nc.scalar.activation(sd[S.q][:], mv[S.q][:, :, 1], ACT.Sqrt,
                                     bias=k["eps"][:, 0:1]).then_inc(s["root"], 1)

            def normalise(t):
                S, j = Super(t), t.slot % J
                if j == 0:
                    act.wait_ge(s["shift"], S.n + 1)
                wait_count(act, s["turned"], t.n - 2)
                nc.scalar.activation(hs[t.slot % 3][:], xs[S.q][:, j, :], ACT.Relu,
                                     bias=nm[S.q][:, j:j + 1], scale=rs[S.q][:, j:j + 1]).then_inc(s["normed"], 1)

            def turn(t):
                act.wait_ge(s["turned"], t.n + 1)
                wait_count(act, s["rp_ready"], t.n - 2)
                nc.scalar.copy(hT1[t.slot % 3][:], hp[t.slot % 2][:, 0:D]).then_inc(s["hT1_ready"], 1)

            def left(t):
                S, j = Super(t), t.slot % J
                act.wait_ge(s["lp_ready"], t.n + 1)
                if j == 0:
                    wait_count(act, stored[S.q], 32 * S.u)
                    wait_count(act, s["g_ready"], S.start - (U - 1) * J)
                nc.scalar.copy(lr[S.q][:, j, 0:2 * B].rearrange("p (i b) -> p i b", i=2), lp[t.slot % 2][:, :, 0:B]).then_inc(s["l_ready"], 1)

            def magnitude(t):
                act.wait_ge(s["g_ready"], t.n + 1)
                wait_count(act, s["own_ready"], t.n - 1)
                nc.scalar.activation(ab[t.slot % 2][:], g[t.slot % 3][:, 0:F], ACT.Abs,
                                     scale=1.0 - LINEAR).then_inc(s["ab_ready"], 1)

            pipeline(act, R.tiles, UNROLL,
                     [(15, turn), (18, left), (20, magnitude), (13, normalise), (7, R.final(deviation))], R.tiles - 1)

        @block.gpsimd
        def _(pool):
            def add(t):
                S, j = Super(t), t.slot % J
                pool.wait_ge(s["l_ready"], t.n + 1)
                pool.wait_ge(s["r_ready"], t.n + 1)
                wait_count(pool, s["own_ready"], t.n - 2)
                nc.gpsimd.tensor_tensor(g[t.slot % 3][:], lr[S.q][:, j, 0:F + H], lr[S.q][:, j, F + H:2 * (F + H)],
                                        ALU.add).then_inc(s["g_ready"], 1)

            pipeline(pool, R.tiles, UNROLL, [(19, add)], R.tiles - 1)

        @block.tensor
        def _(pe):
            pe.wait_ge(s["split"], 1)

            def transposes(t):
                pe.wait_ge(s["normed"], t.n + 1)
                wait_count(pe, s["hT2_ready"], t.n - 1)
                for c in range(KC):
                    ins = nc.tensor.transpose(hp[t.slot % 2][:, c * P:(c + 1) * P],
                                              hs[t.slot % 3][:, c * P:(c + 1) * P], k["ident"][:])
                ins.then_inc(s["turned"], 1)

            def products(t):
                b, h1, h2 = t.slot % 2, hT1[t.slot % 3], hT2[t.slot % 3]
                passes = [(h1, 0), (h1, 1), (h2, 0)]
                pe.wait_ge(s["hT2_ready"], t.n + 1)
                wait_count(pe, s["l_ready"], t.n - 1)
                wait_count(pe, s["r_ready"], t.n - 1)
                for i, (out, ready) in enumerate(((lp[b][:, 0, 0:B], None), (lp[b][:, 1, 0:B], "lp_ready"),
                                                  (rp[b][:, 0:B], "rp_ready"))):
                    for n, (c, (h, part)) in enumerate([(c, q) for c in range(KC) for q in passes]):
                        ins = nc.tensor.matmul(out, h[:, c * P:(c + 1) * P], 
                                               w_parts[part][:, c].rearrange("p i f -> p (i f)")[:, i * B:(i + 1) * B],
                                               start=(n == 0), stop=(n == 3 * KC - 1))
                    if ready:
                        ins.then_inc(s[ready], 1)

            pipeline(pe, R.tiles, UNROLL, [(17, products), (14, transposes)], R.tiles - 1)


def edge_softmax(nc, k, name, xl, xr, agg, att, H):
    T, U = k["t"], 8
    F = agg.shape[1] - 2 * H
    C = F // H
    W = agg.shape[1]
    with ExitStack() as ctx:
        ph = Phase(nc, ctx, name)
        cols = [ph.sb(f"cols{q}", [P, 2]) for q in range(U)]
        idx = [ph.sb(f"idx{q}", [P, 2], I32) for q in range(U)]
        last = [ph.sb(f"last{q}", [P, 1], I32) for q in range(U)]
        gl = [ph.sb(f"gl{q}", [P, F + H]) for q in range(U)]
        gr = [ph.sb(f"gr{q}", [P, F + H]) for q in range(U)]
        g = [ph.sb(f"g{q}", [P, F + H]) for q in range(2)]
        ab = [ph.sb(f"ab{q}", [P, F]) for q in range(2)]
        junk2 = ph.sb("junk2", [P, H, P])
        e = [ph.sb(f"e{q}", [P, H]) for q in range(U)]
        same = [ph.sb(f"same{q}", [P, P]) for q in range(U)]
        away = [ph.sb(f"away{q}", [P, P]) for q in range(U)]
        m = [ph.sb(f"m{q}", [P, H]) for q in range(U)]
        dif = [ph.sb(f"dif{q}", [P, H]) for q in range(U)]
        p = [ph.sb(f"p{q}", [P, H]) for q in range(U)]
        pd = [ph.sb(f"pd{q}", [P, H]) for q in range(U)]
        v = [ph.sb(f"v{q}", [P, F]) for q in range(2)]
        out = [ph.sb(f"out{q}", [P, W]) for q in range(U)]
        row = ph.ps("row", [P, 2, P])
        eb = [ph.ps(f"eb{q}", [P, H, P] if H > 1 else [P, 4, P]) for q in range(2)]
        acc = [ph.ps(f"acc{q}", [P, 512]) for q in range(2)]
        den = [ph.ps(f"den{q}", [P, 512]) for q in range(2)]
        mb = ph.ps("mb", [P, 512])
        gl_in, gr_in, written = ph.sems("gl_in", U), ph.sems("gr_in", U), ph.sems("written", U)
        names = ("cols_ready", "idx_ready", "last_ready", "g_ready", "ab_ready", "e_ready", "row_ready",
                 "match_ready", "joined", "eb_ready", "m_ready", "mb_ready", "dif0_ready", "dif_ready", "clamped",
                 "p_ready", "v_ready", "pd_ready", "taken_over", "acc_ready", "out_ready", "outm_ready")
        s = {n: ph.sem(n) for n in names}
        block = ctx.enter_context(nc.Block())

        @block.gpsimd
        def _(pool):
            def gather(t):
                pool.wait_ge(s["idx_ready"], t.n + 1)
                wait_count(pool, s["v_ready"], t.n - U + 1)
                settle(pool, k["passed"]["pool"])
                pool.indirect_dma_start(gl[t.slot][:], None, xl, bass.IndirectOffsetOnAxis(idx[t.slot][:, 0:1], 0),
                                        bounds_check=k["n"] - 1).then_inc(gl_in[t.slot], 16)
                pool.indirect_dma_start(gr[t.slot][:], None, xr, bass.IndirectOffsetOnAxis(idx[t.slot][:, 1:2], 0),
                                        bounds_check=k["n"] - 1).then_inc(gr_in[t.slot], 16)

            def write(t):
                pool.wait_ge(s["out_ready"], t.n + 1)
                pool.wait_ge(s["outm_ready"], t.n + 1)
                pool.wait_ge(s["last_ready"], t.n + 1)
                settle(pool, k["passed"]["pool"])
                pool.indirect_dma_start(agg, bass.IndirectOffsetOnAxis(last[t.slot][:], 0), out[t.slot][:], None,
                                        bounds_check=k["n"] - 1, oob_is_err=False).then_inc(written[t.slot], 16)

            pipeline(pool, T, U, [(1, gather), (10, write)])
            for q in range(U):
                pool.wait_ge(written[q], 16 * ((T - 1 - q) // U + 1))

        @block.scalar
        def _(act):
            def weigh(t):
                act.wait_ge(s["p_ready"], t.n + 1)
                act.wait_ge(gl_in[t.slot], 16 * (t.u + 1))
                wait_count(act, s["acc_ready"], t.n - 1)
                for h in range(H):
                    ins = nc.scalar.activation(v[t.slot % 2][:, h * C:(h + 1) * C], gl[t.slot][:, h * C:(h + 1) * C],
                                               ACT.Copy, scale=p[t.slot][:, h:h + 1])
                ins.then_inc(s["v_ready"], 1)

            def magnitude(t):
                act.wait_ge(s["g_ready"], t.n + 1)
                wait_count(act, s["e_ready"], t.n - 1)
                nc.scalar.activation(ab[t.slot % 2][:], g[t.slot % 2][:, 0:F], ACT.Abs,
                                     scale=1.0 - LINEAR).then_inc(s["ab_ready"], 1)

            def exponent(t):
                act.wait_ge(s["clamped"], t.n + 1)
                wait_count(act, s["taken_over"], t.n - U + 1)
                nc.scalar.activation(p[t.slot][:], dif[t.slot][:], ACT.Exp).then_inc(s["p_ready"], 1)

            def drain(t):
                if not (t.static and t.n == T - 1):
                    act.wait_ge(s["taken_over"], t.n + 2)
                act.wait_ge(s["acc_ready"], t.n + 1)
                wait_count(act, written[t.slot], 16 * t.u)
                nc.scalar.copy(out[t.slot][:, 0:F], acc[t.slot % 2][:, 0:F])
                nc.scalar.copy(out[t.slot][:, F:F + H], den[t.slot % 2][:, 0:H]).then_inc(s["out_ready"], 1)

            pipeline(act, T, U, [(6, exponent), (7, weigh), (4, magnitude), (9, drain)])

        @block.vector
        def _(dve):
            def stage(t):
                wait_count(dve, gl_in[t.slot], 16 * t.u)
                wait_count(dve, gr_in[t.slot], 16 * t.u)
                nc.vector.tensor_copy(idx[t.slot][:], k["ci"][:, bass.ds(t.n, 1), 0:2].rearrange("p a b -> p (a b)")
                                      ).then_inc(s["idx_ready"], 1)
                wait_count(dve, s["row_ready"], t.n - U + 1)
                nc.vector.tensor_copy(cols[t.slot][:], k["cf"][:, bass.ds(t.n, 1), :].rearrange("p a b -> p (a b)")
                                      ).then_inc(s["cols_ready"], 1)

            def join(t):
                dve.wait_ge(s["e_ready"], t.n + 1)
                if t.static and t.n == 0:
                    nc.vector.memset(e[0][0:1, :], 0.0).then_inc(s["joined"], 1)
                    return
                dve.wait_ge(s["m_ready"], t.n)
                nc.vector.tensor_copy(e[t.slot][0:1, :], m[(t.slot - 1) % U][0:1, :]).then_inc(s["joined"], 1)

            def take_over(t):
                q, before = t.slot % 2, (t.slot + 1) % 2
                dve.wait_ge(s["p_ready"], t.n + 1)
                wait_count(dve, s["acc_ready"], t.n - U + 1)
                nc.vector.tensor_copy(pd[t.slot][:], p[t.slot][:]).then_inc(s["pd_ready"], 1)
                dve.wait_ge(s["pd_ready"], t.n + 1)
                if t.static and t.n == 0:
                    nc.vector.memset(pd[0][0:1, :], 0.0)
                    dve.wait_ge(s["v_ready"], 1)
                    nc.vector.memset(v[0][0:1, :], 0.0).then_inc(s["taken_over"], 1)
                    return
                dve.wait_ge(s["acc_ready"], t.n)
                nc.vector.tensor_tensor(pd[t.slot][0:1, :], den[before][0:1, 0:H], p[t.slot][0:1, :], ALU.mult)
                dve.wait_ge(s["v_ready"], t.n + 1)
                nc.vector.tensor_tensor(v[q][0:1, :].rearrange("p (h c) -> p h c", h=H),
                                        acc[before][0:1, 0:F].rearrange("p (h c) -> p h c", h=H),
                                        p[t.slot][0:1, :].unsqueeze(2).to_broadcast([1, H, C]),
                                        ALU.mult).then_inc(s["taken_over"], 1)

            def add(t):
                q = t.slot % 2
                dve.wait_ge(gl_in[t.slot], 16 * (t.u + 1))
                dve.wait_ge(gr_in[t.slot], 16 * (t.u + 1))
                wait_count(dve, s["ab_ready"], t.n - 1)
                wait_count(dve, s["e_ready"], t.n - 1)
                nc.vector.tensor_tensor(g[q][:], gl[t.slot][:], gr[t.slot][:], ALU.add).then_inc(s["g_ready"], 1)

            def match(t):
                dve.wait_ge(s["row_ready"], t.n + 1)
                wait_count(dve, s["acc_ready"], t.n - U + 1)
                nc.vector.tensor_scalar(same[t.slot][:], row[:, 1, :], cols[t.slot][:, 0:1], None, ALU.is_equal)
                wait_count(dve, s["m_ready"], t.n - U + 1)
                nc.vector.tensor_scalar(away[t.slot][:], row[:, 0, :], cols[t.slot][:, 1:2], -BIG, ALU.not_equal,
                                        ALU.mult).then_inc(s["match_ready"], 1)

            def maximum(t):
                dve.wait_ge(s["eb_ready"], t.n + 1)
                dve.wait_ge(s["match_ready"], t.n + 1)
                wait_count(dve, s["outm_ready"], t.n - U + 1)
                settle(dve, k["passed"]["dve"])
                for h in range(H):
                    ins = nc.vector.tensor_tensor_reduce(junk2[:, h, :], eb[t.slot % 2][:, h, :], away[t.slot][:],
                                                         1.0, -3.0e38, ALU.add, ALU.max, m[t.slot][:, h:h + 1])
                ins.then_inc(s["m_ready"], 1)

            def score(t):
                q = t.slot % 2
                dve.wait_ge(s["ab_ready"], t.n + 1)
                dve.wait_ge(s["g_ready"], t.n + 1)
                wait_count(dve, s["eb_ready"], t.n - U + 1)
                for h in range(H):
                    ins = nc.vector.tensor_tensor_reduce(ab[q][:, h * C:(h + 1) * C], ab[q][:, h * C:(h + 1) * C],
                                                         att[:, h * C:(h + 1) * C], 1.0, g[q][:, F + h:F + h + 1],
                                                         ALU.mult, ALU.add, e[t.slot][:, h:h + 1])
                ins.then_inc(s["e_ready"], 1)

            def difference(t):
                dve.wait_ge(s["m_ready"], t.n + 1)
                wait_count(dve, s["p_ready"], t.n - U + 1)
                nc.vector.tensor_tensor(dif[t.slot][:], e[t.slot][:], m[t.slot][:],
                                        ALU.subtract).then_inc(s["dif_ready"], 1)

            def carried(t):
                dve.wait_ge(s["mb_ready"], t.n + 1)
                dve.wait_ge(s["dif_ready"], t.n + 1)
                nc.vector.tensor_tensor(dif[t.slot][0:1, :], e[t.slot][0:1, :], mb[0:1, 0:H],
                                        ALU.subtract).then_inc(s["dif0_ready"], 1)
                dve.wait_ge(s["dif0_ready"], t.n + 1)
                nc.vector.tensor_scalar(dif[t.slot][0:1, :], dif[t.slot][0:1, :], 0.0, None,
                                        ALU.min).then_inc(s["clamped"], 1)

            def result(t):
                wait_count(dve, written[t.slot], 16 * t.u)
                nc.vector.tensor_copy(out[t.slot][:, F + H:F + 2 * H], m[t.slot][:]).then_inc(s["outm_ready"], 1)
                nc.vector.tensor_copy(last[t.slot][:], k["ci"][:, bass.ds(t.n, 1), 2]).then_inc(s["last_ready"], 1)

            pipeline(dve, T, U, [(6, carried), (5, join), (8, take_over), (4, add), (4, match), (5, maximum), (4, score),
                                 (5, difference), (6, result), (0, stage)])

        @block.tensor
        def _(pe):
            def rows_of(t):
                pe.wait_ge(s["cols_ready"], t.n + 1)
                wait_count(pe, s["match_ready"], t.n)
                for c in range(2):
                    ins = nc.tensor.transpose(row[:, c, :], cols[t.slot][:, c:c + 1].to_broadcast([P, P]),
                                              k["ident"][:])
                ins.then_inc(s["row_ready"], 1)

            def scores(t):
                pe.wait_ge(s["joined"], t.n + 1)
                wait_count(pe, s["m_ready"], t.n - 1)
                for h in range(H):
                    ins = nc.tensor.transpose(eb[t.slot % 2][:, h, :], e[t.slot][:, h:h + 1].to_broadcast([P, P]),
                                              k["ident"][:])
                ins.then_inc(s["eb_ready"], 1)

            def next_maximum(t):
                pe.wait_ge(s["m_ready"], t.n + 1)
                wait_count(pe, s["dif0_ready"], t.n)
                nc.tensor.matmul(mb[:, 0:H], k["row_one"][:], m[t.slot][:], start=True, stop=True
                                 ).then_inc(s["mb_ready"], 1)

            def total(t):
                q = t.slot % 2
                pe.wait_ge(s["taken_over"], t.n + 1)
                pe.wait_ge(s["match_ready"], t.n + 1)
                wait_count(pe, s["out_ready"], t.n - 1)
                nc.tensor.matmul(den[q][:, 0:H], same[t.slot][:], pd[t.slot][:], start=True, stop=True)
                nc.tensor.matmul(acc[q][:, 0:F], same[t.slot][:], v[q][:], start=True,
                                 stop=True).then_inc(s["acc_ready"], 1)

            pipeline(pe, T, U, [(5, scores), (8, total), (3, rows_of), (5, next_maximum)])


def combined(nc, dve, act, b, s, k, R, U, H, own_all, F):
    def differences(t):
        S, w = Super(t), R.width(t)
        ag, top, dif = (b[n][S.q] for n in ("agg", "top", "dif"))
        dve.wait_ge(b["agg_in"][S.q], 16 * (S.u + 1))
        wait_count(dve, s["dif_ready"], S.n - U + 1)
        nc.vector.tensor_tensor(top[:, 0:w, :], ag[:, 0:w, F + H:F + 2 * H], own_all[:, bass.ds(S.start, w), :],
                                ALU.max).then_inc(s["top_ready"], 1)
        dve.wait_ge(s["top_ready"], S.n + 1)
        wait_count(dve, s["exp_ready"], S.n - U + 1)
        nc.vector.tensor_tensor(dif[:, 0, 0:w, :], ag[:, 0:w, F + H:F + 2 * H], top[:, 0:w, :], ALU.subtract)
        nc.vector.tensor_tensor(dif[:, 1, 0:w, :], own_all[:, bass.ds(S.start, w), :], top[:, 0:w, :],
                                ALU.subtract).then_inc(s["dif_ready"], 1)

    def exponents(t):
        S, w = Super(t), R.width(t)
        act.wait_ge(s["dif_ready"], S.n + 1)
        wait_count(act, s["fac_ready"], S.n - U + 1)
        nc.scalar.activation(b["ex"][S.q][:, :, 0:w, :], b["dif"][S.q][:, :, 0:w, :], ACT.Exp
                             ).then_inc(s["exp_ready"], 1)

    def factors(t):
        S, w = Super(t), R.width(t)
        ag, wh, ex, fac = (b[n][S.q] for n in ("agg", "whole", "ex", "fac"))
        dve.wait_ge(s["exp_ready"], S.n + 1)
        nc.vector.tensor_tensor(wh[:, 0:w, :], ag[:, 0:w, F:F + H], ex[:, 0, 0:w, :],
                                ALU.mult).then_inc(s["whole_ready"], 1)
        dve.wait_ge(s["whole_ready"], 3 * S.n + 1)
        nc.vector.tensor_tensor(wh[:, 0:w, :], wh[:, 0:w, :], ex[:, 1, 0:w, :], ALU.add).then_inc(s["whole_ready"], 1)
        dve.wait_ge(s["whole_ready"], 3 * S.n + 2)
        nc.vector.reciprocal(wh[:, 0:w, :], wh[:, 0:w, :]).then_inc(s["whole_ready"], 1)
        wait_count(dve, s["mixed"], S.start - (U - 1) * J)
        dve.wait_ge(s["whole_ready"], 3 * S.n + 3)
        nc.vector.tensor_tensor(fac[:, 0, 0:w, :], wh[:, 0:w, :], ex[:, 0, 0:w, :], ALU.mult)
        nc.vector.tensor_tensor(fac[:, 1, 0:w, :], wh[:, 0:w, :], ex[:, 1, 0:w, :], ALU.mult
                                ).then_inc(s["fac_ready"], 1)

    return differences, exponents, factors


COMBINED = ("top_ready", "dif_ready", "exp_ready", "whole_ready", "fac_ready", "scaled", "mixed")


def combined_buffers(ph, U, H, W):
    b = {"agg": [ph.sb(f"agg{q}", [P, J, W]) for q in range(U)],
         "top": [ph.sb(f"top{q}", [P, J, H]) for q in range(U)],
         "dif": [ph.sb(f"dif{q}", [P, 2, J, H]) for q in range(U)],
         "ex": [ph.sb(f"ex{q}", [P, 2, J, H]) for q in range(U)],
         "whole": [ph.sb(f"whole{q}", [P, J, H]) for q in range(U)],
         "fac": [ph.sb(f"fac{q}", [P, 2, J, H]) for q in range(U)],
         "agg_in": ph.sems("agg_in", U)}
    return b


def node_hidden(nc, k, xl, agg, w2l, w2r, xl2, xr2, agg2):
    R = k["rows"]
    U = 3
    H, G = k["h1"], w2l.shape[1]
    F = w2l.shape[0]
    C = F // H
    KC = F // P
    with ExitStack() as ctx:
        ph = Phase(nc, ctx, "np2")
        w_sb = ph.sb("w", [P, KC, 2 * G])
        w_parts = [ph.sb(f"w_part{i}", [P, KC, 2, G + 2], F32R) for i in range(2)]
        fold = ph.sb("fold", [P, KC, 2])
        b = combined_buffers(ph, U, H, agg.shape[1])
        ls = [ph.sb(f"l{q}", [P, J, F]) for q in range(U)]
        mix = [ph.sb(f"mix{q}", [P, F]) for q in range(3)]
        hT = [ph.sb(f"hT{q}", [P, F]) for q in range(2)]
        hT1 = [ph.sb(f"hTa{q}", [P, F], F32R) for q in range(3)]
        hT2 = [ph.sb(f"hTb{q}", [P, F], F32R) for q in range(3)]
        lr = [ph.sb(f"lr{q}", [P, 2, J, G + 1]) for q in range(U)]
        g = [ph.sb(f"g{q}", [P, G + 1]) for q in range(3)]
        ab = [ph.sb(f"ab{q}", [P, G]) for q in range(2)]
        junk = ph.sb("junk", [P, 2 * G])
        own = [ph.sb(f"own{q}", [P, J, 1]) for q in range(U)]
        hp = [ph.ps(f"hp{q}", [P, F]) for q in range(2)]
        op = [ph.ps(f"op{q}", [P, 2, 512]) for q in range(2)]
        l_in, stored = ph.sems("l_in", U), ph.sems("stored", U)
        neutral, cleared = ph.sb("neutral", [P, agg2.shape[1]]), ph.sem("cleared")
        names = COMBINED + ("neutral_ready", "weights", "order", "split", "turned", "hT_ready", "hT1_ready", "hT2_ready", "op_ready",
                            "lr_ready", "g_ready", "ab_ready", "own_ready", "own_kept")
        s = {n: ph.sem(n) for n in names}
        block = ctx.enter_context(nc.Block())

        @block.sync
        def _(sp):
            for i, w in enumerate((w2l, w2r)):
                for c in range(KC):
                    sp.dma_start(w_sb[:, c, i * G:(i + 1) * G], w[c * P:(c + 1) * P, :]).then_inc(s["weights"], 16)

            def load(t):
                S, w = Super(t), R.width(t)
                wait_count(sp, s["mixed"], S.start - (U - 1) * J)
                ap, p = R.dram(agg, t)
                settle(sp, k["passed"]["sp"])
                sp.dma_start(b["agg"][S.q][0:p, 0:w, :], ap).then_inc(b["agg_in"][S.q], 16)
                ap, p = R.dram(xl, t, F)
                sp.dma_start(ls[S.q][0:p, 0:w, :], ap).then_inc(l_in[S.q], 16)

            def store(t):
                S, w = Super(t), R.width(t)
                sp.wait_ge(s["lr_ready"], S.start + w)
                for i, table in enumerate((xl2, xr2)):
                    ap, p = R.dram(table, t)
                    settle(sp, k["passed"]["sp"])
                    sp.dma_start(ap, lr[S.q][0:p, i, 0:w, :]).then_inc(stored[S.q], 16)

            sp.wait_ge(s["neutral_ready"], 2)
            clear = clear_rows(sp, k, neutral, agg2, cleared)
            pipeline(sp, R.tiles, UNROLL, [(0, R.first(load)), (3, clear), (17, R.final(store))], R.tiles - 1)
            sp.wait_ge(cleared, 16 * (R.supers + 1))
            for q in range(U):
                sp.wait_ge(stored[q], 32 * ((R.supers - q) // U + 1))

        @block.vector
        def _(dve):
            fill_neutral(nc, k, neutral, 1, s["neutral_ready"])
            dve.wait_ge(s["weights"], 16 * 2 * KC)
            n = split_weights(nc, dve, w_sb, [a[:, :, :, 0:G] for a in w_parts],
                              [fold] + [a[:, :, :, G:G + 2] for a in w_parts], k["a2"], 1, junk, s["order"])
            dve.wait_ge(s["order"], n)
            nc.vector.memset(junk[:, 0:1], 0.0).then_inc(s["split"], 1)
            differences, _, factors = combined(nc, dve, None, b, s, k, R, U, H, k["own1"], F)

            def mixture(t):
                S, j, m = Super(t), t.slot % J, mix[t.slot % 3]
                if j == 0:
                    dve.wait_ge(l_in[S.q], 16 * (S.u + 1))
                dve.wait_ge(s["scaled"], t.n + 1)
                for h in range(H):
                    ins = nc.vector.scalar_tensor_tensor(out=m[:, h * C:(h + 1) * C],
                                                         in0=ls[S.q][:, j, h * C:(h + 1) * C],
                                                         scalar=b["fac"][S.q][:, 1, j, h:h + 1],
                                                         in1=m[:, h * C:(h + 1) * C], op0=ALU.mult, op1=ALU.add)
                ins.then_inc(s["mixed"], 1)

            def rest(t):
                dve.wait_ge(s["hT1_ready"], t.n + 1)
                wait_count(dve, s["op_ready"], t.n - 2)
                nc.vector.tensor_tensor(hT2[t.slot % 3][:], hT[t.slot % 2][:], hT1[t.slot % 3][:].bitcast(F32),
                                        ALU.subtract).then_inc(s["hT2_ready"], 1)

            def out_copy(t):
                S, j, c = Super(t), t.slot % J, t.slot % 2
                dve.wait_ge(s["op_ready"], t.n + 1)
                if j == 0:
                    wait_count(dve, stored[S.q], 32 * S.u)
                    wait_count(dve, s["g_ready"], S.start - (U - 1) * J)
                nc.vector.tensor_copy(lr[S.q][:, :, j, :], op[c][:, :, 0:G + 1]).then_inc(s["lr_ready"], 1)

            def own_score(t):
                S, j, c = Super(t), t.slot % J, t.slot % 2
                dve.wait_ge(s["ab_ready"], t.n + 1)
                if j == 0:
                    wait_count(dve, s["own_kept"], S.n - U + 1)
                nc.vector.tensor_tensor_reduce(ab[c][:], ab[c][:], k["a2"][:], 1.0, g[t.slot % 3][:, G:G + 1],
                                               ALU.mult, ALU.add, own[S.q][:, j, 0:1]).then_inc(s["own_ready"], 1)

            def keep(t):
                S, w = Super(t), R.width(t)
                dve.wait_ge(s["own_ready"], S.start + w)
                nc.vector.tensor_copy(k["own2"][:, bass.ds(S.start, w), :],
                                      own[S.q][:, 0:w, :]).then_inc(s["own_kept"], 1)

            pipeline(dve, R.tiles, UNROLL,
                     [(11, mixture), (14, rest), (16, out_copy), (19, own_score), (6, R.first(differences)),
                      (8, R.first(factors)), (20, R.final(keep))], R.tiles - 1)

        @block.scalar
        def _(act):
            _, exponents, _ = combined(nc, None, act, b, s, k, R, U, H, k["own1"], F)

            def scale(t):
                S, j, m = Super(t), t.slot % J, mix[t.slot % 3]
                if j == 0:
                    act.wait_ge(s["fac_ready"], S.n + 1)
                wait_count(act, s["turned"], t.n - 2)
                for h in range(H):
                    ins = nc.scalar.activation(m[:, h * C:(h + 1) * C], b["agg"][S.q][:, j, h * C:(h + 1) * C],
                                               ACT.Copy, scale=b["fac"][S.q][:, 0, j, h:h + 1])
                ins.then_inc(s["scaled"], 1)

            def turn(t):
                c = t.slot % 2
                act.wait_ge(s["turned"], t.n + 1)
                wait_count(act, s["hT2_ready"], t.n - 1)
                for q in range(KC):
                    ins = nc.scalar.activation(hT[c][:, q * P:(q + 1) * P], hp[c][:, q * P:(q + 1) * P], ACT.Relu,
                                               bias=k["b1"][:, q:q + 1])
                ins.then_inc(s["hT_ready"], 1)

            def high(t):
                c = t.slot % 2
                act.wait_ge(s["hT_ready"], t.n + 1)
                wait_count(act, s["op_ready"], t.n - 2)
                nc.scalar.copy(hT1[t.slot % 3][:], hT[c][:]).then_inc(s["hT1_ready"], 1)

            def magnitude(t):
                act.wait_ge(s["g_ready"], t.n + 1)
                wait_count(act, s["own_ready"], t.n - 1)
                nc.scalar.activation(ab[t.slot % 2][:], g[t.slot % 3][:, 0:G], ACT.Abs,
                                     scale=1.0 - LINEAR).then_inc(s["ab_ready"], 1)

            pipeline(act, R.tiles, UNROLL,
                     [(13, turn), (10, scale), (13, high), (18, magnitude), (7, R.first(exponents))], R.tiles - 1)

        @block.gpsimd
        def _(pool):
            def add(t):
                S, j = Super(t), t.slot % J
                pool.wait_ge(s["lr_ready"], t.n + 1)
                wait_count(pool, s["own_ready"], t.n - 2)
                nc.gpsimd.tensor_tensor(g[t.slot % 3][:], lr[S.q][:, 0, j, :], lr[S.q][:, 1, j, :],
                                        ALU.add).then_inc(s["g_ready"], 1)

            pipeline(pool, R.tiles, UNROLL, [(17, add)], R.tiles - 1)

        @block.tensor
        def _(pe):
            pe.wait_ge(s["split"], 1)

            def transposes(t):
                pe.wait_ge(s["mixed"], t.n + 1)
                wait_count(pe, s["hT_ready"], t.n - 1)
                for c in range(KC):
                    ins = nc.tensor.transpose(hp[t.slot % 2][:, c * P:(c + 1) * P],
                                              mix[t.slot % 3][:, c * P:(c + 1) * P], k["ident"][:])
                ins.then_inc(s["turned"], 1)

            def products(t):
                q, h1, h2 = t.slot % 2, hT1[t.slot % 3], hT2[t.slot % 3]
                passes = [(h1, 0), (h1, 1), (h2, 0)]
                pe.wait_ge(s["hT2_ready"], t.n + 1)
                wait_count(pe, s["lr_ready"], t.n - 1)
                for n, (c, (h, part)) in enumerate([(c, x) for c in range(KC) for x in passes]):
                    for i in range(2):
                        ins = nc.tensor.matmul(op[q][:, i, 0:G + 2], h[:, c * P:(c + 1) * P],
                                               w_parts[part][:, c, i, :], start=(n == 0), stop=(n == 3 * KC - 1))
                ins.then_inc(s["op_ready"], 1)

            pipeline(pe, R.tiles, UNROLL, [(15, products), (12, transposes)], R.tiles - 1)


def node_output(nc, k, xl2, agg2, x1, out):
    R = k["rows"]
    U = 3
    F = out.shape[1]
    with ExitStack() as ctx:
        ph = Phase(nc, ctx, "out")
        b = combined_buffers(ph, U, 1, agg2.shape[1])
        ls = [ph.sb(f"l{q}", [P, J, F]) for q in range(U)]
        xs = [ph.sb(f"x{q}", [P, J, F]) for q in range(U)]
        mix = [ph.sb(f"mix{q}", [P, J, F]) for q in range(U)]
        ys = [ph.sb(f"y{q}", [P, J, F]) for q in range(U)]
        l_in, x_in, stored = ph.sems("l_in", U), ph.sems("x_in", U), ph.sems("stored", U)
        names = COMBINED + ("y_ready", "biased")
        s = {n: ph.sem(n) for n in names}
        block = ctx.enter_context(nc.Block())

        @block.sync
        def _(sp):
            def load(t):
                S, w = Super(t), R.width(t)
                wait_count(sp, s["mixed"], S.start - (U - 1) * J)
                ap, p = R.dram(agg2, t)
                settle(sp, k["passed"]["sp"])
                sp.dma_start(b["agg"][S.q][0:p, 0:w, :], ap).then_inc(b["agg_in"][S.q], 16)
                ap, p = R.dram(xl2, t, F)
                sp.dma_start(ls[S.q][0:p, 0:w, :], ap).then_inc(l_in[S.q], 16)
                wait_count(sp, s["y_ready"], S.n - U + 1)
                ap, p = R.dram(x1, t, F)
                settle(sp, k["passed"]["sp"])
                sp.dma_start(xs[S.q][0:p, 0:w, :], ap).then_inc(x_in[S.q], 16)

            pipeline(sp, R.tiles, UNROLL, [(0, R.first(load))], R.tiles - 1)

        @block.vector
        def _(dve):
            differences, _, factors = combined(nc, dve, None, b, s, k, R, U, 1, k["own2"], F)

            def mixture(t):
                S, j = Super(t), t.slot % J
                if j == 0:
                    dve.wait_ge(l_in[S.q], 16 * (S.u + 1))
                dve.wait_ge(s["scaled"], t.n + 1)
                nc.vector.scalar_tensor_tensor(out=mix[S.q][:, j, :], in0=ls[S.q][:, j, :],
                                               scalar=b["fac"][S.q][:, 1, j, 0:1], in1=mix[S.q][:, j, :],
                                               op0=ALU.mult, op1=ALU.add).then_inc(s["mixed"], 1)

            def result(t):
                S, w = Super(t), R.width(t)
                dve.wait_ge(s["biased"], S.n + 1)
                wait_count(dve, stored[S.q], 16 * S.u)
                dve.wait_ge(s["mixed"], S.start + w)
                nc.vector.tensor_tensor(ys[S.q][:, 0:w, :], mix[S.q][:, 0:w, :], xs[S.q][:, 0:w, :],
                                        ALU.add).then_inc(s["y_ready"], 1)

            pipeline(dve, R.tiles, UNROLL, [(10, mixture), (10, R.final(result)), (6, R.first(differences)),
                                            (8, R.first(factors))], R.tiles - 1)

        @block.scalar
        def _(act):
            _, exponents, _ = combined(nc, None, act, b, s, k, R, U, 1, k["own2"], F)

            def scale(t):
                S, j = Super(t), t.slot % J
                if j == 0:
                    act.wait_ge(s["fac_ready"], S.n + 1)
                    wait_count(act, s["y_ready"], S.n - U + 1)
                nc.scalar.activation(mix[S.q][:, j, :], b["agg"][S.q][:, j, 0:F], ACT.Copy,
                                     scale=b["fac"][S.q][:, 0, j, 0:1]).then_inc(s["scaled"], 1)

            def store(t):
                S = Super(t)
                act.wait_ge(s["y_ready"], S.n + 1)
                ap, p = R.dram(out, t)
                settle(act, k["passed"]["act"])
                act.dma_start(ap, ys[S.q][0:p, 0:R.width(t), :]).then_inc(stored[S.q], 16)

            pipeline(act, R.tiles, UNROLL, [(9, scale), (7, R.first(exponents)), (11, R.final(store))], R.tiles - 1)
            for q in range(U):
                act.wait_ge(stored[q], 16 * ((R.supers - q) // U + 1))

        @block.gpsimd
        def _(pool):
            def bias(t):
                S, w = Super(t), R.width(t)
                pool.wait_ge(x_in[S.q], 16 * (S.u + 1))
                nc.gpsimd.tensor_tensor(xs[S.q][:, 0:w, :], xs[S.q][:, 0:w, :],
                                        k["b2"][:].unsqueeze(1).to_broadcast([P, w, F]), ALU.add
                                        ).then_inc(s["biased"], 1)

            pipeline(pool, R.tiles, UNROLL, [(6, R.first(bias))], R.tiles - 1)


def gnn(nc, x, src, dst, edge_weight, W1l, W1r, a1, b1, W2l, W2r, a2, b2, out):
    N, D = x.shape
    E = src.shape[0]
    H, C = a1.shape
    F1, F2 = H * C, W2l.shape[1]
    T = (E + Q - 1) // Q
    dram = lambda name, shape, dt=F32: nc.dram_tensor(name, shape, dt).ap()
    x1 = dram("x1", (N + 2 * P, D))
    xl1, xr1 = dram("xl1", (N, F1 + H)), dram("xr1", (N, F1 + H))
    agg1, agg2 = dram("agg1", (N, F1 + 2 * H)), dram("agg2", (N, F2 + 2))
    xl2, xr2 = dram("xl2", (N, F2 + 1)), dram("xr2", (N, F2 + 1))
    with ExitStack() as ctx:
        ph = Phase(nc, ctx, "kept", last=True)
        rows = Rows(N)
        k = {"n": N, "e": E, "t": T, "rows": rows, "h1": H, "agg_m": {H: F1 + H, 1: F2 + 1},
             "ident": ph.sb("ident", [P, P]), "row_one": ph.sb("row_one", [P, P]),
             "before": ph.sb("before", [P, 2 * P]), "x1_copied": ph.sem("x1_copied"),
             "x1_copies": N // 400 // 25 + 1,
             "dump_i": ph.sb("dump_i", [P, 2], I32), "dump": ph.sb("dump", [P, 2]), "eps": ph.sb("eps", [P, 1]),
             "ci": ph.sb("ci", [P, T, 3], I32), "cf": ph.sb("cf", [P, T, 2]), "li_src": ph.sb("li_src", [P, T, 2]),
             "own1": ph.sb("own1", [P, rows.tiles, H]), "own2": ph.sb("own2", [P, rows.tiles, 1]),
             "a1": ph.sb("a1", [P, F1]), "a2": ph.sb("a2", [P, F2]), "b1": ph.sb("b1", [P, F1 // P]),
             "b2": ph.sb("b2", [P, F2]), "ready": ph.sem("ready"),
             "passed": {e: ph.sem(f"passed_{e}") for e in ("sp", "act", "pool", "dve")}}
        constants(nc, k)
        with nc.Block() as block:
            @block.sync
            def _(sp):
                sp.dma_start(k["a1"][:], a1.rearrange("h c -> (h c)").partition_broadcast(P)).then_inc(k["ready"], 16)
                sp.dma_start(k["a2"][:], a2.rearrange("h c -> (h c)").partition_broadcast(P)).then_inc(k["ready"], 16)
                sp.dma_start(k["b2"][:], b2.partition_broadcast(P)).then_inc(k["ready"], 16)
                sp.dma_start(k["b1"][:], b1.rearrange("(c p) -> p c", p=P),
                             allow_slow_non_contiguous=True).then_inc(k["ready"], 16)
                sp.wait_ge(k["ready"], 64)
        ordered = [dram("ordered_src", (E,), I32), dram("ordered_dst", (E,), I32), dram("ordered_weight", (E,))]
        order_edges(nc, k, (src, dst, edge_weight), ordered)
        edge_columns(nc, k, *ordered, ordered[1][1:E], x, x1)
        weighted_scatter(nc, k, x, x1)
        node_projections(nc, k, x1, W1l, W1r, xl1, xr1, agg1)
        edge_softmax(nc, k, "ed1", xl1, xr1, agg1, k["a1"], H)
        node_hidden(nc, k, xl1, agg1, W2l, W2r, xl2, xr2, agg2)
        edge_softmax(nc, k, "ed2", xl2, xr2, agg2, k["a2"], 1)
        node_output(nc, k, xl2, agg2, x1, out)


_INS = ["x", "src", "dst", "edge_weight", "L1_gnn_W1l", "L1_gnn_W1r", "L1_gnn_a1", "L1_gnn_b1", "L1_gnn_W2l",
        "L1_gnn_W2r", "L1_gnn_a2", "L1_gnn_b2"]


def kernel(**inputs):
    import numpy as _np
    import concourse.bacc as _bacc
    from concourse import mybir as _mybir
    from concourse.bass_utils import run_bass_kernel_spmd as _run

    nc = _bacc.Bacc("TRN2", target_bir_lowering=False, num_devices=1)
    arrays, args = {}, []
    for name in _INS:
        a = _np.ascontiguousarray(inputs[name])
        arrays[f"in_{name}_dram"] = a
        args.append(nc.dram_tensor(f"in_{name}_dram", a.shape, _mybir.dt.from_np(a.dtype), kind="ExternalInput").ap())
    out = nc.dram_tensor("out_0_dram", inputs["x"].shape, _mybir.dt.float32, kind="ExternalOutput").ap()
    gnn(nc, *args, out)
    r = _run(nc, [arrays], core_ids=[0])
    return r.results[0]["out_0_dram"]
```
